# Optimizing a Trainium2 kernel written in Bass

```python
import numpy as np
import jax
import jax.numpy as jnp

def _softmax(x, axis=-1):
    return jax.nn.softmax(x, axis=axis)

def _gelu(x):
    return jax.nn.gelu(x, approximate=True)

def _silu(x):
    return jax.nn.silu(x)

def _sigmoid(x):
    return jax.nn.sigmoid(x)

def _layernorm(x, axis=-1, eps=1e-05):
    m = jnp.mean(x, axis=axis, keepdims=True)
    v = jnp.var(x, axis=axis, keepdims=True)
    return (x - m) / jnp.sqrt(v + eps)

def _scatter_add(tgt, idx, src, axis=0):
    return tgt.at[idx].add(src)

def _segment_sum(src, seg, n):
    return jax.ops.segment_sum(src, seg, n)
kernel_name = 'mk_decoder_preln_d1_seqx_r8_f0fbf6'

def setup_inputs(seed: int=0):
    np.random.seed(seed)
    _w = jnp.asarray

    def _rec_inputs():
        import jax
        import jax.numpy as jnp
        _rk = jax.random.key(seed)
        x = 0.0002417 + 0.9998 * jax.random.normal(jax.random.fold_in(_rk, 1), (4, 512, 128), jnp.float32)
        _lenS = 512 - jax.random.randint(jax.random.fold_in(_rk, 7), (4,), 0, max(1, 512 // 4) + 1, jnp.int32)
        _lenS2 = 77 - jax.random.randint(jax.random.fold_in(_rk, 8), (4,), 0, max(1, 77 // 4) + 1, jnp.int32)
        _ctx_1024P = jax.random.normal(jax.random.fold_in(_rk, 11), (4, 16, 128), jnp.float32)
        _ctx_1024c = jax.random.dirichlet(jax.random.fold_in(_rk, 511), 0.3 * jnp.ones((16,), jnp.float32), (4, 77))
        _ctx_1024t = jnp.einsum('bsk,bkd->bsd', _ctx_1024c, _ctx_1024P)
        _ctx_1024t = _ctx_1024t * jax.lax.rsqrt(jnp.mean(jnp.square(_ctx_1024t)) + 1e-12) * 0.953939
        ctx_1024 = 7.22013e-05 + 1.00017 * (_ctx_1024t + 0.3 * jax.random.normal(jax.random.fold_in(_rk, 611), (4, 77, 128), jnp.float32))
        return (x, ctx_1024)
    x, ctx_1024 = _rec_inputs()

    def _L0_attn_setup():
        import jax, jax.numpy as jnp
        import numpy as np
        D_IN = 128
        D_OUT = 128
        key = jax.random.key(seed)
        kx, kq, kk, kv = jax.random.split(key, 4)
        x = jax.random.normal(kx, (4, 256, D_IN), dtype=jnp.float32)
        s = 1.0 / np.sqrt(D_IN)
        W_query = jax.random.uniform(kq, (D_OUT, D_IN), dtype=jnp.float32, minval=-s, maxval=s)
        W_key = jax.random.uniform(kk, (D_OUT, D_IN), dtype=jnp.float32, minval=-s, maxval=s)
        W_value = jax.random.uniform(kv, (D_OUT, D_IN), dtype=jnp.float32, minval=-s, maxval=s)
        return {'x': x, 'W_query': W_query, 'W_key': W_key, 'W_value': W_value}
    _L0_attn_all = _L0_attn_setup()
    _L0_attn_in = {k: v for k, v in _L0_attn_all.items() if k in ('W_query', 'W_key', 'W_value')}
    del _L0_attn_all

    def _L0_xattn_setup():
        import jax, jax.numpy as jnp
        import numpy as np
        EMBED = 128
        HEADS = 16
        HEAD_DIM = EMBED // HEADS
        EXP_DIM = 2 * HEAD_DIM

        def _feature_map(x, fm_w, fm_b):
            z = jnp.einsum('nshd,ed->nshe', x, fm_w) + fm_b
            return jnp.concatenate([jnp.exp(z), jnp.exp(-z)], axis=-1)
        key = jax.random.key(seed)
        ks = jax.random.split(key, 7)
        N, S = (4, 256)
        values = jax.random.normal(ks[0], (N, S, EMBED), dtype=jnp.float32)
        keys_ = jax.random.normal(ks[1], (N, S, EMBED), dtype=jnp.float32)
        query = jax.random.normal(ks[2], (N, S, EMBED), dtype=jnp.float32)
        fm_w = jnp.eye(HEAD_DIM, dtype=jnp.float32) + 0.02 * jax.random.normal(ks[3], (HEAD_DIM, HEAD_DIM), dtype=jnp.float32)
        fm_b = 0.02 * jax.random.normal(ks[4], (HEAD_DIM,), dtype=jnp.float32)
        fc_w = jax.random.normal(ks[5], (EMBED, HEADS * EXP_DIM), dtype=jnp.float32) * (1.0 / np.sqrt(HEADS * EXP_DIM))
        fc_b = jnp.zeros((EMBED,), dtype=jnp.float32)
        return {'values': values, 'keys': keys_, 'query': query, 'fm_w': fm_w, 'fm_b': fm_b, 'fc_w': fc_w, 'fc_b': fc_b}
    _L0_xattn_all = _L0_xattn_setup()
    _L0_xattn_in = {k: v for k, v in _L0_xattn_all.items() if k in ('fm_w', 'fm_b', 'fc_w', 'fc_b')}
    del _L0_xattn_all

    def _L0_ffn_setup():
        import jax, jax.numpy as jnp
        import numpy as np
        DIM = 128
        DEPTH = 6
        HEADS = 16
        DIM_HEAD = 64
        WINDOW = 32
        INNER = HEADS * DIM_HEAD
        DIM_INNER = int(DIM * 4 * 2 / 3)
        QK_SCALE = 8.0

        def shift_tokens(t):
            a, s = jnp.split(t, 2, -1)
            s = jnp.pad(s, ((0, 0), (1, 0), (0, 0)))[:, :-1]
            return jnp.concatenate([a, s], -1)

        def l2norm(t):
            return t / jnp.maximum(jnp.linalg.norm(t, axis=-1, keepdims=True), 1e-12)

        def rotate_half(x):
            x1, x2 = jnp.split(x, 2, -1)
            return jnp.concatenate([-x2, x1], -1)

        def rotary_tables(n):
            half = jnp.arange(0, DIM_HEAD, 2, dtype=jnp.float32)
            inv_freq = 1.0 / 10000.0 ** (half / DIM_HEAD)
            t = jnp.arange(n, dtype=jnp.float32)
            freqs = t[:, None] * inv_freq[None, :]
            freqs = jnp.concatenate([freqs, freqs], -1)
            base_scale = (half + 0.4 * DIM_HEAD) / (1.4 * DIM_HEAD)
            power = (t - n // 2) / (WINDOW // 2)
            scale = base_scale[None, :] ** power[:, None]
            scale = jnp.concatenate([scale, scale], -1)
            return (freqs, scale)

        def local_attention(q, k, v):
            b, h, n, d = q.shape
            w = WINDOW
            nw = n // w
            bq = q.reshape(b, h, nw, w, d)
            bk = k.reshape(b, h, nw, w, d)
            bv = v.reshape(b, h, nw, w, d)

            def look(t):
                p = jnp.pad(t, ((0, 0), (0, 0), (1, 0), (0, 0), (0, 0)))
                return jnp.concatenate([p[:, :, :nw], p[:, :, 1:]], axis=3)
            bk2, bv2 = (look(bk), look(bv))
            seq = jnp.arange(n).reshape(nw, w)
            seq_p = jnp.pad(seq, ((1, 0), (0, 0)), constant_values=-1)
            jt = jnp.concatenate([seq_p[:nw], seq_p[1:]], axis=1)
            it = seq[:, :, None]
            jb = jt[:, None, :]
            mask = (it < jb) | (it > jb + w) | (jb == -1)
            sim = jnp.einsum('bhwie,bhwje->bhwij', bq, bk2) * QK_SCALE
            sim = jnp.where(mask, -jnp.finfo(sim.dtype).max, sim)
            attn = jax.nn.softmax(sim, -1)
            out = jnp.einsum('bhwij,bhwje->bhwie', attn, bv2)
            return out.reshape(b, h, n, d)

        def attn_layer(x, Wqkv, qs, ksc, Wo):
            b, n, _ = x.shape
            qkv = x @ Wqkv
            q, k, v = jnp.split(qkv, 3, -1)
            sh = lambda t: t.reshape(b, n, HEADS, DIM_HEAD).transpose(0, 2, 1, 3)
            q, k, v = (sh(q), sh(k), sh(v))
            q = l2norm(q) * qs
            k = l2norm(k) * ksc
            freqs, scale = rotary_tables(n)
            cos, sin = (jnp.cos(freqs), jnp.sin(freqs))
            q = q * cos * scale + rotate_half(q) * sin * scale
            inv = 1.0 / scale
            k = k * cos * inv + rotate_half(k) * sin * inv
            out = local_attention(q, k, v)
            out = out.transpose(0, 2, 1, 3).reshape(b, n, INNER)
            return out @ Wo

        def ffn_layer(x, g, bln, W1, b1, W2, b2):
            mu = x.mean(-1, keepdims=True)
            var = ((x - mu) ** 2).mean(-1, keepdims=True)
            xn = (x - mu) / jnp.sqrt(var + 1e-05) * g + bln
            hg = xn @ W1 + b1
            a, gate = jnp.split(hg, 2, -1)
            return a * jax.nn.gelu(gate, approximate=False) @ W2 + b2
        key = jax.random.key(seed)
        ks = jax.random.split(key, 8)
        B, N = (2, 256)
        init = lambda k, shape: jax.random.normal(k, shape, jnp.float32) * 0.02
        return {'x': jax.random.normal(ks[0], (B, N, DIM), jnp.float32), 'Wqkv': init(ks[1], (DEPTH, DIM, 3 * INNER)), 'q_scale': jnp.ones((DEPTH, DIM_HEAD), jnp.float32), 'k_scale': jnp.ones((DEPTH, DIM_HEAD), jnp.float32), 'Wo': init(ks[2], (DEPTH, INNER, DIM)), 'ln_g': jnp.ones((DEPTH, DIM), jnp.float32), 'ln_b': jnp.zeros((DEPTH, DIM), jnp.float32), 'W1': init(ks[3], (DEPTH, DIM, 2 * DIM_INNER)), 'b1': jnp.zeros((DEPTH, 2 * DIM_INNER), jnp.float32), 'W2': init(ks[4], (DEPTH, DIM_INNER, DIM)), 'b2': jnp.zeros((DEPTH, DIM), jnp.float32)}
    _L0_ffn_all = _L0_ffn_setup()
    _L0_ffn_in = {k: v for k, v in _L0_ffn_all.items() if k in ('Wqkv', 'q_scale', 'k_scale', 'Wo', 'ln_g', 'ln_b', 'W1', 'b1', 'W2', 'b2')}
    del _L0_ffn_all
    return {'x': x, 'ctx_1024': ctx_1024, 'L0_attn_W_query': _L0_attn_in['W_query'], 'L0_attn_W_key': _L0_attn_in['W_key'], 'L0_attn_W_value': _L0_attn_in['W_value'], 'L0_xattn_fm_w': _L0_xattn_in['fm_w'], 'L0_xattn_fm_b': _L0_xattn_in['fm_b'], 'L0_xattn_fc_w': _L0_xattn_in['fc_w'], 'L0_xattn_fc_b': _L0_xattn_in['fc_b'], 'L0_ffn_Wqkv': _L0_ffn_in['Wqkv'], 'L0_ffn_q_scale': _L0_ffn_in['q_scale'], 'L0_ffn_k_scale': _L0_ffn_in['k_scale'], 'L0_ffn_Wo': _L0_ffn_in['Wo'], 'L0_ffn_ln_g': _L0_ffn_in['ln_g'], 'L0_ffn_ln_b': _L0_ffn_in['ln_b'], 'L0_ffn_W1': _L0_ffn_in['W1'], 'L0_ffn_b1': _L0_ffn_in['b1'], 'L0_ffn_W2': _L0_ffn_in['W2'], 'L0_ffn_b2': _L0_ffn_in['b2']}

def reference(x, ctx_1024, L0_attn_W_query, L0_attn_W_key, L0_attn_W_value, L0_xattn_fm_w, L0_xattn_fm_b, L0_xattn_fc_w, L0_xattn_fc_b, L0_ffn_Wqkv, L0_ffn_q_scale, L0_ffn_k_scale, L0_ffn_Wo, L0_ffn_ln_g, L0_ffn_ln_b, L0_ffn_W1, L0_ffn_b1, L0_ffn_W2, L0_ffn_b2):
    import jax
    import jax.numpy as jnp

    def _L0_attn_ref(x, W_query, W_key, W_value):
        import jax, jax.numpy as jnp
        import numpy as np
        D_IN = 128
        D_OUT = 128
        b, n, _ = x.shape
        d_out = W_query.shape[0]
        q = jnp.einsum('bnd,od->bno', x, W_query)
        k = jnp.einsum('bnd,od->bno', x, W_key)
        v = jnp.einsum('bnd,od->bno', x, W_value)
        scores = jnp.einsum('bqo,bko->bqk', q, k)
        causal = jnp.tril(jnp.ones((n, n), dtype=bool))
        scores = jnp.where(causal, scores, -jnp.inf)
        weights = jax.nn.softmax(scores / jnp.sqrt(jnp.asarray(d_out, dtype=scores.dtype)), axis=-1)
        return jnp.einsum('bqk,bko->bqo', weights, v)

    def _L0_xattn_ref(values, keys, query, fm_w, fm_b, fc_w, fc_b):
        import jax, jax.numpy as jnp
        import numpy as np
        EMBED = 128
        HEADS = 16
        HEAD_DIM = EMBED // HEADS
        EXP_DIM = 2 * HEAD_DIM

        def _feature_map(x, fm_w, fm_b):
            z = jnp.einsum('nshd,ed->nshe', x, fm_w) + fm_b
            return jnp.concatenate([jnp.exp(z), jnp.exp(-z)], axis=-1)
        N, S, _ = query.shape
        v = values.reshape(N, -1, HEADS, HEAD_DIM)
        k = keys.reshape(N, -1, HEADS, HEAD_DIM)
        q = query.reshape(N, -1, HEADS, HEAD_DIM)
        v, k, q = (_feature_map(x, fm_w, fm_b) for x in (v, k, q))
        scores = jnp.einsum('nqhd,nkhd->nhqk', q, k) / jnp.sqrt(jnp.float32(EMBED))
        attn = jax.nn.softmax(scores, axis=-1)
        out = jnp.einsum('nhql,nlhd->nqhd', attn, v)
        out = out.reshape(N, S, HEADS * EXP_DIM)
        return out @ fc_w.T + fc_b

    def _L0_ffn_ref(x, Wqkv, q_scale, k_scale, Wo, ln_g, ln_b, W1, b1, W2, b2):
        import jax, jax.numpy as jnp
        import numpy as np
        DIM = 128
        DEPTH = 6
        HEADS = 16
        DIM_HEAD = 64
        WINDOW = 32
        INNER = HEADS * DIM_HEAD
        DIM_INNER = int(DIM * 4 * 2 / 3)
        QK_SCALE = 8.0

        def shift_tokens(t):
            a, s = jnp.split(t, 2, -1)
            s = jnp.pad(s, ((0, 0), (1, 0), (0, 0)))[:, :-1]
            return jnp.concatenate([a, s], -1)

        def l2norm(t):
            return t / jnp.maximum(jnp.linalg.norm(t, axis=-1, keepdims=True), 1e-12)

        def rotate_half(x):
            x1, x2 = jnp.split(x, 2, -1)
            return jnp.concatenate([-x2, x1], -1)

        def rotary_tables(n):
            half = jnp.arange(0, DIM_HEAD, 2, dtype=jnp.float32)
            inv_freq = 1.0 / 10000.0 ** (half / DIM_HEAD)
            t = jnp.arange(n, dtype=jnp.float32)
            freqs = t[:, None] * inv_freq[None, :]
            freqs = jnp.concatenate([freqs, freqs], -1)
            base_scale = (half + 0.4 * DIM_HEAD) / (1.4 * DIM_HEAD)
            power = (t - n // 2) / (WINDOW // 2)
            scale = base_scale[None, :] ** power[:, None]
            scale = jnp.concatenate([scale, scale], -1)
            return (freqs, scale)

        def local_attention(q, k, v):
            b, h, n, d = q.shape
            w = WINDOW
            nw = n // w
            bq = q.reshape(b, h, nw, w, d)
            bk = k.reshape(b, h, nw, w, d)
            bv = v.reshape(b, h, nw, w, d)

            def look(t):
                p = jnp.pad(t, ((0, 0), (0, 0), (1, 0), (0, 0), (0, 0)))
                return jnp.concatenate([p[:, :, :nw], p[:, :, 1:]], axis=3)
            bk2, bv2 = (look(bk), look(bv))
            seq = jnp.arange(n).reshape(nw, w)
            seq_p = jnp.pad(seq, ((1, 0), (0, 0)), constant_values=-1)
            jt = jnp.concatenate([seq_p[:nw], seq_p[1:]], axis=1)
            it = seq[:, :, None]
            jb = jt[:, None, :]
            mask = (it < jb) | (it > jb + w) | (jb == -1)
            sim = jnp.einsum('bhwie,bhwje->bhwij', bq, bk2) * QK_SCALE
            sim = jnp.where(mask, -jnp.finfo(sim.dtype).max, sim)
            attn = jax.nn.softmax(sim, -1)
            out = jnp.einsum('bhwij,bhwje->bhwie', attn, bv2)
            return out.reshape(b, h, n, d)

        def attn_layer(x, Wqkv, qs, ksc, Wo):
            b, n, _ = x.shape
            qkv = x @ Wqkv
            q, k, v = jnp.split(qkv, 3, -1)
            sh = lambda t: t.reshape(b, n, HEADS, DIM_HEAD).transpose(0, 2, 1, 3)
            q, k, v = (sh(q), sh(k), sh(v))
            q = l2norm(q) * qs
            k = l2norm(k) * ksc
            freqs, scale = rotary_tables(n)
            cos, sin = (jnp.cos(freqs), jnp.sin(freqs))
            q = q * cos * scale + rotate_half(q) * sin * scale
            inv = 1.0 / scale
            k = k * cos * inv + rotate_half(k) * sin * inv
            out = local_attention(q, k, v)
            out = out.transpose(0, 2, 1, 3).reshape(b, n, INNER)
            return out @ Wo

        def ffn_layer(x, g, bln, W1, b1, W2, b2):
            mu = x.mean(-1, keepdims=True)
            var = ((x - mu) ** 2).mean(-1, keepdims=True)
            xn = (x - mu) / jnp.sqrt(var + 1e-05) * g + bln
            hg = xn @ W1 + b1
            a, gate = jnp.split(hg, 2, -1)
            return a * jax.nn.gelu(gate, approximate=False) @ W2 + b2
        for i in range(DEPTH):
            x = attn_layer(shift_tokens(x), Wqkv[i], q_scale[i], k_scale[i], Wo[i]) + x
            x = ffn_layer(shift_tokens(x), ln_g[i], ln_b[i], W1[i], b1[i], W2[i], b2[i]) + x
        return x
    x = x + _L0_attn_ref(_layernorm(x, axis=-1), L0_attn_W_query, L0_attn_W_key, L0_attn_W_value)
    x = x + _L0_xattn_ref(ctx_1024, ctx_1024, _layernorm(x, axis=-1), L0_xattn_fm_w, L0_xattn_fm_b, L0_xattn_fc_w, L0_xattn_fc_b)
    x = x + _L0_ffn_ref(_layernorm(x, axis=-1), L0_ffn_Wqkv, L0_ffn_q_scale, L0_ffn_k_scale, L0_ffn_Wo, L0_ffn_ln_g, L0_ffn_ln_b, L0_ffn_W1, L0_ffn_b1, L0_ffn_W2, L0_ffn_b2)
    return x

_drawn_inputs = setup_inputs


def setup_inputs(seed=0):
    import zlib

    import numpy as np

    out = dict(_drawn_inputs(seed))
    spreads = {'L0_xattn_fc_b': (0.0, 0.8),
     'L0_ffn_q_scale': (1.0, 0.6),
     'L0_ffn_k_scale': (1.0, 0.6),
     'L0_ffn_ln_g': (1.0, 0.6),
     'L0_ffn_ln_b': (0.0, 0.8),
     'L0_ffn_b1': (0.0, 0.8),
     'L0_ffn_b2': (0.0, 0.455)}
    factors = {'L0_ffn_W1': 8.0, 'L0_ffn_W2': 8.0}
    for name, (base, spread) in spreads.items():
        noise = np.random.default_rng([zlib.crc32(name.encode()), seed]).standard_normal(out[name].shape)
        drawn = base * np.exp(spread * noise) if base else spread * noise
        out[name] = jnp.asarray(drawn.astype(out[name].dtype))
    for name, factor in factors.items():
        out[name] = (out[name] * factor).astype(out[name].dtype)
    return out
```

```python
from contextlib import ExitStack

import numpy as np

import concourse.bass as bass
from concourse import mybir

ALU = mybir.AluOpType
ACT = mybir.ActivationFunctionType
AX = mybir.AxisListType
F32 = mybir.dt.float32
BF16 = mybir.dt.bfloat16
I32 = mybir.dt.int32

P = 128
D = 128
BATCH, SEQ = 4, 512
GPB = SEQ // P
DEPTH = 6
NIT = DEPTH * BATCH
HEADS, DH = 16, 64
INNER = HEADS * DH
WIN = 32
PAIRS = HEADS // 2
FF = 341
FCH = [(0, 128), (128, 128), (256, FF - 256)]
CTX = 77
XH, XE, XF = 16, 8, 16
ATT_SCALE = 1.0 / float(np.sqrt(128.0))
NEG = -1e30
RSQRT_MAGIC = float(0x5F3759DF)
LN_EPS = 1e-5
FFN_STEPS = [[0, 1], [2, 3, 4], [5, 6, 7, 8], [9]]
FJOBS = 10
DMAS_FFN = 10


def rotary_tables():
    f = np.float32
    half = np.arange(0, DH, 2, dtype=f)
    inv_freq = (f(1.0) / np.power(f(10000.0), half / f(DH))).astype(f)
    t = np.arange(SEQ, dtype=f)
    ang = (t[:, None] * inv_freq[None, :]).astype(f).astype(np.float64)
    base = ((half + f(0.4 * DH)) / f(1.4 * DH)).astype(f)
    power = ((t - SEQ // 2) / f(WIN // 2)).astype(f)
    scale = np.power(base[None, :].astype(np.float64), power[:, None].astype(np.float64))
    cos, sin = np.cos(ang), np.sin(ang)
    kinds = []
    for s in (8.0 * scale, 1.0 / scale):
        kinds.append(np.concatenate([cos * s, cos * s], 1))
        kinds.append(np.concatenate([sin * s, -sin * s], 1))
    tab = np.stack(kinds, 1).astype(f)
    return np.ascontiguousarray(tab.reshape(GPB, P, 4, DH).transpose(1, 2, 0, 3))


def window_masks():
    m = np.zeros((2, P, 2, 64), np.float32)
    q = np.arange(WIN)[:, None]
    c = np.arange(WIN)[None, :]
    blk = np.concatenate([np.where(c >= q, 0.0, NEG), np.where(c <= q, 0.0, NEG)], 1)
    for first in range(2):
        for hp in range(2):
            for wpar in range(2):
                rows = slice(hp * 64 + wpar * 32, hp * 64 + wpar * 32 + 32)
                for half in range(2):
                    b = blk.copy()
                    if first and half == 0 and wpar == 0:
                        b[:, :WIN] = NEG
                    m[first, rows, half, :] = b
    return np.ascontiguousarray(m.reshape(2, P, P).transpose(1, 0, 2))


def causal_mask():
    q = np.arange(P)[:, None]
    return np.where(np.arange(P)[None, :] <= q, 0.0, NEG).astype(np.float32)


def head_mask():
    return (np.arange(P)[:, None] // XE == np.arange(XH)[None, :]).astype(np.float32)


def cnt(it, per, c):
    return it * per + c


def need(eng, semaphore, value):
    if isinstance(value, int) and value <= 0:
        return
    eng.wait_ge(semaphore, value)


def rsqrt_guess(v, y, w):
    return v.tensor_scalar(y.bitcast(I32), w.bitcast(I32), -0.5, RSQRT_MAGIC, ALU.mult, ALU.add)


def rsqrt_step(v, n, y, w, t):
    if n == 0:
        return v.scalar_tensor_tensor(out=t, in0=y, scalar=-0.5, in1=y, op0=ALU.mult, op1=ALU.mult)
    if n == 1:
        return v.tensor_tensor(t, t, w, ALU.mult)
    return v.scalar_tensor_tensor(out=y, in0=t, scalar=1.5, in1=y, op0=ALU.add, op1=ALU.mult)


def bcast(ap, axis, n):
    u = ap.unsqueeze(axis)
    shape = list(u.shape)
    shape[axis] = n
    return u.broadcast_to(shape)


def rows(dram, n):
    return bass.AP(tensor=dram.tensor, offset=dram.offset, ap=[[0, n]] + [list(x) for x in dram.ap])


def decoder(nc, a, out):
    with ExitStack() as ctx:
        def sb(name, shape, dt=F32):
            return ctx.enter_context(nc.sbuf_tensor(name, shape, dt))

        k = dict(
            bank=[ctx.enter_context(nc.psum_tensor(f"bank{i}", [P, 512], F32)) for i in range(8)],
            table_d=nc.inline_tensor(rotary_tables(), "rotary_const").ap(),
            mask_d=nc.inline_tensor(window_masks(), "mask_const").ap(),
            causal_d=nc.inline_tensor(causal_mask(), "causal_const").ap(),
            hmask_d=nc.inline_tensor(head_mask(), "head_const").ap(),
            stream=sb("stream", [P, BATCH * GPB, D]),
            skip=sb("skip", [P, BATCH * GPB, D]),
            ident=sb("ident", [P, P]),
            identb=sb("identb", [P, P], BF16),
            maskb=sb("maskb", [P, 2, P], BF16),
            rot=sb("rot", [P, DEPTH, 4, GPB * DH]),
        )
        with ExitStack() as part:
            front(nc, part, a, k)
        with ExitStack() as part:
            stack(nc, part, a, k, out)


def layer_norm_tiles(dve, link, src, st, mv, w, y, t, dst, last):
    for j in range(GPB):
        link(dve.bn_stats(st[:, j, :], src(j)), j == GPB - 1)
    for j in range(GPB):
        link(dve.bn_aggr(mv[:, j, :], st[:, j, :]), j == GPB - 1)
    link(dve.tensor_scalar(w, mv[:, :, 1], LN_EPS, None, ALU.add))
    link(rsqrt_guess(dve, y, w))
    for _ in range(3):
        for n in range(3):
            link(rsqrt_step(dve, n, y, w, t))
    for j in range(GPB):
        ins = dve.tensor_scalar(dst(j), src(j), mv[:, j, 0:1], y[:, j:j + 1], ALU.subtract, ALU.mult)
    last(ins)


def front(nc, part, a, k):
    bank, stream, skip, ident, identb, maskb, rot = (
        k[n] for n in ("bank", "stream", "skip", "ident", "identb", "maskb", "rot"))

    def sb(name, shape, dt=F32):
        return part.enter_context(nc.sbuf_tensor("front_" + name, shape, dt))

    def sem(name):
        return part.enter_context(nc.semaphore("front_" + name))

    NJ = XH // 4
    CW = 4 * CTX
    table = sb("table", [P, 4, GPB * DH])
    qscl = sb("qscl", [P, DEPTH, DH])
    kscl = sb("kscl", [P, DEPTH, DH])
    maskf = sb("maskf", [P, 2, P])
    causal = sb("causal", [P, P])
    hmask = sb("hmask", [P, XH])
    fmb = sb("fmb", [P, 1])
    fmbn = sb("fmbn", [P, 1])
    fmrow = sb("fmrow", [CTX, P])
    fcb = sb("fcb", [P, D])
    bd = sb("bd", [P, P])
    fcw = sb("fcw", [P, 2, P])
    fcT = sb("fcT", [P, 2, P])
    wq = sb("wq", [P, P])
    wk = sb("wk", [P, P])
    wv = sb("wv", [P, P])
    mqk = sb("mqk", [P, P])
    wvT = sb("wvT", [P, P])
    cx = sb("cx", [CTX, BATCH, D])
    cxs = sb("cxs", [CTX, D])
    cxT = sb("cxT", [P, CTX])
    ek = sb("ek", [P, 2, CTX])
    zrow = sb("zrow", [CTX, P])
    vx = sb("vx", [CTX, XH, XF])
    kx = sb("kx", [P, 2, XH, CTX])
    xn = sb("xn", [P, GPB, D])
    xnT = sb("xnT", [P, SEQ])
    qp = sb("qp", [P, SEQ])
    va = sb("va", [P, GPB, D])
    eq = sb("eq", [P, 2, SEQ])
    pa = sb("pa", [P, 2, SEQ])
    paT = sb("paT", [P, 2, SEQ])
    xd = sb("xd", [P, 2, CW])
    xp = sb("xp", [P, 2, CW])
    xpT = sb("xpT", [CTX, 2, 512])
    xon = sb("xon", [P, XH, XF])
    xoT = sb("xoT", [P, 2, P])
    st = sb("st", [P, GPB, 6])
    mv = sb("mv", [P, GPB, 2])
    lw = sb("lw", [P, 3, GPB])
    amax = sb("amax", [P, GPB])
    asum = sb("asum", [P, GPB])
    ainv = sb("ainv", [P, GPB])
    xmax = sb("xmax", [P, 2, 4])
    xsum = sb("xsum", [P, 2, XH])
    xinv = sb("xinv", [P, XH])

    s_x, s_w, s_zero, s_bd, s_id = sem("x_in"), sem("weights_in"), sem("bd_zeroed"), sem("bd_in"), sem("ident_made")
    s_const, s_nb, s_prep, s_prepped = sem("const_ready"), sem("fmbn_ready"), sem("prep_made"), sem("prep_out")
    s_xn, s_xnT_p, s_xnT = sem("xn_ready"), sem("xnT_made"), sem("xnT_ready")
    s_qp_p, s_qp, s_va_p, s_va = sem("qp_made"), sem("qp_ready"), sem("va_made"), sem("va_ready")
    s_sc, s_nm, s_pa, s_paT_p, s_paT = sem("scores_made"), sem("max_ready"), sem("p_ready"), sem("pT_made"), sem("pT_ready")
    s_pv, s_att = sem("pv_made"), sem("att_added")
    s_cxs, s_cxT_p, s_cxT, s_zk, s_ek, s_zr, s_vx, s_kx = (
        sem(n) for n in ("cxs_ready", "cxT_made", "cxT_ready", "zk_made", "ek_ready", "zrow_ready", "vx_ready", "kx_ready"))
    s_zq, s_eq = sem("zq_made"), sem("eq_ready")
    s_xs, s_xd, s_xp, s_xm, s_xpT_p, s_xpT = (
        sem(n) for n in ("xscores_made", "xdiff_ready", "xp_ready", "xsum_ready", "xpT_made", "xpT_ready"))
    s_xav, s_xon, s_xoT_p, s_xoT, s_fc, s_xadd = (
        sem(n) for n in ("xav_made", "xon_ready", "xoT_made", "xoT_ready", "fc_made", "xatt_added"))
    s_link = sem("dve_link")
    consts = [
        (table[:, :, :].rearrange("p k (j d) -> p k j d", d=DH), k["table_d"]),
        (maskf[:, :, :], k["mask_d"]), (causal[:, :], k["causal_d"]), (hmask[:, :], k["hmask_d"]),
        (qscl[:, :, :], rows(a["L0_ffn_q_scale"], P)), (kscl[:, :, :], rows(a["L0_ffn_k_scale"], P)),
        (wq[:, :], a["L0_attn_W_query"]), (wk[:, :], a["L0_attn_W_key"]), (wv[:, :], a["L0_attn_W_value"]),
        (cx[:, :, :], a["ctx_1024"].rearrange("b s d -> s b d")),
        (fcw[:, :, :], a["L0_xattn_fc_w"].rearrange("o (c f) -> o c f", c=2)),
        (fcb[:, :], rows(a["L0_xattn_fc_b"], P)),
        (fmrow[:, :], bass.AP(tensor=a["L0_xattn_fm_b"].tensor, offset=0, ap=[[0, CTX], [0, XH], [1, XE]])),
        (fmb[:, :], bass.AP(tensor=a["L0_xattn_fm_b"].tensor, offset=0, ap=[[0, XH], [1, XE], [1, 1]])),
    ]
    x_d = a["x"].rearrange("b (j p) d -> p (b j) d", p=P)

    with nc.Block() as block:
        @block.sync
        def _(sp):
            for b in range(BATCH):
                sp.dma_start(stream[:, GPB * b:GPB * (b + 1), :], x_d[:, GPB * b:GPB * (b + 1), :]).then_inc(s_x, 16)
            for dst, src in consts[:7]:
                sp.dma_start(dst, src).then_inc(s_w, 16)
            sp.wait_ge(s_zero, 1)
            with nc.allow_non_contiguous_dma(reason="8 x 8 transposed blocks"):
                for h in range(XH):
                    r = slice(XE * h, XE * h + XE)
                    sp.dma_start(bd[r, r], a["L0_xattn_fm_w"].rearrange("e d -> d e")).then_inc(s_bd, 16)

        @block.gpsimd
        def _(pool):
            pool.memset(bd[:, :], 0.0).then_inc(s_zero, 1)
            pool.memset(ident[:, :], 0.0).then_inc(s_id, 1)
            pool.wait_ge(s_id, 1)
            pool.affine_select(out=ident[:, :], in_=ident[:, :], compare_op=ALU.not_equal, fill=1.0, base=0,
                               pattern=[[-1, P]], channel_multiplier=1).then_inc(s_id, 1)
            pool.wait_ge(s_w, 16 * len(consts))
            pool.wait_ge(s_id, 2)
            pool.tensor_copy(identb[:, :], ident[:, :]).then_inc(s_const, 1)
            pool.tensor_copy(maskb[:, :, :], maskf[:, :, :]).then_inc(s_const, 1)
            for layer in range(DEPTH):
                for n, scl in enumerate((qscl, kscl)):
                    pool.tensor_tensor(
                        rot[:, layer, 2 * n:2 * n + 2, :].rearrange("p k (j d) -> p (k j) d", d=DH),
                        table[:, 2 * n:2 * n + 2, :].rearrange("p k (j d) -> p (k j) d", d=DH),
                        bcast(scl[:, layer, :], 1, 2 * GPB), ALU.mult).then_inc(s_const, 1)

        @block.tensor
        def _(pe):
            pe.wait_ge(s_id, 2)
            pe.wait_ge(s_w, 16 * len(consts))
            pe.matmul(bank[0][:, 0:P], wq[:, :], wk[:, :], start=True, stop=True)
            pe.transpose(bank[0][:, P:2 * P], wv[:, :], ident[:, :])
            pe.transpose(bank[0][:, 2 * P:3 * P], fcw[:, 0, :], ident[:, :])
            pe.transpose(bank[0][:, 3 * P:4 * P], fcw[:, 1, :], ident[:, :]).then_inc(s_prep, 1)
            pe.wait_ge(s_bd, 16 * XH)
            pe.wait_ge(s_prepped, 1)
            with pe.Fori(0, BATCH) as b:
                pe.wait_ge(s_xn, cnt(b, 3, 1))
                for j in range(GPB):
                    last = pe.transpose(bank[0][:, P * j:P * j + P], xn[:, j, :], ident[:, :])
                last.then_inc(s_xnT_p, 1)
                pe.wait_ge(s_xnT, cnt(b, 2, 1))
                pe.matmul(bank[1][:, :], mqk[:, :], xnT[:, :], start=True, stop=True).then_inc(s_qp_p, 1)
                for j in range(GPB):
                    last = pe.matmul(bank[2][:, P * j:P * j + P], xnT[:, P * j:P * j + P], wvT[:, :],
                                     start=True, stop=True)
                last.then_inc(s_va_p, 1)
                pe.wait_ge(s_qp, cnt(b, 1, 1))
                for i in range(GPB):
                    pe.matmul(bank[3 + i][:, 0:P * (i + 1)], qp[:, P * i:P * i + P], xnT[:, 0:P * (i + 1)],
                              start=True, stop=True).then_inc(s_sc, 1)
                pe.wait_ge(s_va, cnt(b, 1, 1))
                for i in range(GPB):
                    pe.wait_ge(s_pa, cnt(b, GPB, i + 1))
                    if i >= 2:
                        pe.wait_ge(s_paT, cnt(b, GPB, i - 1))
                    tb = bank[7] if i % 2 == 0 else bank[1]
                    for c in range(i + 1):
                        last = pe.transpose(tb[:, P * c:P * c + P], pa[:, i % 2, P * c:P * c + P], ident[:, :])
                    last.then_inc(s_paT_p, 1)
                    pe.wait_ge(s_paT, cnt(b, GPB, i + 1))
                    if i >= 2:
                        pe.wait_ge(s_att, cnt(b, GPB, i - 1))
                    for c in range(i + 1):
                        last = pe.matmul(bank[2 * (i % 2)][:, 0:P], paT[:, i % 2, P * c:P * c + P], va[:, c, :],
                                         start=(c == 0), stop=(c == i))
                    last.then_inc(s_pv, 1)
                pe.wait_ge(s_att, cnt(b, GPB, GPB))
                pe.wait_ge(s_cxs, cnt(b, 1, 1))
                pe.transpose(bank[2][:, 0:CTX], cxs[:, :], ident[0:CTX, 0:CTX]).then_inc(s_cxT_p, 1)
                pe.wait_ge(s_cxT, cnt(b, 1, 1))
                pe.matmul(bank[2][:, P:P + CTX], bd[:, :], cxT[:, :], start=True, stop=True)
                pe.matmul(bank[2][0:CTX, 2 * P:3 * P], cxT[:, :], bd[:, :], start=True, stop=True).then_inc(s_zk, 1)
                pe.wait_ge(s_xn, cnt(b, 3, 2))
                for j in range(GPB):
                    last = pe.transpose(bank[0][:, P * j:P * j + P], xn[:, j, :], ident[:, :])
                last.then_inc(s_xnT_p, 1)
                pe.wait_ge(s_xnT, cnt(b, 2, 2))
                pe.matmul(bank[1][:, :], bd[:, :], xnT[:, :], start=True, stop=True).then_inc(s_zq, 1)
                pe.wait_ge(s_eq, cnt(b, 1, 1))
                pe.wait_ge(s_kx, cnt(b, 1, 1))
                pe.wait_ge(s_vx, cnt(b, 1, 1))
                N = GPB * NJ
                for n in range(N + 3):
                    if n < N:
                        g, c = n // NJ, n % NJ
                        if n >= 2:
                            pe.wait_ge(s_xd, cnt(b, N, n - 1))
                        sc = bank[3 + n % 2][:, 0:CW]
                        for e in range(2):
                            last = pe.matmul(sc, eq[:, e, P * g:P * g + P],
                                             kx[:, e, 4 * c:4 * c + 4, :].rearrange("p h s -> p (h s)"),
                                             start=(e == 0), stop=(e == 1))
                        last.then_inc(s_xs, 1)
                    if 1 <= n < N + 1:
                        m = n - 1
                        pe.wait_ge(s_xp, cnt(b, N, m + 1))
                        if m >= 2:
                            pe.wait_ge(s_xpT, cnt(b, N, m - 1))
                        for h in range(4):
                            last = pe.transpose(bank[5 + m % 2][0:CTX, P * h:P * h + P],
                                                xp[:, m % 2, CTX * h:CTX * h + CTX], ident[:, :])
                        last.then_inc(s_xpT_p, 1)
                    if 2 <= n < N + 2:
                        m = n - 2
                        g, c = m // NJ, m % NJ
                        pe.wait_ge(s_xpT, cnt(b, N, m + 1))
                        if c == 0 and g > 0:
                            pe.wait_ge(s_xon, cnt(b, GPB, g))
                        for h in range(4):
                            hh = 4 * c + h
                            last = pe.matmul(bank[7][:, XF * hh:XF * hh + XF], xpT[:, m % 2, P * h:P * h + P],
                                             vx[:, hh, :], start=True, stop=True)
                        last.then_inc(s_xav, 1)
                    if n >= 3 and (n - 3) % NJ == NJ - 1:
                        g = (n - 3) // NJ
                        pe.wait_ge(s_xon, cnt(b, GPB, g + 1))
                        for c in range(2):
                            last = pe.transpose(
                                bank[1][:, P * c:P * c + P],
                                xon[:, XH // 2 * c:XH // 2 * (c + 1), :].rearrange("p h f -> p (h f)"), ident[:, :])
                        last.then_inc(s_xoT_p, 1)
                        pe.wait_ge(s_xoT, cnt(b, GPB, g + 1))
                        if g > 0:
                            pe.wait_ge(s_xadd, cnt(b, GPB, g))
                        for c in range(2):
                            last = pe.matmul(bank[2][:, 0:D], xoT[:, c, :], fcT[:, c, :], start=(c == 0), stop=(c == 1))
                        last.then_inc(s_fc, 1)
                pe.wait_ge(s_xadd, cnt(b, GPB, GPB))

        @block.scalar
        def _(act):
            for dst, src in consts[7:]:
                act.dma_start(dst, src).then_inc(s_w, 16)
            act.wait_ge(s_w, 16 * len(consts))
            act.mul(fmbn[:, :], fmb[:, :], -1.0).then_inc(s_nb, 1)
            act.wait_ge(s_prep, 1)
            act.copy(mqk[:, :], bank[0][:, 0:P])
            act.copy(wvT[:, :], bank[0][:, P:2 * P])
            act.copy(fcT[:, :, :].rearrange("p c o -> p (c o)"), bank[0][:, 2 * P:4 * P]).then_inc(s_prepped, 1)
            act.wait_ge(s_nb, 1)
            with act.Fori(0, BATCH) as b:
                act.wait_ge(s_xnT_p, cnt(b, 2, 1))
                act.copy(xnT[:, :], bank[0][:, :]).then_inc(s_xnT, 1)
                act.wait_ge(s_qp_p, cnt(b, 1, 1))
                act.copy(qp[:, :], bank[1][:, :]).then_inc(s_qp, 1)
                act.wait_ge(s_va_p, cnt(b, 1, 1))
                act.copy(va[:, :, :].rearrange("p j d -> p (j d)"), bank[2][:, :]).then_inc(s_va, 1)
                act.copy(cxs[:, :], cx[:, b, :]).then_inc(s_cxs, 1)
                for i in range(GPB):
                    w = P * (i + 1)
                    act.wait_ge(s_nm, cnt(b, GPB, i + 1))
                    if i >= 2:
                        act.wait_ge(s_paT_p, cnt(b, GPB, i - 1))
                    act.activation(pa[:, i % 2, 0:w], bank[3 + i][:, 0:w], ACT.Exp, bias=amax[:, i:i + 1],
                                   scale=ATT_SCALE, accum_out=asum[:, i:i + 1]).then_inc(s_pa, 1)
                    act.wait_ge(s_paT_p, cnt(b, GPB, i + 1))
                    if i >= 2:
                        act.wait_ge(s_pv, cnt(b, GPB, i - 1))
                    tb = bank[7] if i % 2 == 0 else bank[1]
                    act.copy(paT[:, i % 2, 0:w], tb[:, 0:w]).then_inc(s_paT, 1)
                act.wait_ge(s_cxT_p, cnt(b, 1, 1))
                act.copy(cxT[:, :], bank[2][:, 0:CTX]).then_inc(s_cxT, 1)
                act.wait_ge(s_zk, cnt(b, 1, 1))
                act.activation(ek[:, 0, :], bank[2][:, P:P + CTX], ACT.Exp, bias=fmb[:, 0:1])
                act.activation(ek[:, 1, :], bank[2][:, P:P + CTX], ACT.Exp, bias=fmbn[:, 0:1],
                               scale=-1.0).then_inc(s_ek, 1)
                act.wait_ge(s_zr, cnt(b, 1, 1))
                z3 = zrow[:, :].rearrange("p (h e) -> p h e", e=XE)
                act.activation(vx[:, :, 0:XE], z3, ACT.Exp)
                act.activation(vx[:, :, XE:XF], z3, ACT.Exp, scale=-1.0).then_inc(s_vx, 1)
                act.wait_ge(s_xnT_p, cnt(b, 2, 2))
                act.copy(xnT[:, :], bank[0][:, :]).then_inc(s_xnT, 1)
                act.wait_ge(s_zq, cnt(b, 1, 1))
                act.activation(eq[:, 0, :], bank[1][:, :], ACT.Exp, bias=fmb[:, 0:1])
                act.activation(eq[:, 1, :], bank[1][:, :], ACT.Exp, bias=fmbn[:, 0:1], scale=-1.0).then_inc(s_eq, 1)
                N = GPB * NJ
                for n in range(N + 3):
                    if n < N:
                        act.wait_ge(s_xd, cnt(b, N, n + 1))
                        if n >= 2:
                            act.wait_ge(s_xpT_p, cnt(b, N, n - 1))
                            act.wait_ge(s_xm, cnt(b, N, n - 1))
                        act.activation(xp[:, n % 2, :], xd[:, n % 2, :], ACT.Exp, scale=ATT_SCALE).then_inc(s_xp, 1)
                    if 1 <= n < N + 1:
                        m = n - 1
                        act.wait_ge(s_xpT_p, cnt(b, N, m + 1))
                        if m >= 2:
                            act.wait_ge(s_xav, cnt(b, N, m - 1))
                        act.copy(xpT[:, m % 2, :], bank[5 + m % 2][0:CTX, :]).then_inc(s_xpT, 1)
                    if n >= 3 and (n - 3) % NJ == NJ - 1:
                        g = (n - 3) // NJ
                        act.wait_ge(s_xoT_p, cnt(b, GPB, g + 1))
                        act.copy(xoT[:, :, :].rearrange("p c o -> p (c o)"), bank[1][:, 0:2 * P]).then_inc(s_xoT, 1)

        @block.vector
        def _(dve):
            links = [0]

            def link(ins, wait=True):
                links[0] += 1
                ins.then_inc(s_link, 1)
                if wait:
                    dve.wait_ge(s_link, links[0])

            dve.wait_ge(s_x, 16 * BATCH)
            dve.wait_ge(s_w, 16 * len(consts))
            with dve.Fori(0, BATCH) as b:
                links[0] = 0

                def tile(j):
                    return stream[:, b * GPB + j, :]

                def norm(dst, signal):
                    layer_norm_tiles(dve, link, tile, st, mv, lw[:, 0, :], lw[:, 1, :], lw[:, 2, :], dst, signal)

                norm(lambda j: xn[:, j, :], lambda ins: ins.then_inc(s_xn, 1))
                for i in range(GPB):
                    dve.wait_ge(s_sc, cnt(b, GPB, i + 1))
                    w = P * (i + 1)
                    diag = bank[3 + i][:, P * i:w]
                    link(dve.tensor_tensor(diag, diag, causal[:, :], ALU.add))
                    link(dve.tensor_reduce(amax[:, i:i + 1], bank[3 + i][:, 0:w], AX.X, ALU.max))
                    dve.tensor_scalar(amax[:, i:i + 1], amax[:, i:i + 1], -ATT_SCALE, None, ALU.mult).then_inc(s_nm, 1)
                for i in range(GPB):
                    dve.wait_ge(s_pa, cnt(b, GPB, i + 1))
                    link(dve.reciprocal(ainv[:, i:i + 1], asum[:, i:i + 1]))
                    dve.wait_ge(s_pv, cnt(b, GPB, i + 1))
                    dve.scalar_tensor_tensor(out=tile(i), in0=bank[2 * (i % 2)][:, 0:P], scalar=ainv[:, i:i + 1],
                                             in1=tile(i), op0=ALU.mult, op1=ALU.add).then_inc(s_att, 1)
                dve.wait_ge(s_att, cnt(b, GPB, GPB))
                dve.nop(nofuse=True)
                norm(lambda j: xn[:, j, :], lambda ins: ins.then_inc(s_xn, 1))
                dve.wait_ge(s_ek, cnt(b, 1, 1))
                for e in range(2):
                    last = dve.tensor_tensor(kx[:, e, :, :], bcast(ek[:, e, :], 1, XH), bcast(hmask[:, :], 2, CTX),
                                             ALU.mult)
                last.then_inc(s_kx, 1)
                dve.tensor_tensor(zrow[:, :], bank[2][0:CTX, 2 * P:3 * P], fmrow[:, :], ALU.add).then_inc(s_zr, 1)
                N = GPB * NJ
                for n in range(N + 4):
                    if n < N:
                        dve.wait_ge(s_xs, cnt(b, N, n + 1))
                        sc = bank[3 + n % 2][:, 0:CW].rearrange("p (h s) -> p h s", h=4)
                        link(dve.tensor_reduce(xmax[:, n % 2, :], sc, AX.X, ALU.max))
                        if n >= 2:
                            dve.wait_ge(s_xp, cnt(b, N, n - 1))
                        dve.tensor_tensor(xd[:, n % 2, :].rearrange("p (h s) -> p h s", h=4), sc,
                                          bcast(xmax[:, n % 2, :], 2, CTX), ALU.subtract).then_inc(s_xd, 1)
                    if 1 <= n < N + 1:
                        m = n - 1
                        g, c = m // NJ, m % NJ
                        dve.wait_ge(s_xp, cnt(b, N, m + 1))
                        dve.tensor_reduce(xsum[:, g % 2, 4 * c:4 * c + 4],
                                          xp[:, m % 2, :].rearrange("p (h s) -> p h s", h=4),
                                          AX.X, ALU.add).then_inc(s_xm, 1)
                    if n >= 2 and (n - 2) % NJ == NJ - 1 and n - 2 < N:
                        g = (n - 2) // NJ
                        dve.wait_ge(s_xm, cnt(b, N, NJ * (g + 1)))
                        link(dve.reciprocal(xinv[:, :], xsum[:, g % 2, :]))
                        dve.wait_ge(s_xav, cnt(b, N, NJ * (g + 1)))
                        if g > 0:
                            dve.wait_ge(s_xoT_p, cnt(b, GPB, g))
                        dve.tensor_tensor(xon[:, :, :], bank[7][:, 0:XH * XF].rearrange("p (h f) -> p h f", h=XH),
                                          bcast(xinv[:, :], 2, XF), ALU.mult).then_inc(s_xon, 1)
                    if n >= 4 and (n - 4) % NJ == NJ - 1:
                        g = (n - 4) // NJ
                        dve.wait_ge(s_fc, cnt(b, GPB, g + 1))
                        link(dve.tensor_tensor(tile(g), bank[2][:, 0:D], tile(g), ALU.add))
                        dve.tensor_tensor(tile(g), tile(g), fcb[:, :], ALU.add).then_inc(s_xadd, 1)
                dve.wait_ge(s_xadd, cnt(b, GPB, GPB))
                link(dve.tensor_copy(skip[:, bass.ds(b * GPB, GPB), :], stream[:, bass.ds(b * GPB, GPB), :]))
                norm(tile, lambda ins: ins.then_inc(s_xn, 1))
                dve.wait_ge(s_xn, cnt(b, 3, 3))
                dve.sem_inc(s_link, -links[0])


def stack(nc, part, a, k, out):
    bank, stream, skip, ident, identb, maskb, rot = (
        k[n] for n in ("bank", "stream", "skip", "ident", "identb", "maskb", "rot"))

    def sb(name, shape, dt=F32):
        return part.enter_context(nc.sbuf_tensor(name, shape, dt))

    def sem(name):
        return part.enter_context(nc.semaphore(name))

    xT = sb("xT", [P, WIN + SEQ + 1])
    xs = sb("xs", [P, 2, D])
    wqkv = sb("wqkv", [P, 3 * INNER])
    wo = sb("wo", [P, PAIRS, D])
    w1 = sb("w1", [P, 2 * FF])
    w2 = sb("w2", [P, 3, D])
    lng = sb("lng", [P, 1])
    lnb = sb("lnb", [P, 1])
    b1c = sb("b1c", [P, 6])
    b2b = sb("b2b", [P, D])
    sq = sb("sq", [P, 2, 512])
    qk_c = sb("qk_c", [P, 2, 2, INNER])
    qk_s = sb("qk_s", [P, 2, 2, INNER])
    ssq = sb("ssq", [P, 2, 2 * HEADS])
    nrm = sb("nrm", [P, 2, 2 * HEADS])
    ntmp = sb("ntmp", [P, 2 * HEADS])
    qT = sb("qT", [P, PAIRS, P])
    kT = sb("kT", [P, PAIRS, WIN + SEQ])
    v_own = sb("v_own", [P, GPB, INNER])
    v_back = sb("v_back", [P, GPB, INNER])
    smax = sb("smax", [P, 2, PAIRS])
    sdif = sb("sdif", [P, 2, 512])
    prob = sb("prob", [P, 2, 2 * 512])
    psm = sb("psm", [P, 2, 8])
    pinv = sb("pinv", [P, 2, 8])
    pT = sb("pT", [P, PAIRS, P])
    att = sb("att", [P, INNER])
    attT = sb("attT", [P, PAIRS, P])
    f_x = sb("f_x", [P, GPB, D])
    f_xT = sb("f_xT", [P, SEQ + 1])
    f_n = sb("f_n", [P, GPB, D])
    f_nT = sb("f_nT", [P, SEQ])
    f_g = sb("f_g", [P, SEQ])
    f_h = sb("f_h", [P, 3, SEQ])
    st = sb("st", [P, GPB, 6])
    mv = sb("mv", [P, GPB, 2])
    lw = sb("lw", [P, 3, GPB])

    names = dict(
        zeroed="edges_zeroed", wq_in="wq_in", wk_in="wk_in", wv_in="wv_in", wo_in="wo_in", wf_in="ffn_weights_in",
        xs_r="xs_ready", xt_p="xT_made", xt_r="xT_ready", proj="proj_made", ab="cos_sin_ready", sqr="squares_ready",
        red="square_sums_ready", nr="norms_ready", rotd="rotated", qkn="qk_normed", v_r="values_ready",
        qkT_p="qkT_made", qkT_r="qkT_ready", sc="scores_made", sub="scores_read", ex="exp_ready", ps="prob_sums_ready",
        pn="prob_normed", pT_p="probT_made", pT_r="probT_ready", av="av_made", av_r="att_ready", aT_p="attT_made",
        aT_r="attT_ready", wo_p="attn_out_made", added="attn_added", misc="shared_bank_read", fx="ffn_x_ready",
        f_p="ffn_made", f1="ffn_shifted_ready", f2="ffn_shiftedT_ready", f3="ffn_normed", f4="ffn_normedT_ready",
        fg="ffn_gate_ready", fh="ffn_hidden_ready", fadd="ffn_added", link="dve_chain", flink="dve_ffn_chain",
        sum_r="out_summed", stored="out_stored", adp="att_add_done")
    s = {key: sem(name) for key, name in names.items()}

    class Step:

        def __init__(self, it, j):
            self.it, self.j = it, j

        def on(self, off):
            return not isinstance(self.it, int) or 0 <= GPB * self.it + self.j + off < GPB * NIT

        def count(self, per, off, c):
            return self.it * (per * GPB) + (per * (self.j + off) + c)

        def idx(self, off):
            return (self.j + off) % GPB

        def slot(self, off):
            return (self.it * GPB + (self.j + off)) % (BATCH * GPB)

        def par(self, off):
            return (self.j + off) % 2

    def round_on(it, back):
        return not isinstance(it, int) or 0 <= it - back < NIT

    def weights_due(it, back, dmas):
        return ((it - back) // BATCH + 1) * (16 * dmas)

    w_d = {n: a["L0_ffn_" + n] for n in ("Wqkv", "Wo", "ln_g", "ln_b", "W1", "b1", "W2", "b2")}
    LAST_LOOP = NIT

    def rounds(eng, body):
        for it in (0, 1):
            body(it)
        with eng.Fori(2, LAST_LOOP) as it:
            body(it)
        for it in (NIT, NIT + 1):
            body(it)

    with nc.Block() as block:
        @block.sync
        def _(sp):
            def load(layer, part_no):
                w = w_d["Wqkv"][layer, :, :]
                cols = slice(INNER * part_no, INNER * (part_no + 1))
                sp.dma_start(wqkv[:, cols], w[:, cols]).then_inc(s[("wq_in", "wk_in", "wv_in")[part_no]], 16)

            def load_wo(layer):
                sp.dma_start(wo[:, :, :], w_d["Wo"][layer, :, :].rearrange("(c p) d -> p c d", p=P)).then_inc(s["wo_in"], 16)

            def load_ffn(layer):
                sp.dma_start(w1[:, :], w_d["W1"][layer, :, :]).then_inc(s["wf_in"], 16)
                w2_d = w_d["W2"][layer, :, :]
                sp.dma_start(w2[:, 0:2, :], w2_d[0:2 * P, :].rearrange("(c p) d -> p c d", p=P)).then_inc(s["wf_in"], 16)
                lo, m = FCH[2]
                sp.dma_start(w2[0:m, 2, :], w2_d[lo:lo + m, :]).then_inc(s["wf_in"], 16)
                col = lambda v, n: v.rearrange("(p o) -> p o", o=1)
                sp.dma_start(lng[:, :], col(w_d["ln_g"][layer, :], 1)).then_inc(s["wf_in"], 16)
                sp.dma_start(lnb[:, :], col(w_d["ln_b"][layer, :], 1)).then_inc(s["wf_in"], 16)
                b1 = w_d["b1"][layer, :]
                for n in range(2):
                    sp.dma_start(b1c[:, 3 * n:3 * n + 2],
                                 b1[FF * n:FF * n + 2 * P].rearrange("(c p) -> p c", p=P)).then_inc(s["wf_in"], 16)
                    sp.dma_start(b1c[0:m, 3 * n + 2:3 * n + 3], col(b1[FF * n + lo:FF * n + lo + m], 1)).then_inc(s["wf_in"], 16)
                sp.dma_start(b2b[:, :], w_d["b2"][layer:layer + 1, :].broadcast_to([P, D])).then_inc(s["wf_in"], 16)

            with nc.allow_non_contiguous_dma(reason="bias columns"):
                for n in range(3):
                    load(0, n)
                load_wo(0)
                load_ffn(0)
                for layer in range(1, DEPTH):
                    g = BATCH * GPB * layer
                    for n in range(3):
                        sp.wait_ge(s["proj"], 8 * (g - 1) + (2, 4, 8)[n])
                        load(layer, n)
                    sp.wait_ge(s["wo_p"], g)
                    load_wo(layer)
                    sp.wait_ge(s["fadd"], BATCH * layer)
                    load_ffn(layer)
            sp.wait_ge(s["sum_r"], 1)
            sp.dma_start(out.rearrange("b (j p) d -> p (b j) d", p=P), skip[:, :, :]).then_inc(s["stored"], 16)
            sp.wait_ge(s["stored"], 16)

        @block.tensor
        def _(pe):
            front_job = [None]

            def shared_bank(reader, value):
                if front_job[0] is not None:
                    pe.wait_ge(*front_job[0])
                front_job[0] = (s[reader], value)

            def transpose_x(q):
                if not q.on(1):
                    return
                shared_bank("xt_r", q.count(1, 1, 1))
                pe.wait_ge(s["xs_r"], q.count(1, 1, 1))
                pe.transpose(bank[7][:, 0:P], xs[:, q.par(1), :], ident[:, :]).then_inc(s["xt_p"], 1)

            def ffn_job(q, n):
                if not round_on(q.it, 2):
                    return
                row = q.it - 2
                if n < 2:
                    shared_bank(("f1", "f2")[n], row + 1)
                elif n == 2:
                    shared_bank("f4", row + 1)
                elif n < 9:
                    shared_bank(("fg", "fh")[(n - 3) % 2], row * 3 + ((n - 3) // 2 + 1))
                else:
                    shared_bank("fadd", row + 1)
                b7 = bank[7]
                if n == 0:
                    pe.wait_ge(s["fx"], row + 1)
                    for c in range(GPB):
                        last = pe.transpose(b7[:, P * c:P * c + P], f_x[:, c, :], ident[:, :])
                elif n == 1:
                    pe.wait_ge(s["f1"], row + 1)
                    for c in range(GPB):
                        last = pe.transpose(b7[:, P * c:P * c + P], f_xT[:, P * c:P * c + P], ident[:, :])
                elif n == 2:
                    pe.wait_ge(s["wf_in"], weights_due(q.it, 2, DMAS_FFN))
                    pe.wait_ge(s["f3"], row + 1)
                    for c in range(GPB):
                        last = pe.transpose(b7[:, P * c:P * c + P], f_n[:, c, :], ident[:, :])
                elif n < 9:
                    c, value = (n - 3) // 2, (n - 3) % 2
                    lo, m = FCH[c]
                    if n == 3:
                        pe.wait_ge(s["f4"], row + 1)
                    col = lo if value else FF + lo
                    last = pe.matmul(b7[0:m, :], w1[:, col:col + m], f_nT[:, :], start=True, stop=True)
                else:
                    pe.wait_ge(s["fh"], row * 3 + 3)
                    for t in range(GPB):
                        for c, (lo, m) in enumerate(FCH):
                            last = pe.matmul(b7[:, P * t:P * t + P], f_h[0:m, c, P * t:P * t + P], w2[0:m, c, :],
                                             start=(c == 0), stop=(c == 2))
                last.then_inc(s["f_p"], 1)

            def transpose_qk(q):
                for n in range(4):
                    kind, half = n // 2, n % 2
                    if half == 0:
                        pe.wait_ge(s["qkn"], q.count(2, -2, kind + 1))
                    if kind == 0:
                        need(pe, s["pT_r"], q.count(2, -4, half + 1))
                    else:
                        pe.wait_ge(s["qkT_r"], q.count(4, -2, half + 1))
                    for c in range(4):
                        pair = 4 * half + c
                        last = pe.transpose(bank[2 + half][:, P * c:P * c + P],
                                            qk_c[:, q.par(-2), kind, P * pair:P * pair + P], ident[:, :])
                    last.then_inc(s["qkT_p"], 1)

            def scores(q, half):
                b = bank[4 + half]
                if half == 0:
                    need(pe, s["av_r"], q.count(2, -4, 2))
                else:
                    need(pe, s["sub"], q.count(2, -3, 2))
                pe.wait_ge(s["qkT_r"], q.count(4, -2, 3 + half))
                j = q.idx(-2)
                first = 1 if j == 0 else 0
                pe.matmul(b[:, :], identb[:, :], bcast(maskb[:, first, :], 1, 4), start=True, stop=False,
                          skip_group_check=True)
                for c in range(4):
                    pair = 4 * half + c
                    for w in range(4):
                        for hp in range(2):
                            half_w, wpar = w // 2, w % 2
                            r = slice(64 * hp, 64 * hp + 64)
                            o = 64 * hp + 32 * wpar
                            last = pe.matmul(
                                b[o:o + 32, P * c + 64 * half_w:P * c + 64 * half_w + 64],
                                qT[r, pair, WIN * w:WIN * w + WIN],
                                kT[r, pair, P * j + WIN * w:P * j + WIN * w + 64],
                                start=False, stop=True, skip_group_check=True)
                last.then_inc(s["sc"], 1)

            def transpose_prob(q, half):
                pe.wait_ge(s["pn"], q.count(2, -3, half + 1))
                if q.on(-4):
                    pe.wait_ge(s["aT_r"], q.count(2, -4, half + 1))
                else:
                    need(pe, s["qkT_r"], q.count(4, -2, 3 + half))
                for c in range(4):
                    last = pe.transpose(bank[2 + half][:, P * c:P * c + P],
                                        prob[:, q.par(-3), 512 * half + P * c:512 * half + P * c + P], ident[:, :])
                last.then_inc(s["pT_p"], 1)

            def attend(q, half):
                if half == 0:
                    b = bank[6]
                    need(pe, s["av_r"], q.count(2, -4, 1))
                else:
                    b = bank[4]
                    if q.on(-2):
                        pe.wait_ge(s["sub"], q.count(2, -2, 1))
                    else:
                        pe.wait_ge(s["av_r"], q.count(2, -4, 2))
                pe.wait_ge(s["pT_r"], q.count(2, -3, half + 1))
                pe.wait_ge(s["v_r"], q.count(4, -3, 3 + half))
                pe.nop(nofuse=True)
                j = q.idx(-3)
                for c in range(4):
                    pair = 4 * half + c
                    for w in range(4):
                        for hp in range(2):
                            half_w, wpar = w // 2, w % 2
                            r = slice(64 * half_w, 64 * half_w + 64)
                            v = (v_own if wpar else v_back)[r, j, DH * (2 * pair + hp):DH * (2 * pair + hp + 1)]
                            last = pe.matmul(b[WIN * w:WIN * w + WIN, DH * (2 * c + hp):DH * (2 * c + hp + 1)],
                                             pT[r, pair, 64 * hp + 32 * wpar:64 * hp + 32 * wpar + 32], v,
                                             start=True, stop=True)
                last.then_inc(s["av"], 1)

            def transpose_att(q, half):
                pe.wait_ge(s["av_r"], q.count(2, -4, half + 1))
                if q.on(-2):
                    pe.wait_ge(s["qkT_r"], q.count(4, -2, 3 + half))
                else:
                    need(pe, s["pT_r"], q.count(2, -4, half + 1))
                for c in range(4):
                    last = pe.transpose(bank[2 + half][:, P * c:P * c + P],
                                        att[:, 512 * half + P * c:512 * half + P * c + P], ident[:, :])
                last.then_inc(s["aT_p"], 1)

            def out_proj(q):
                shared_bank("added", q.count(1, -4, 1))
                pe.wait_ge(s["aT_r"], q.count(2, -4, 2))
                if q.j == 0:
                    pe.wait_ge(s["wo_in"], weights_due(q.it, 1, 1))
                for c in range(PAIRS):
                    last = pe.matmul(bank[7][:, 0:D], attT[:, c, :], wo[:, c, :], start=(c == 0), stop=(c == PAIRS - 1))
                last.then_inc(s["wo_p"], 1)

            def project(q, n):
                part_no = min(n // 2, 2)
                if q.j == 0 and n % 2 == 0 and n < 6:
                    pe.wait_ge(s[("wq_in", "wk_in", "wv_in")[part_no]], weights_due(q.it, 0, 1))
                if n < 2:
                    if n == 0:
                        pe.wait_ge(s["xt_r"], q.count(1, 0, 1))
                    need(pe, s["v_r"], q.count(4, -1, 3 + n))
                elif n < 6:
                    pe.wait_ge(s["ab"], q.count(4, 0, n - 1))
                else:
                    pe.wait_ge(s["v_r"], q.count(4, 0, n - 5))
                lo = P * q.j + (0 if n >= 6 else WIN)
                col = INNER * part_no + 512 * (n % 2)
                pe.matmul(bank[n % 2][:, :], xT[:, lo:lo + P], wqkv[:, col:col + 512],
                          start=True, stop=True).then_inc(s["proj"], 1)

            def body(it):
                first = Step(it, 0)
                if isinstance(it, int) and it > NIT:
                    front_job[0] = (s["added"], first.count(1, -5, 1))
                else:
                    front_job[0] = (s["xt_r"], first.count(1, 0, 1))
                for j in range(GPB):
                    q = Step(it, j)
                    if q.on(-2):
                        transpose_qk(q)
                    ffn_job(q, FFN_STEPS[j][0])
                    if q.on(-4):
                        transpose_att(q, 0)
                        transpose_att(q, 1)
                    if q.on(-2):
                        scores(q, 0)
                        scores(q, 1)
                    if q.on(-4):
                        out_proj(q)
                    if q.on(-3):
                        transpose_prob(q, 0)
                        transpose_prob(q, 1)
                    if len(FFN_STEPS[j]) > 1:
                        ffn_job(q, FFN_STEPS[j][1])
                    if q.on(-3):
                        attend(q, 0)
                    transpose_x(q)
                    if q.on(0):
                        for n in range(4):
                            project(q, n)
                    if len(FFN_STEPS[j]) > 2:
                        ffn_job(q, FFN_STEPS[j][2])
                    if q.on(-3):
                        attend(q, 1)
                    if q.on(0):
                        for n in range(4, 8):
                            project(q, n)
                    if len(FFN_STEPS[j]) > 3:
                        ffn_job(q, FFN_STEPS[j][3])

            pe.wait_ge(s["zeroed"], 3)
            transpose_x(Step(0, -1))
            rounds(pe, body)

        @block.scalar
        def _(act):
            def copy_x(q):
                if not q.on(2):
                    return
                need(act, s["xt_p"], q.count(1, 0, 1))
                act.copy(xs[:, q.par(2), :], stream[:, q.slot(2), :]).then_inc(s["xs_r"], 1)

            def shift_x(q):
                if not q.on(1):
                    return
                act.wait_ge(s["xt_p"], q.count(1, 1, 1))
                need(act, s["proj"], q.count(8, -2, 8))
                lo = WIN + P * q.idx(1)
                act.copy(xT[0:64, lo:lo + P], bank[7][0:64, 0:P])
                act.copy(xT[64:P, lo + 1:lo + 1 + P], bank[7][64:P, 0:P]).then_inc(s["xt_r"], 1)

            def store_qkT(q, n):
                kind, half = n // 2, n % 2
                act.wait_ge(s["qkT_p"], q.count(4, -2, n + 1))
                need(act, s["sc"], q.count(2, -3, 2))
                src = bank[2 + half][:, :].rearrange("p (c t) -> p c t", c=4)
                if kind == 0:
                    dst = qT[:, 4 * half:4 * half + 4, :]
                else:
                    lo = WIN + P * q.idx(-2)
                    dst = kT[:, 4 * half:4 * half + 4, lo:lo + P]
                act.copy(dst, src).then_inc(s["qkT_r"], 1)

            def store_attT(q, half):
                act.wait_ge(s["aT_p"], q.count(2, -4, half + 1))
                need(act, s["wo_p"], q.count(1, -5, 1))
                act.copy(attT[:, 4 * half:4 * half + 4, :].rearrange("p c t -> p (c t)"),
                         bank[2 + half][:, :]).then_inc(s["aT_r"], 1)

            def store_probT(q, half):
                act.wait_ge(s["pT_p"], q.count(2, -3, half + 1))
                need(act, s["av"], q.count(2, -4, 2))
                act.copy(pT[:, 4 * half:4 * half + 4, :].rearrange("p c t -> p (c t)"),
                         bank[2 + half][:, :]).then_inc(s["pT_r"], 1)

            def exponentials(q, half):
                act.wait_ge(s["sub"], q.count(2, -2, half + 1))
                need(act, s["pT_p"], q.count(2, -4, half + 1))
                act.activation(prob[:, q.par(-2), 512 * half:512 * half + 512], sdif[:, half, :],
                               ACT.Exp).then_inc(s["ex"], 1)

            def store_att(q, half):
                act.wait_ge(s["av"], q.count(2, -3, half + 1))
                need(act, s["aT_p"], q.count(2, -4, half + 1))
                act.copy(att[:, 512 * half:512 * half + 512], bank[6 if half == 0 else 4][:, :]).then_inc(s["av_r"], 1)

            def squares(q, n):
                act.wait_ge(s["proj"], q.count(8, 0, n + 1))
                need(act, s["red"], q.count(4, 0, n - 1))
                act.activation(sq[:, n % 2, :], bank[n % 2][:, :], ACT.Square).then_inc(s["sqr"], 1)

            def store_values(q, n):
                act.wait_ge(s["proj"], q.count(8, 0, 5 + n))
                need(act, s["av"], q.count(2, -4, 2))
                dst = v_own if n < 2 else v_back
                act.copy(dst[:, q.idx(0), 512 * (n % 2):512 * (n % 2) + 512], bank[n % 2][:, :]).then_inc(s["v_r"], 1)

            def ffn_job(q, n):
                if not round_on(q.it, 2):
                    return
                row = q.it - 2
                if n in (0, 1, 2, 3, 5, 7):
                    act.wait_ge(s["f_p"], row * FJOBS + (n + 1))
                if n == 0:
                    act.copy(f_xT[0:64, 0:SEQ], bank[7][0:64, :])
                    act.copy(f_xT[64:P, 1:SEQ + 1], bank[7][64:P, :]).then_inc(s["f1"], 1)
                elif n == 1:
                    act.copy(f_x[:, :, :].rearrange("p j d -> p (j d)"), bank[7][:, :]).then_inc(s["f2"], 1)
                elif n == 2:
                    act.activation(f_nT[:, :], bank[7][:, :], ACT.Identity, bias=lnb[:, 0:1],
                                   scale=lng[:, 0:1]).then_inc(s["f4"], 1)
                elif n in (3, 5, 7):
                    c = (n - 3) // 2
                    m = FCH[c][1]
                    if c > 0:
                        act.wait_ge(s["fh"], row * 3 + c)
                    act.activation(f_g[0:m, :], bank[7][0:m, :], ACT.Gelu,
                                   bias=b1c[0:m, 3 + c:4 + c]).then_inc(s["fg"], 1)

            def copy_row(it):
                if not round_on(it, 2):
                    return
                act.wait_ge(s["added"], (it - 1) * GPB)
                act.copy(f_x[:, :, :], stream[:, bass.ds(((it - 2) % BATCH) * GPB, GPB), :]).then_inc(s["fx"], 1)

            def body(it):
                copy_row(it)
                for j in range(GPB):
                    q = Step(it, j)
                    if q.on(-2):
                        for n in range(4):
                            store_qkT(q, n)
                    ffn_job(q, FFN_STEPS[j][0])
                    if q.on(-4):
                        store_attT(q, 0)
                        store_attT(q, 1)
                    if q.on(-3):
                        store_probT(q, 0)
                        store_probT(q, 1)
                    if q.on(-2):
                        exponentials(q, 0)
                        exponentials(q, 1)
                    if len(FFN_STEPS[j]) > 1:
                        ffn_job(q, FFN_STEPS[j][1])
                    if q.on(-3):
                        store_att(q, 0)
                    shift_x(q)
                    if q.on(0):
                        for n in range(4):
                            squares(q, n)
                    if len(FFN_STEPS[j]) > 2:
                        ffn_job(q, FFN_STEPS[j][2])
                    if q.on(-3):
                        store_att(q, 1)
                    if q.on(0):
                        for n in range(4):
                            store_values(q, n)
                    if len(FFN_STEPS[j]) > 3:
                        ffn_job(q, FFN_STEPS[j][3])
                    copy_x(q)

            act.wait_ge(s["zeroed"], 3)
            copy_x(Step(0, -2))
            copy_x(Step(0, -1))
            shift_x(Step(0, -1))
            rounds(act, body)

        @block.gpsimd
        def _(pool):
            def normalise(q, kind):
                pool.wait_ge(s["nr"], q.count(1, -1, 1))
                pool.wait_ge(s["rotd"], q.count(2, -1, kind + 1))
                x = qk_c[:, q.par(-1), kind, :].rearrange("p (h d) -> p h d", d=DH)
                pool.tensor_tensor(x, x, bcast(nrm[:, q.par(-1), HEADS * kind:HEADS * (kind + 1)], 2, DH),
                                   ALU.mult).then_inc(s["qkn"], 1)

            def normalise_prob(q, half):
                pool.wait_ge(s["ps"], q.count(2, -2, half + 1))
                x = prob[:, q.par(-2), 512 * half:512 * half + 512].rearrange("p (c s) -> p c s", s=64)
                pool.tensor_tensor(x, x, bcast(pinv[:, half, :], 2, 64), ALU.mult).then_inc(s["pn"], 1)

            def rotate(q, kind):
                pool.wait_ge(s["ab"], q.count(4, 0, 2 * kind + 2))
                x = qk_c[:, q.par(0), kind, :]
                pool.tensor_tensor(x, x, qk_s[:, q.par(0), kind, :], ALU.add).then_inc(s["rotd"], 1)

            def body(it):
                for j in range(GPB):
                    q = Step(it, j)
                    if q.on(-1):
                        normalise(q, 0)
                        normalise(q, 1)
                    if q.on(-2):
                        normalise_prob(q, 0)
                        normalise_prob(q, 1)
                    if q.on(0):
                        rotate(q, 0)
                        rotate(q, 1)

            pool.memset(xT[:, 0:WIN + 1], 0.0).then_inc(s["zeroed"], 1)
            pool.memset(kT[:, :, 0:WIN], 0.0).then_inc(s["zeroed"], 1)
            pool.memset(f_xT[:, 0:1], 0.0).then_inc(s["zeroed"], 1)
            rounds(pool, body)

        @block.vector
        def _(dve):
            links = [0]

            def link(ins):
                links[0] += 1
                ins.then_inc(s["link"], 1)
                return links[0]

            def linked(n):
                dve.wait_ge(s["link"], n)

            norm_link = [0]

            def norm_step(q, n):
                if not q.on(-1):
                    return
                w, y = ssq[:, q.par(-1), :], nrm[:, q.par(-1), :]
                if n == 0:
                    dve.wait_ge(s["red"], q.count(4, -1, 4))
                    norm_link[0] = link(dve.tensor_scalar(w, w, 1e-24, None, ALU.max))
                    return
                linked(norm_link[0])
                if n == 1:
                    need(dve, s["qkn"], q.count(2, -3, 2))
                    norm_link[0] = link(rsqrt_guess(dve, y, w))
                    return
                ins = rsqrt_step(dve, (n - 2) % 3, y, w, ntmp[:, :])
                if n == 10:
                    ins.then_inc(s["nr"], 1)
                else:
                    norm_link[0] = link(ins)

            def score_max(q, half):
                dve.wait_ge(s["sc"], q.count(2, -2, half + 1))
                b = bank[4 + half][:, :].rearrange("p (c s) -> p c s", s=64)
                return link(dve.tensor_reduce(smax[:, half, :], b, AX.X, ALU.max))

            def score_sub(q, half, after):
                linked(after)
                need(dve, s["ex"], q.count(2, -3, half + 1))
                b = bank[4 + half][:, :].rearrange("p (c s) -> p c s", s=64)
                dve.tensor_tensor(sdif[:, half, :].rearrange("p (c s) -> p c s", s=64), b,
                                  bcast(smax[:, half, :], 2, 64), ALU.subtract).then_inc(s["sub"], 1)

            def prob_sum(q, half):
                dve.wait_ge(s["ex"], q.count(2, -2, half + 1))
                x = prob[:, q.par(-2), 512 * half:512 * half + 512].rearrange("p (c s) -> p c s", s=64)
                return link(dve.tensor_reduce(psm[:, half, :], x, AX.X, ALU.add))

            def prob_inv(q, half, after):
                linked(after)
                need(dve, s["pn"], q.count(2, -3, half + 1))
                dve.reciprocal(pinv[:, half, :], psm[:, half, :]).then_inc(s["ps"], 1)

            def add_attention(q):
                dve.wait_ge(s["wo_p"], q.count(1, -4, 1))
                x = stream[:, q.slot(-4), :]
                dve.tensor_tensor(x, bank[7][:, 0:D], x, ALU.add).then_inc(s["added"], 1)

            def cos_part(q, n):
                kind, half = n // 2, n % 2
                dve.wait_ge(s["sqr"], q.count(4, 0, n + 1))
                need(dve, s["qkT_p"], q.count(4, -2, 2 * kind + 2))
                dve.tensor_tensor(
                    qk_c[:, q.par(0), kind, 512 * half:512 * half + 512].rearrange("p (h d) -> p h d", d=DH),
                    bank[n % 2][:, :].rearrange("p (h d) -> p h d", d=DH),
                    bcast(table(q, 2 * kind), 1, 8), ALU.mult)

            def sin_part(q, n):
                kind, half = n // 2, n % 2
                b = bank[n % 2][:, :].rearrange("p (h r d) -> p h r d", r=2, d=DH // 2)
                dst = qk_s[:, q.par(0), kind, 512 * half:512 * half + 512].rearrange("p (h r d) -> p h r d", r=2, d=DH // 2)
                dve.tensor_tensor(dst[:, :, ::-1, :], b,
                                  bcast(table(q, 2 * kind + 1).rearrange("p (r d) -> p r d", r=2), 1, 8),
                                  ALU.mult).then_inc(s["ab"], 1)

            def table(q, kind):
                layer = q.it // BATCH
                lo = (layer * 4 + kind) * (GPB * DH) + q.j * DH
                flat = rot[:, :, :, :].rearrange("p l k n -> p (l k n)")
                return flat[:, lo:lo + DH] if isinstance(lo, int) else flat[:, bass.ds(lo, DH)]

            def square_sum(q, n):
                dve.wait_ge(s["sqr"], q.count(4, 0, n + 1))
                dve.tensor_reduce(ssq[:, q.par(0), 8 * n:8 * n + 8],
                                  sq[:, n % 2, :].rearrange("p (h d) -> p h d", d=DH),
                                  AX.X, ALU.add).then_inc(s["red"], 1)

            def ffn_norm(it):
                if not round_on(it, 2):
                    return
                dve.wait_ge(s["f2"], it - 1)

                def chain(ins, wait=True):
                    n = link(ins)
                    if wait:
                        linked(n)

                layer_norm_tiles(dve, chain, lambda j: f_x[:, j, :], st, mv, lw[:, 0, :], lw[:, 1, :], lw[:, 2, :],
                                 lambda j: f_n[:, j, :], lambda ins: ins.then_inc(s["f3"], 1))

            def ffn_job(q, n):
                if not round_on(q.it, 2):
                    return
                row = q.it - 2
                if n in (4, 6, 8):
                    c = (n - 3) // 2
                    m = FCH[c][1]
                    dve.wait_ge(s["f_p"], row * FJOBS + (n + 1))
                    dve.wait_ge(s["fg"], row * 3 + (c + 1))
                    dve.scalar_tensor_tensor(out=f_h[0:m, c, :], in0=bank[7][0:m, :], scalar=b1c[0:m, c:c + 1],
                                             in1=f_g[0:m, :], op0=ALU.add, op1=ALU.mult).then_inc(s["fh"], 1)
                elif n == 9:
                    dve.wait_ge(s["f_p"], row * FJOBS + (n + 1))
                    x = stream[:, bass.ds((row % BATCH) * GPB, GPB), :]
                    linked(link(dve.tensor_tensor(x, bank[7][:, :].rearrange("p (j d) -> p j d", d=D), x, ALU.add)))
                    dve.tensor_tensor(x, x, bcast(b2b[:, :], 1, GPB), ALU.add).then_inc(s["fadd"], 1)

            def body(it):
                links[0] = 0
                for j in range(GPB):
                    q = Step(it, j)
                    norm_step(q, 0)
                    ffn_job(q, FFN_STEPS[j][0])
                    norm_step(q, 1)
                    if q.on(-2):
                        m0 = score_max(q, 0)
                        norm_step(q, 2)
                        score_sub(q, 0, m0)
                        norm_step(q, 3)
                        m1 = score_max(q, 1)
                        norm_step(q, 4)
                        score_sub(q, 1, m1)
                    else:
                        for n in range(2, 5):
                            norm_step(q, n)
                    norm_step(q, 5)
                    if q.on(-4):
                        add_attention(q)
                    norm_step(q, 6)
                    if len(FFN_STEPS[j]) > 1:
                        ffn_job(q, FFN_STEPS[j][1])
                    norm_step(q, 7)
                    if q.on(-2):
                        p0 = prob_sum(q, 0)
                        norm_step(q, 8)
                        p1 = prob_sum(q, 1)
                        norm_step(q, 9)
                        prob_inv(q, 0, p0)
                        norm_step(q, 10)
                        prob_inv(q, 1, p1)
                    else:
                        for n in range(8, 11):
                            norm_step(q, n)
                    if q.on(0):
                        for n in range(4):
                            cos_part(q, n)
                            sin_part(q, n)
                            square_sum(q, n)
                    if len(FFN_STEPS[j]) > 2:
                        ffn_job(q, FFN_STEPS[j][2])
                    if j == 0:
                        ffn_norm(it)
                    if len(FFN_STEPS[j]) > 3:
                        ffn_job(q, FFN_STEPS[j][3])
                if links[0]:
                    linked(links[0])
                    dve.sem_inc(s["link"], -links[0])

            rounds(dve, body)
            dve.wait_ge(s["fadd"], NIT)
            dve.tensor_tensor(skip[:, :, :], skip[:, :, :], stream[:, :, :], ALU.add).then_inc(s["sum_r"], 1)


_INS = ['x', 'ctx_1024', 'L0_attn_W_query', 'L0_attn_W_key', 'L0_attn_W_value', 'L0_xattn_fm_w', 'L0_xattn_fm_b',
        'L0_xattn_fc_w', 'L0_xattn_fc_b', 'L0_ffn_Wqkv', 'L0_ffn_q_scale', 'L0_ffn_k_scale', 'L0_ffn_Wo',
        'L0_ffn_ln_g', 'L0_ffn_ln_b', 'L0_ffn_W1', 'L0_ffn_b1', 'L0_ffn_W2', 'L0_ffn_b2']
_OUTS = [((4, 512, 128), 'float32')]


def kernel(**inputs):
    import numpy as _np
    import concourse.bacc as _bacc
    from concourse import mybir as _mybir
    from concourse.bass_utils import run_bass_kernel_spmd as _run

    nc = _bacc.Bacc("TRN2", target_bir_lowering=False, num_devices=1)
    arrays, args = {}, {}
    for name in _INS:
        a = _np.ascontiguousarray(inputs[name])
        arrays[f"in_{name}_dram"] = a
        args[name] = nc.dram_tensor(f"in_{name}_dram", a.shape, _mybir.dt.from_np(a.dtype), kind="ExternalInput").ap()
    outs = []
    for i, (shape, dtype) in enumerate(_OUTS):
        dt = _mybir.dt.from_np(_np.dtype(dtype))
        outs.append(nc.dram_tensor(f"out_{i}_dram", shape, dt, kind="ExternalOutput").ap())
    decoder(nc, args, *outs)
    r = _run(nc, [arrays], core_ids=[0])
    got = tuple(r.results[0][f"out_{i}_dram"] for i in range(len(_OUTS)))
    return got[0]
```

```python
from contextlib import ExitStack

import numpy as np

import concourse.bass as bass
from concourse import mybir

ALU = mybir.AluOpType
ACT = mybir.ActivationFunctionType
AX = mybir.AxisListType
F32 = mybir.dt.float32
F32R = mybir.dt.float32r
I32 = mybir.dt.int32

P = 128
D = 128
BATCH, SEQ = 4, 512
GPB = SEQ // P
DEPTH = 6
NIT = DEPTH * BATCH
HEADS, DH = 16, 64
INNER = HEADS * DH
WIN = 32
PAIRS = HEADS // 2
FF = 341
FCH = [(0, 128), (128, 128), (256, FF - 256)]
CTX = 77
XH, XE, XF = 16, 8, 16
ATT_SCALE = 1.0 / float(np.sqrt(128.0))
NEG = -1e30
RSQRT_MAGIC = float(0x5F3759DF)
LN_EPS = 1e-5
FFN_PLACES = {(0, 2): 0, (0, 3): 1, (2, 2): 2, (2, 4): 3, (2, 5): 4, (3, 0): 5, (3, 1): 6, (3, 2): 7, (3, 3): 8, (3, 5): 9}
FJOBS = 10
DMAS_FFN = 10


def rotary_tables():
    f = np.float32
    half = np.arange(0, DH, 2, dtype=f)
    inv_freq = (f(1.0) / np.power(f(10000.0), half / f(DH))).astype(f)
    t = np.arange(SEQ, dtype=f)
    ang = (t[:, None] * inv_freq[None, :]).astype(f).astype(np.float64)
    base = ((half + f(0.4 * DH)) / f(1.4 * DH)).astype(f)
    power = ((t - SEQ // 2) / f(WIN // 2)).astype(f)
    scale = np.power(base[None, :].astype(np.float64), power[:, None].astype(np.float64))
    cos, sin = np.cos(ang), np.sin(ang)
    kinds = []
    for s in (8.0 * scale, 1.0 / scale):
        kinds.append(np.concatenate([cos * s, cos * s], 1))
        kinds.append(np.concatenate([sin * s, -sin * s], 1))
    tab = np.stack(kinds, 1).astype(f)
    return np.ascontiguousarray(tab.reshape(GPB, P, 4, DH).transpose(1, 2, 0, 3))


def window_masks():
    m = np.zeros((2, P, 2, 64), np.float32)
    q = np.arange(WIN)[:, None]
    c = np.arange(WIN)[None, :]
    blk = np.concatenate([np.where(c >= q, 0.0, NEG), np.where(c <= q, 0.0, NEG)], 1)
    for first in range(2):
        for hp in range(2):
            for wpar in range(2):
                rows = slice(hp * 64 + wpar * 32, hp * 64 + wpar * 32 + 32)
                for half in range(2):
                    b = blk.copy()
                    if first and half == 0 and wpar == 0:
                        b[:, :WIN] = NEG
                    m[first, rows, half, :] = b
    return np.ascontiguousarray(m.reshape(2, P, P).transpose(1, 0, 2))


def causal_mask():
    q = np.arange(P)[:, None]
    return np.where(np.arange(P)[None, :] <= q, 0.0, NEG).astype(np.float32)


def head_mask():
    return (np.arange(P)[:, None] // XE == np.arange(XH)[None, :]).astype(np.float32)


def cnt(it, per, c):
    return it * per + c


def need(eng, semaphore, value):
    if isinstance(value, int) and value <= 0:
        return
    eng.wait_ge(semaphore, value)


def rsqrt_guess(v, y, w):
    return v.tensor_scalar(y.bitcast(I32), w.bitcast(I32), -0.5, RSQRT_MAGIC, ALU.mult, ALU.add)


def rsqrt_step(v, n, y, w, t):
    if n == 0:
        return v.scalar_tensor_tensor(out=t, in0=y, scalar=-0.5, in1=y, op0=ALU.mult, op1=ALU.mult)
    if n == 1:
        return v.tensor_tensor(t, t, w, ALU.mult)
    return v.scalar_tensor_tensor(out=y, in0=t, scalar=1.5, in1=y, op0=ALU.add, op1=ALU.mult)


def bcast(ap, axis, n):
    u = ap.unsqueeze(axis)
    shape = list(u.shape)
    shape[axis] = n
    return u.broadcast_to(shape)


def rows(dram, n):
    return bass.AP(tensor=dram.tensor, offset=dram.offset, ap=[[0, n]] + [list(x) for x in dram.ap])


def decoder(nc, a, out):
    with ExitStack() as ctx:
        def sb(name, shape, dt=F32):
            return ctx.enter_context(nc.sbuf_tensor(name, shape, dt))

        k = dict(
            bank=[ctx.enter_context(nc.psum_tensor(f"bank{i}", [P, 512], F32)) for i in range(8)],
            table_d=nc.inline_tensor(rotary_tables(), "rotary_const").ap(),
            mask_d=nc.inline_tensor(window_masks(), "mask_const").ap(),
            causal_d=nc.inline_tensor(causal_mask(), "causal_const").ap(),
            hmask_d=nc.inline_tensor(head_mask(), "head_const").ap(),
            stream=sb("stream", [P, BATCH * GPB, D]),
            skip=sb("skip", [P, BATCH * GPB, D]),
            ident=sb("ident", [P, P]),
            mask=sb("mask", [P, 2, P]),
            w_hi=nc.dram_tensor("proj_w_high", [DEPTH, P, 3 * INNER], F32, kind="Internal").ap(),
            w_lo=nc.dram_tensor("proj_w_low", [DEPTH, P, 3 * INNER], F32, kind="Internal").ap(),
            rot=sb("rot", [P, DEPTH, 4, GPB * DH]),
        )
        with ExitStack() as part:
            front(nc, part, a, k)
        with ExitStack() as part:
            stack(nc, part, a, k, out)


def layer_norm_tiles(dve, link, src, st, mv, w, y, t, dst, last):
    for j in range(GPB):
        link(dve.bn_stats(st[:, j, :], src(j)), j == GPB - 1)
    for j in range(GPB):
        link(dve.bn_aggr(mv[:, j, :], st[:, j, :]), j == GPB - 1)
    link(dve.tensor_scalar(w, mv[:, :, 1], LN_EPS, None, ALU.add))
    link(rsqrt_guess(dve, y, w))
    for _ in range(3):
        for n in range(3):
            link(rsqrt_step(dve, n, y, w, t))
    for j in range(GPB):
        ins = dve.tensor_scalar(dst(j), src(j), mv[:, j, 0:1], y[:, j:j + 1], ALU.subtract, ALU.mult)
    last(ins)


def front(nc, part, a, k):
    bank, stream, skip, ident, mask, rot = (k[n] for n in ("bank", "stream", "skip", "ident", "mask", "rot"))

    def sb(name, shape, dt=F32):
        return part.enter_context(nc.sbuf_tensor("front_" + name, shape, dt))

    def sem(name):
        return part.enter_context(nc.semaphore("front_" + name))

    NJ = XH // 4
    CW = 4 * CTX
    table = sb("table", [P, 4, GPB * DH])
    qscl = sb("qscl", [P, DEPTH, DH])
    kscl = sb("kscl", [P, DEPTH, DH])
    raw = sb("raw", [P, 3, INNER])
    high = sb("high", [P, 3, INNER], F32R)
    low = sb("low", [P, 3, INNER], F32R)
    causal = sb("causal", [P, P])
    hmask = sb("hmask", [P, XH])
    fmb = sb("fmb", [P, 1])
    fmbn = sb("fmbn", [P, 1])
    fmrow = sb("fmrow", [CTX, P])
    fcb = sb("fcb", [P, D])
    bd = sb("bd", [P, P])
    fcw = sb("fcw", [P, 2, P])
    fcT = sb("fcT", [P, 2, P])
    wq = sb("wq", [P, P])
    wk = sb("wk", [P, P])
    wv = sb("wv", [P, P])
    mqk = sb("mqk", [P, P])
    wvT = sb("wvT", [P, P])
    cx = sb("cx", [CTX, BATCH, D])
    cxs = sb("cxs", [CTX, D])
    cxT = sb("cxT", [P, CTX])
    ek = sb("ek", [P, 2, CTX])
    zrow = sb("zrow", [CTX, P])
    vx = sb("vx", [CTX, XH, XF])
    kx = sb("kx", [P, 2, XH, CTX])
    xn = sb("xn", [P, GPB, D])
    xnT = sb("xnT", [P, SEQ])
    qp = sb("qp", [P, SEQ])
    va = sb("va", [P, GPB, D])
    eq = sb("eq", [P, 2, SEQ])
    pa = sb("pa", [P, 2, SEQ])
    paT = sb("paT", [P, 2, SEQ])
    xd = sb("xd", [P, 2, CW])
    xp = sb("xp", [P, 2, CW])
    xpT = sb("xpT", [CTX, 2, 512])
    xon = sb("xon", [P, XH, XF])
    xoT = sb("xoT", [P, 2, P])
    st = sb("st", [P, GPB, 6])
    mv = sb("mv", [P, GPB, 2])
    lw = sb("lw", [P, 3, GPB])
    amax = sb("amax", [P, GPB])
    asum = sb("asum", [P, GPB])
    ainv = sb("ainv", [P, GPB])
    xmax = sb("xmax", [P, 2, 4])
    xsum = sb("xsum", [P, 2, XH])
    xinv = sb("xinv", [P, XH])

    s_x, s_w, s_zero, s_bd, s_id = sem("x_in"), sem("weights_in"), sem("bd_zeroed"), sem("bd_in"), sem("ident_made")
    s_const, s_nb, s_prep, s_prepped = sem("const_ready"), sem("fmbn_ready"), sem("prep_made"), sem("prep_out")
    s_xn, s_xnT_p, s_xnT = sem("xn_ready"), sem("xnT_made"), sem("xnT_ready")
    s_qp_p, s_qp, s_va_p, s_va = sem("qp_made"), sem("qp_ready"), sem("va_made"), sem("va_ready")
    s_sc, s_nm, s_pa, s_paT_p, s_paT = sem("scores_made"), sem("max_ready"), sem("p_ready"), sem("pT_made"), sem("pT_ready")
    s_pv, s_att = sem("pv_made"), sem("att_added")
    s_cxs, s_cxT_p, s_cxT, s_zk, s_ek, s_zr, s_vx, s_kx = (
        sem(n) for n in ("cxs_ready", "cxT_made", "cxT_ready", "zk_made", "ek_ready", "zrow_ready", "vx_ready", "kx_ready"))
    s_zq, s_eq = sem("zq_made"), sem("eq_ready")
    s_xs, s_xd, s_xp, s_xm, s_xpT_p, s_xpT = (
        sem(n) for n in ("xscores_made", "xdiff_ready", "xp_ready", "xsum_ready", "xpT_made", "xpT_ready"))
    s_xav, s_xon, s_xoT_p, s_xoT, s_fc, s_xadd = (
        sem(n) for n in ("xav_made", "xon_ready", "xoT_made", "xoT_ready", "fc_made", "xatt_added"))
    s_link = sem("dve_link")
    s_raw = [sem(f"raw_in_{c}") for c in range(3)]
    s_wst = [sem(f"parts_stored_{c}") for c in range(3)]
    s_high, s_low = sem("high_ready"), sem("low_ready")
    consts = [
        (table[:, :, :].rearrange("p k (j d) -> p k j d", d=DH), k["table_d"]),
        (mask[:, :, :], k["mask_d"]), (causal[:, :], k["causal_d"]), (hmask[:, :], k["hmask_d"]),
        (qscl[:, :, :], rows(a["L0_ffn_q_scale"], P)), (kscl[:, :, :], rows(a["L0_ffn_k_scale"], P)),
        (wq[:, :], a["L0_attn_W_query"]), (wk[:, :], a["L0_attn_W_key"]), (wv[:, :], a["L0_attn_W_value"]),
        (cx[:, :, :], a["ctx_1024"].rearrange("b s d -> s b d")),
        (fcw[:, :, :], a["L0_xattn_fc_w"].rearrange("o (c f) -> o c f", c=2)),
        (fcb[:, :], rows(a["L0_xattn_fc_b"], P)),
        (fmrow[:, :], bass.AP(tensor=a["L0_xattn_fm_b"].tensor, offset=0, ap=[[0, CTX], [0, XH], [1, XE]])),
        (fmb[:, :], bass.AP(tensor=a["L0_xattn_fm_b"].tensor, offset=0, ap=[[0, XH], [1, XE], [1, 1]])),
    ]
    x_d = a["x"].rearrange("b (j p) d -> p (b j) d", p=P)

    with nc.Block() as block:
        @block.sync
        def _(sp):
            for b in range(BATCH):
                sp.dma_start(stream[:, GPB * b:GPB * (b + 1), :], x_d[:, GPB * b:GPB * (b + 1), :]).then_inc(s_x, 16)
            for dst, src in consts[:7]:
                sp.dma_start(dst, src).then_inc(s_w, 16)
            sp.wait_ge(s_zero, 1)
            with nc.allow_non_contiguous_dma(reason="8 x 8 transposed blocks"):
                for h in range(XH):
                    r = slice(XE * h, XE * h + XE)
                    sp.dma_start(bd[r, r], a["L0_xattn_fm_w"].rearrange("e d -> d e")).then_inc(s_bd, 16)

            def split(layer):
                for c in range(3):
                    need(sp, s_low, 3 * layer + (c - 2))
                    sp.dma_start(raw[:, c, :], a["L0_ffn_Wqkv"][layer, :, INNER * c:INNER * (c + 1)]).then_inc(s_raw[c], 16)
                for c in range(3):
                    sp.wait_ge(s_low, 3 * layer + (c + 1))
                    sp.dma_start(k["w_hi"][layer, :, INNER * c:INNER * (c + 1)], high[:, c, :].bitcast(F32)).then_inc(s_wst[c], 16)
                    sp.dma_start(k["w_lo"][layer, :, INNER * c:INNER * (c + 1)], low[:, c, :].bitcast(F32)).then_inc(s_wst[c], 16)

            split(0)
            with sp.Fori(1, DEPTH) as layer:
                split(layer)
            for c in range(3):
                sp.wait_ge(s_wst[c], 32 * DEPTH)

        @block.gpsimd
        def _(pool):
            pool.memset(bd[:, :], 0.0).then_inc(s_zero, 1)
            pool.memset(ident[:, :], 0.0).then_inc(s_id, 1)
            pool.wait_ge(s_id, 1)
            pool.affine_select(out=ident[:, :], in_=ident[:, :], compare_op=ALU.not_equal, fill=1.0, base=0,
                               pattern=[[-1, P]], channel_multiplier=1).then_inc(s_id, 1)
            pool.wait_ge(s_w, 16 * len(consts))
            for layer in range(DEPTH):
                for n, scl in enumerate((qscl, kscl)):
                    pool.tensor_tensor(
                        rot[:, layer, 2 * n:2 * n + 2, :].rearrange("p k (j d) -> p (k j) d", d=DH),
                        table[:, 2 * n:2 * n + 2, :].rearrange("p k (j d) -> p (k j) d", d=DH),
                        bcast(scl[:, layer, :], 1, 2 * GPB), ALU.mult).then_inc(s_const, 1)

            def split(layer):
                for c in range(3):
                    pool.wait_ge(s_raw[c], 16 * (layer + 1))
                    need(pool, s_wst[c], 32 * layer)
                    pool.nop(nofuse=True)
                    pool.tensor_copy(high[:, c, :], raw[:, c, :]).then_inc(s_high, 1)
                    pool.wait_ge(s_high, 3 * layer + (c + 1))
                    pool.tensor_tensor(low[:, c, :], raw[:, c, :], high[:, c, :].bitcast(F32),
                                       ALU.subtract).then_inc(s_low, 1)

            split(0)
            with pool.Fori(1, DEPTH) as layer:
                split(layer)

        @block.tensor
        def _(pe):
            pe.wait_ge(s_id, 2)
            pe.wait_ge(s_w, 16 * len(consts))
            pe.matmul(bank[0][:, 0:P], wq[:, :], wk[:, :], start=True, stop=True)
            pe.transpose(bank[0][:, P:2 * P], wv[:, :], ident[:, :])
            pe.transpose(bank[0][:, 2 * P:3 * P], fcw[:, 0, :], ident[:, :])
            pe.transpose(bank[0][:, 3 * P:4 * P], fcw[:, 1, :], ident[:, :]).then_inc(s_prep, 1)
            pe.wait_ge(s_bd, 16 * XH)
            pe.wait_ge(s_prepped, 1)
            with pe.Fori(0, BATCH) as b:
                pe.wait_ge(s_xn, cnt(b, 3, 1))
                for j in range(GPB):
                    last = pe.transpose(bank[0][:, P * j:P * j + P], xn[:, j, :], ident[:, :])
                last.then_inc(s_xnT_p, 1)
                pe.wait_ge(s_xnT, cnt(b, 2, 1))
                pe.matmul(bank[1][:, :], mqk[:, :], xnT[:, :], start=True, stop=True).then_inc(s_qp_p, 1)
                for j in range(GPB):
                    last = pe.matmul(bank[2][:, P * j:P * j + P], xnT[:, P * j:P * j + P], wvT[:, :],
                                     start=True, stop=True)
                last.then_inc(s_va_p, 1)
                pe.wait_ge(s_qp, cnt(b, 1, 1))
                for i in range(GPB):
                    pe.matmul(bank[3 + i][:, 0:P * (i + 1)], qp[:, P * i:P * i + P], xnT[:, 0:P * (i + 1)],
                              start=True, stop=True).then_inc(s_sc, 1)
                pe.wait_ge(s_va, cnt(b, 1, 1))
                for i in range(GPB):
                    pe.wait_ge(s_pa, cnt(b, GPB, i + 1))
                    if i >= 2:
                        pe.wait_ge(s_paT, cnt(b, GPB, i - 1))
                    tb = bank[7] if i % 2 == 0 else bank[1]
                    for c in range(i + 1):
                        last = pe.transpose(tb[:, P * c:P * c + P], pa[:, i % 2, P * c:P * c + P], ident[:, :])
                    last.then_inc(s_paT_p, 1)
                    pe.wait_ge(s_paT, cnt(b, GPB, i + 1))
                    if i >= 2:
                        pe.wait_ge(s_att, cnt(b, GPB, i - 1))
                    for c in range(i + 1):
                        last = pe.matmul(bank[2 * (i % 2)][:, 0:P], paT[:, i % 2, P * c:P * c + P], va[:, c, :],
                                         start=(c == 0), stop=(c == i))
                    last.then_inc(s_pv, 1)
                pe.wait_ge(s_att, cnt(b, GPB, GPB))
                pe.wait_ge(s_cxs, cnt(b, 1, 1))
                pe.transpose(bank[2][:, 0:CTX], cxs[:, :], ident[0:CTX, 0:CTX]).then_inc(s_cxT_p, 1)
                pe.wait_ge(s_cxT, cnt(b, 1, 1))
                pe.matmul(bank[2][:, P:P + CTX], bd[:, :], cxT[:, :], start=True, stop=True)
                pe.matmul(bank[2][0:CTX, 2 * P:3 * P], cxT[:, :], bd[:, :], start=True, stop=True).then_inc(s_zk, 1)
                pe.wait_ge(s_xn, cnt(b, 3, 2))
                for j in range(GPB):
                    last = pe.transpose(bank[0][:, P * j:P * j + P], xn[:, j, :], ident[:, :])
                last.then_inc(s_xnT_p, 1)
                pe.wait_ge(s_xnT, cnt(b, 2, 2))
                pe.matmul(bank[1][:, :], bd[:, :], xnT[:, :], start=True, stop=True).then_inc(s_zq, 1)
                pe.wait_ge(s_eq, cnt(b, 1, 1))
                pe.wait_ge(s_kx, cnt(b, 1, 1))
                pe.wait_ge(s_vx, cnt(b, 1, 1))
                N = GPB * NJ
                for n in range(N + 3):
                    if n < N:
                        g, c = n // NJ, n % NJ
                        if n >= 2:
                            pe.wait_ge(s_xd, cnt(b, N, n - 1))
                        sc = bank[3 + n % 2][:, 0:CW]
                        for e in range(2):
                            last = pe.matmul(sc, eq[:, e, P * g:P * g + P],
                                             kx[:, e, 4 * c:4 * c + 4, :].rearrange("p h s -> p (h s)"),
                                             start=(e == 0), stop=(e == 1))
                        last.then_inc(s_xs, 1)
                    if 1 <= n < N + 1:
                        m = n - 1
                        pe.wait_ge(s_xp, cnt(b, N, m + 1))
                        if m >= 2:
                            pe.wait_ge(s_xpT, cnt(b, N, m - 1))
                        for h in range(4):
                            last = pe.transpose(bank[5 + m % 2][0:CTX, P * h:P * h + P],
                                                xp[:, m % 2, CTX * h:CTX * h + CTX], ident[:, :])
                        last.then_inc(s_xpT_p, 1)
                    if 2 <= n < N + 2:
                        m = n - 2
                        g, c = m // NJ, m % NJ
                        pe.wait_ge(s_xpT, cnt(b, N, m + 1))
                        if c == 0 and g > 0:
                            pe.wait_ge(s_xon, cnt(b, GPB, g))
                        for h in range(4):
                            hh = 4 * c + h
                            last = pe.matmul(bank[7][:, XF * hh:XF * hh + XF], xpT[:, m % 2, P * h:P * h + P],
                                             vx[:, hh, :], start=True, stop=True)
                        last.then_inc(s_xav, 1)
                    if n >= 3 and (n - 3) % NJ == NJ - 1:
                        g = (n - 3) // NJ
                        pe.wait_ge(s_xon, cnt(b, GPB, g + 1))
                        for c in range(2):
                            last = pe.transpose(
                                bank[1][:, P * c:P * c + P],
                                xon[:, XH // 2 * c:XH // 2 * (c + 1), :].rearrange("p h f -> p (h f)"), ident[:, :])
                        last.then_inc(s_xoT_p, 1)
                        pe.wait_ge(s_xoT, cnt(b, GPB, g + 1))
                        if g > 0:
                            pe.wait_ge(s_xadd, cnt(b, GPB, g))
                        for c in range(2):
                            last = pe.matmul(bank[2][:, 0:D], xoT[:, c, :], fcT[:, c, :], start=(c == 0), stop=(c == 1))
                        last.then_inc(s_fc, 1)
                pe.wait_ge(s_xadd, cnt(b, GPB, GPB))

        @block.scalar
        def _(act):
            for dst, src in consts[7:]:
                act.dma_start(dst, src).then_inc(s_w, 16)
            act.wait_ge(s_w, 16 * len(consts))
            act.mul(fmbn[:, :], fmb[:, :], -1.0).then_inc(s_nb, 1)
            act.wait_ge(s_prep, 1)
            act.copy(mqk[:, :], bank[0][:, 0:P])
            act.copy(wvT[:, :], bank[0][:, P:2 * P])
            act.copy(fcT[:, :, :].rearrange("p c o -> p (c o)"), bank[0][:, 2 * P:4 * P]).then_inc(s_prepped, 1)
            act.wait_ge(s_nb, 1)
            with act.Fori(0, BATCH) as b:
                act.wait_ge(s_xnT_p, cnt(b, 2, 1))
                act.copy(xnT[:, :], bank[0][:, :]).then_inc(s_xnT, 1)
                act.wait_ge(s_qp_p, cnt(b, 1, 1))
                act.copy(qp[:, :], bank[1][:, :]).then_inc(s_qp, 1)
                act.wait_ge(s_va_p, cnt(b, 1, 1))
                act.copy(va[:, :, :].rearrange("p j d -> p (j d)"), bank[2][:, :]).then_inc(s_va, 1)
                act.copy(cxs[:, :], cx[:, b, :]).then_inc(s_cxs, 1)
                for i in range(GPB):
                    w = P * (i + 1)
                    act.wait_ge(s_nm, cnt(b, GPB, i + 1))
                    if i >= 2:
                        act.wait_ge(s_paT_p, cnt(b, GPB, i - 1))
                    act.activation(pa[:, i % 2, 0:w], bank[3 + i][:, 0:w], ACT.Exp, bias=amax[:, i:i + 1],
                                   scale=ATT_SCALE, accum_out=asum[:, i:i + 1]).then_inc(s_pa, 1)
                    act.wait_ge(s_paT_p, cnt(b, GPB, i + 1))
                    if i >= 2:
                        act.wait_ge(s_pv, cnt(b, GPB, i - 1))
                    tb = bank[7] if i % 2 == 0 else bank[1]
                    act.copy(paT[:, i % 2, 0:w], tb[:, 0:w]).then_inc(s_paT, 1)
                act.wait_ge(s_cxT_p, cnt(b, 1, 1))
                act.copy(cxT[:, :], bank[2][:, 0:CTX]).then_inc(s_cxT, 1)
                act.wait_ge(s_zk, cnt(b, 1, 1))
                act.activation(ek[:, 0, :], bank[2][:, P:P + CTX], ACT.Exp, bias=fmb[:, 0:1])
                act.activation(ek[:, 1, :], bank[2][:, P:P + CTX], ACT.Exp, bias=fmbn[:, 0:1],
                               scale=-1.0).then_inc(s_ek, 1)
                act.wait_ge(s_zr, cnt(b, 1, 1))
                z3 = zrow[:, :].rearrange("p (h e) -> p h e", e=XE)
                act.activation(vx[:, :, 0:XE], z3, ACT.Exp)
                act.activation(vx[:, :, XE:XF], z3, ACT.Exp, scale=-1.0).then_inc(s_vx, 1)
                act.wait_ge(s_xnT_p, cnt(b, 2, 2))
                act.copy(xnT[:, :], bank[0][:, :]).then_inc(s_xnT, 1)
                act.wait_ge(s_zq, cnt(b, 1, 1))
                act.activation(eq[:, 0, :], bank[1][:, :], ACT.Exp, bias=fmb[:, 0:1])
                act.activation(eq[:, 1, :], bank[1][:, :], ACT.Exp, bias=fmbn[:, 0:1], scale=-1.0).then_inc(s_eq, 1)
                N = GPB * NJ
                for n in range(N + 3):
                    if n < N:
                        act.wait_ge(s_xd, cnt(b, N, n + 1))
                        if n >= 2:
                            act.wait_ge(s_xpT_p, cnt(b, N, n - 1))
                            act.wait_ge(s_xm, cnt(b, N, n - 1))
                        act.activation(xp[:, n % 2, :], xd[:, n % 2, :], ACT.Exp, scale=ATT_SCALE).then_inc(s_xp, 1)
                    if 1 <= n < N + 1:
                        m = n - 1
                        act.wait_ge(s_xpT_p, cnt(b, N, m + 1))
                        if m >= 2:
                            act.wait_ge(s_xav, cnt(b, N, m - 1))
                        act.copy(xpT[:, m % 2, :], bank[5 + m % 2][0:CTX, :]).then_inc(s_xpT, 1)
                    if n >= 3 and (n - 3) % NJ == NJ - 1:
                        g = (n - 3) // NJ
                        act.wait_ge(s_xoT_p, cnt(b, GPB, g + 1))
                        act.copy(xoT[:, :, :].rearrange("p c o -> p (c o)"), bank[1][:, 0:2 * P]).then_inc(s_xoT, 1)

        @block.vector
        def _(dve):
            links = [0]

            def link(ins, wait=True):
                links[0] += 1
                ins.then_inc(s_link, 1)
                if wait:
                    dve.wait_ge(s_link, links[0])

            dve.wait_ge(s_x, 16 * BATCH)
            dve.wait_ge(s_w, 16 * len(consts))
            with dve.Fori(0, BATCH) as b:
                links[0] = 0

                def tile(j):
                    return stream[:, b * GPB + j, :]

                def norm(dst, signal):
                    layer_norm_tiles(dve, link, tile, st, mv, lw[:, 0, :], lw[:, 1, :], lw[:, 2, :], dst, signal)

                norm(lambda j: xn[:, j, :], lambda ins: ins.then_inc(s_xn, 1))
                for i in range(GPB):
                    dve.wait_ge(s_sc, cnt(b, GPB, i + 1))
                    w = P * (i + 1)
                    diag = bank[3 + i][:, P * i:w]
                    link(dve.tensor_tensor(diag, diag, causal[:, :], ALU.add))
                    link(dve.tensor_reduce(amax[:, i:i + 1], bank[3 + i][:, 0:w], AX.X, ALU.max))
                    dve.tensor_scalar(amax[:, i:i + 1], amax[:, i:i + 1], -ATT_SCALE, None, ALU.mult).then_inc(s_nm, 1)
                for i in range(GPB):
                    dve.wait_ge(s_pa, cnt(b, GPB, i + 1))
                    link(dve.reciprocal(ainv[:, i:i + 1], asum[:, i:i + 1]))
                    dve.wait_ge(s_pv, cnt(b, GPB, i + 1))
                    dve.scalar_tensor_tensor(out=tile(i), in0=bank[2 * (i % 2)][:, 0:P], scalar=ainv[:, i:i + 1],
                                             in1=tile(i), op0=ALU.mult, op1=ALU.add).then_inc(s_att, 1)
                dve.wait_ge(s_att, cnt(b, GPB, GPB))
                dve.nop(nofuse=True)
                norm(lambda j: xn[:, j, :], lambda ins: ins.then_inc(s_xn, 1))
                dve.wait_ge(s_ek, cnt(b, 1, 1))
                for e in range(2):
                    last = dve.tensor_tensor(kx[:, e, :, :], bcast(ek[:, e, :], 1, XH), bcast(hmask[:, :], 2, CTX),
                                             ALU.mult)
                last.then_inc(s_kx, 1)
                dve.tensor_tensor(zrow[:, :], bank[2][0:CTX, 2 * P:3 * P], fmrow[:, :], ALU.add).then_inc(s_zr, 1)
                N = GPB * NJ
                for n in range(N + 4):
                    if n < N:
                        dve.wait_ge(s_xs, cnt(b, N, n + 1))
                        sc = bank[3 + n % 2][:, 0:CW].rearrange("p (h s) -> p h s", h=4)
                        link(dve.tensor_reduce(xmax[:, n % 2, :], sc, AX.X, ALU.max))
                        if n >= 2:
                            dve.wait_ge(s_xp, cnt(b, N, n - 1))
                        dve.tensor_tensor(xd[:, n % 2, :].rearrange("p (h s) -> p h s", h=4), sc,
                                          bcast(xmax[:, n % 2, :], 2, CTX), ALU.subtract).then_inc(s_xd, 1)
                    if 1 <= n < N + 1:
                        m = n - 1
                        g, c = m // NJ, m % NJ
                        dve.wait_ge(s_xp, cnt(b, N, m + 1))
                        dve.tensor_reduce(xsum[:, g % 2, 4 * c:4 * c + 4],
                                          xp[:, m % 2, :].rearrange("p (h s) -> p h s", h=4),
                                          AX.X, ALU.add).then_inc(s_xm, 1)
                    if n >= 2 and (n - 2) % NJ == NJ - 1 and n - 2 < N:
                        g = (n - 2) // NJ
                        dve.wait_ge(s_xm, cnt(b, N, NJ * (g + 1)))
                        link(dve.reciprocal(xinv[:, :], xsum[:, g % 2, :]))
                        dve.wait_ge(s_xav, cnt(b, N, NJ * (g + 1)))
                        if g > 0:
                            dve.wait_ge(s_xoT_p, cnt(b, GPB, g))
                        dve.tensor_tensor(xon[:, :, :], bank[7][:, 0:XH * XF].rearrange("p (h f) -> p h f", h=XH),
                                          bcast(xinv[:, :], 2, XF), ALU.mult).then_inc(s_xon, 1)
                    if n >= 4 and (n - 4) % NJ == NJ - 1:
                        g = (n - 4) // NJ
                        dve.wait_ge(s_fc, cnt(b, GPB, g + 1))
                        link(dve.tensor_tensor(tile(g), bank[2][:, 0:D], tile(g), ALU.add))
                        dve.tensor_tensor(tile(g), tile(g), fcb[:, :], ALU.add).then_inc(s_xadd, 1)
                dve.wait_ge(s_xadd, cnt(b, GPB, GPB))
                link(dve.tensor_copy(skip[:, bass.ds(b * GPB, GPB), :], stream[:, bass.ds(b * GPB, GPB), :]))
                norm(tile, lambda ins: ins.then_inc(s_xn, 1))
                dve.wait_ge(s_xn, cnt(b, 3, 3))
                dve.sem_inc(s_link, -links[0])


def stack(nc, part, a, k, out):
    bank, stream, skip, ident, mask, rot = (k[n] for n in ("bank", "stream", "skip", "ident", "mask", "rot"))

    def sb(name, shape, dt=F32):
        return part.enter_context(nc.sbuf_tensor(name, shape, dt))

    def sem(name):
        return part.enter_context(nc.semaphore(name))

    xT = sb("xT", [P, 2, SEQ + 1], F32R)
    xs = sb("xs", [P, 2, D])
    xs_part = sb("xs_part", [P, 2, 2, D], F32R)
    w_hi = sb("w_hi", [P, 3 * INNER], F32R)
    w_lo = sb("w_lo", [P, 3 * INNER], F32R)
    wo = sb("wo", [P, PAIRS, D])
    w1 = sb("w1", [P, 2 * FF])
    w2 = sb("w2", [P, 3, D])
    lng = sb("lng", [P, 1])
    lnb = sb("lnb", [P, 1])
    b1c = sb("b1c", [P, 6])
    sq = sb("sq", [P, 2, 512])
    qk_c = sb("qk_c", [P, 2, 2, INNER])
    qk_s = sb("qk_s", [P, 2, INNER])
    ssq = sb("ssq", [P, 2, 2 * HEADS])
    nrm = sb("nrm", [P, 2, 2 * HEADS])
    ntmp = sb("ntmp", [P, 2 * HEADS])
    qT = sb("qT", [P, PAIRS, P])
    kT = sb("kT", [P, PAIRS, WIN + SEQ])
    v_own = sb("v_own", [P, GPB, INNER])
    v_back = sb("v_back", [P, GPB, INNER])
    smax = sb("smax", [P, 2, PAIRS])
    sdif = sb("sdif", [P, 2, 512])
    prob = sb("prob", [P, 2, 2 * 512])
    psm = sb("psm", [P, 2, 8])
    pinv = sb("pinv", [P, 2, 8])
    pT = sb("pT", [P, PAIRS, P])
    att = sb("att", [P, INNER])
    attT = sb("attT", [P, PAIRS, P])
    f_x = sb("f_x", [P, GPB, D])
    f_xT = sb("f_xT", [P, SEQ + 1])
    f_n = sb("f_n", [P, GPB, D])
    f_nT = sb("f_nT", [P, SEQ])
    f_v = sb("f_v", [P, 2, SEQ])
    f_h = sb("f_h", [P, 3, SEQ])
    st = sb("st", [P, GPB, 6])
    mv = sb("mv", [P, GPB, 2])
    lw = sb("lw", [P, 3, GPB])

    names = dict(
        zeroed="edges_zeroed", wq_in="wq_in", wk_in="wk_in", wv_in="wv_in", wo_in="wo_in", wf_in="ffn_weights_in",
        xs_r="xs_ready", xt_p="xT_made", xt_r="xT_ready", xlo="x_low_ready", proj="proj_made", ab="cos_sin_ready", sqr="squares_ready",
        red="square_sums_ready", nr="norms_ready", rotd="rotated", qkn="qk_normed", v_r="values_ready",
        qkT_p="qkT_made", qkT_r="qkT_ready", sc="scores_made", sub="scores_read", dif="scores_less_max", ex="exp_ready", ps="prob_sums_ready",
        pn="prob_normed", pT_p="probT_made", pT_r="probT_ready", av="av_made", av_r="att_ready", aT_p="attT_made",
        aT_r="attT_ready", wo_p="attn_out_made", added="attn_added", fx="ffn_x_ready",
        f_p="ffn_made", f1="ffn_shifted_ready", f2="ffn_shiftedT_ready", f3="ffn_normed", f4="ffn_normedT_ready",
        fg="ffn_gate_ready", fv="ffn_value_ready", fh="ffn_hidden_ready", fadd="ffn_added", link="dve_chain",
        sum_r="out_summed", stored="out_stored")
    s = {key: sem(name) for key, name in names.items()}

    class Step:

        def __init__(self, it, j):
            self.it, self.j = it, j

        def on(self, off):
            return not isinstance(self.it, int) or 0 <= GPB * self.it + self.j + off < GPB * NIT

        def count(self, per, off, c):
            return self.it * (per * GPB) + (per * (self.j + off) + c)

        def idx(self, off):
            return (self.j + off) % GPB

        def slot(self, off):
            return (self.it * GPB + (self.j + off)) % (BATCH * GPB)

        def par(self, off):
            return (self.j + off) % 2

    def round_on(it, back):
        return not isinstance(it, int) or 0 <= it - back < NIT

    def weights_due(it, back, dmas):
        return ((it - back) // BATCH + 1) * (16 * dmas)

    shifted = [sem(f"values_shifted_{j}") for j in range(GPB)]

    def need_shifted(eng, q, off):
        row, j = (q.j + off) // GPB, (q.j + off) % GPB
        need(eng, shifted[j], (q.it + (row + 1)) * (16 if j == 0 else 32))

    w_d = {n: a["L0_ffn_" + n] for n in ("Wo", "ln_g", "ln_b", "W1", "b1", "W2", "b2")}
    NPROJ = 6
    FIRST_LOOP = 3

    def rounds(eng, body):
        for it in range(FIRST_LOOP):
            body(it)
        with eng.Fori(FIRST_LOOP, NIT) as it:
            body(it)
        for it in (NIT, NIT + 1):
            body(it)

    with nc.Block() as block:
        @block.sync
        def _(sp):
            def load(layer, part_no):
                cols = slice(INNER * part_no, INNER * (part_no + 1))
                for dst, src in ((w_hi, k["w_hi"]), (w_lo, k["w_lo"])):
                    sp.dma_start(dst[:, cols].bitcast(F32), src[layer, :, cols]).then_inc(s[("wq_in", "wk_in", "wv_in")[part_no]], 16)

            def load_wo(layer):
                sp.dma_start(wo[:, :, :], w_d["Wo"][layer, :, :].rearrange("(c p) d -> p c d", p=P)).then_inc(s["wo_in"], 16)

            def load_ffn(layer):
                sp.dma_start(w1[:, :], w_d["W1"][layer, :, :]).then_inc(s["wf_in"], 16)
                w2_d = w_d["W2"][layer, :, :]
                sp.dma_start(w2[:, 0:2, :], w2_d[0:2 * P, :].rearrange("(c p) d -> p c d", p=P)).then_inc(s["wf_in"], 16)
                lo, m = FCH[2]
                sp.dma_start(w2[0:m, 2, :], w2_d[lo:lo + m, :]).then_inc(s["wf_in"], 16)
                col = lambda v, n: v.rearrange("(p o) -> p o", o=1)
                sp.dma_start(lng[:, :], col(w_d["ln_g"][layer, :], 1)).then_inc(s["wf_in"], 16)
                sp.dma_start(lnb[:, :], col(w_d["ln_b"][layer, :], 1)).then_inc(s["wf_in"], 16)
                b1 = w_d["b1"][layer, :]
                for n in range(2):
                    sp.dma_start(b1c[:, 3 * n:3 * n + 2],
                                 b1[FF * n:FF * n + 2 * P].rearrange("(c p) -> p c", p=P)).then_inc(s["wf_in"], 16)
                    sp.dma_start(b1c[0:m, 3 * n + 2:3 * n + 3], col(b1[FF * n + lo:FF * n + lo + m], 1)).then_inc(s["wf_in"], 16)
                sp.dma_start(w2[m:m + 1, 2, :], w_d["b2"][layer:layer + 1, :]).then_inc(s["wf_in"], 16)

            with nc.allow_non_contiguous_dma(reason="bias columns"):
                for n in range(3):
                    load(0, n)
                load_wo(0)
                load_ffn(0)
                def shift_values(it, j):
                    q = Step(it, j)
                    sp.wait_ge(s["v_r"], q.count(2, 0, 2))
                    if j > 0:
                        sp.dma_start(v_back[0:WIN, j, :], v_own[P - WIN:P, j - 1, :]).then_inc(shifted[j], 16)
                    sp.dma_start(v_back[WIN:P, j, :], v_own[0:P - WIN, j, :]).then_inc(shifted[j], 16)

                def layer_rows(layer):
                    g = BATCH * GPB * layer
                    for row in range(BATCH):
                        for j in range(GPB):
                            if layer > 0 and row == 1 and j == 0:
                                sp.wait_ge(s["wo_p"], g)
                                load_wo(layer)
                            shift_values(BATCH * layer + row, j)
                            if layer > 0 and row == 2 and j == 0:
                                sp.wait_ge(s["fadd"], BATCH * layer)
                                load_ffn(layer)

                layer_rows(0)
                for layer in range(1, DEPTH):
                    for n in range(3):
                        sp.wait_ge(s["proj"], NPROJ * (BATCH * GPB * layer - 1) + 2 * n + 2)
                        load(layer, n)
                    layer_rows(layer)
            sp.wait_ge(s["sum_r"], 1)
            sp.dma_start(out.rearrange("b (j p) d -> p (b j) d", p=P), skip[:, :, :]).then_inc(s["stored"], 16)
            sp.wait_ge(s["stored"], 16)

        @block.tensor
        def _(pe):
            front_job = [None]

            def shared_bank(reader, value):
                if front_job[0] is not None:
                    pe.wait_ge(*front_job[0])
                front_job[0] = (s[reader], value)

            def transpose_x(q):
                if not q.on(1):
                    return
                shared_bank("xt_r", q.count(1, 1, 1))
                pe.wait_ge(s["xlo"], q.count(1, 1, 1))
                for n in range(2):
                    last = pe.transpose(bank[7][:, P * n:P * n + P], xs_part[:, q.par(1), n, :].bitcast(F32), ident[:, :])
                last.then_inc(s["xt_p"], 1)

            def ffn_job(q, n):
                if not round_on(q.it, 2):
                    return
                row = q.it - 2
                if n < 2:
                    shared_bank(("f1", "f2")[n], row + 1)
                elif n == 2:
                    shared_bank("f4", row + 1)
                elif n < 9:
                    shared_bank(("fg", "fv")[(n - 3) % 2], row * 3 + ((n - 3) // 2 + 1))
                else:
                    shared_bank("fadd", row + 1)
                b7 = bank[7]
                if n == 0:
                    pe.wait_ge(s["fx"], row + 1)
                    for c in range(GPB):
                        last = pe.transpose(b7[:, P * c:P * c + P], f_x[:, c, :], ident[:, :])
                elif n == 1:
                    pe.wait_ge(s["f1"], row + 1)
                    for c in range(GPB):
                        last = pe.transpose(b7[:, P * c:P * c + P], f_xT[:, P * c:P * c + P], ident[:, :])
                elif n == 2:
                    pe.wait_ge(s["wf_in"], weights_due(q.it, 2, DMAS_FFN))
                    pe.wait_ge(s["f3"], row + 1)
                    for c in range(GPB):
                        last = pe.transpose(b7[:, P * c:P * c + P], f_n[:, c, :], ident[:, :])
                elif n < 9:
                    c, value = (n - 3) // 2, (n - 3) % 2
                    lo, m = FCH[c]
                    if n == 3:
                        pe.wait_ge(s["f4"], row + 1)
                    col = lo if value else FF + lo
                    last = pe.matmul(b7[0:m, :], w1[:, col:col + m], f_nT[:, :], start=True, stop=True)
                else:
                    pe.wait_ge(s["fh"], row * 3 + 3)
                    for t in range(GPB):
                        for c, (lo, m) in enumerate(FCH):
                            m += c == 2
                            last = pe.matmul(b7[:, P * t:P * t + P], f_h[0:m, c, P * t:P * t + P], w2[0:m, c, :],
                                             start=(c == 0), stop=(c == 2))
                last.then_inc(s["f_p"], 1)

            def ffn_place(q, place):
                if (q.j, place) in FFN_PLACES:
                    ffn_job(q, FFN_PLACES[q.j, place])

            def transpose_qk(q, kind):
                for half in range(2):
                    if half == 0:
                        pe.wait_ge(s["qkn"], q.count(2, -2, kind + 1))
                    if kind == 0:
                        need(pe, s["pT_r"], q.count(2, -4, half + 1))
                    else:
                        pe.wait_ge(s["qkT_r"], q.count(4, -2, half + 1))
                    for c in range(4):
                        pair = 4 * half + c
                        last = pe.transpose(bank[2 + half][:, P * c:P * c + P],
                                            qk_c[:, q.par(-2), kind, P * pair:P * pair + P], ident[:, :])
                    last.then_inc(s["qkT_p"], 1)

            def scores(q, half):
                b = bank[4 + half]
                if half == 0:
                    need(pe, s["av_r"], q.count(2, -4, 2))
                else:
                    need(pe, s["sub"], q.count(2, -3, 2))
                pe.wait_ge(s["qkT_r"], q.count(4, -2, 3 + half))
                j = q.idx(-2)
                pe.nop(nofuse=True)
                for c in range(4):
                    pair = 4 * half + c
                    for w in range(4):
                        for hp in range(2):
                            half_w, wpar = w // 2, w % 2
                            r = slice(64 * hp, 64 * hp + 64)
                            o = 64 * hp + 32 * wpar
                            last = pe.matmul(
                                b[o:o + 32, P * c + 64 * half_w:P * c + 64 * half_w + 64],
                                qT[r, pair, WIN * w:WIN * w + WIN],
                                kT[r, pair, P * j + WIN * w:P * j + WIN * w + 64],
                                start=True, stop=True)
                last.then_inc(s["sc"], 1)

            def transpose_prob(q, half):
                pe.wait_ge(s["pn"], q.count(2, -3, half + 1))
                if q.on(-4):
                    pe.wait_ge(s["aT_r"], q.count(2, -4, half + 1))
                else:
                    need(pe, s["qkT_r"], q.count(4, -2, 3 + half))
                for c in range(4):
                    last = pe.transpose(bank[2 + half][:, P * c:P * c + P],
                                        prob[:, q.par(-3), 512 * half + P * c:512 * half + P * c + P], ident[:, :])
                last.then_inc(s["pT_p"], 1)

            def attend(q, half):
                if half == 0:
                    b = bank[6]
                    need(pe, s["av_r"], q.count(2, -4, 1))
                else:
                    b = bank[4]
                    if q.on(-2):
                        pe.wait_ge(s["sub"], q.count(2, -2, 1))
                    else:
                        pe.wait_ge(s["av_r"], q.count(2, -4, 2))
                pe.wait_ge(s["pT_r"], q.count(2, -3, half + 1))
                pe.wait_ge(s["v_r"], q.count(2, -3, half + 1))
                need_shifted(pe, q, -3)
                pe.nop(nofuse=True)
                j = q.idx(-3)
                for c in range(4):
                    pair = 4 * half + c
                    for w in range(4):
                        for hp in range(2):
                            half_w, wpar = w // 2, w % 2
                            r = slice(64 * half_w, 64 * half_w + 64)
                            v = (v_own if wpar else v_back)[r, j, DH * (2 * pair + hp):DH * (2 * pair + hp + 1)]
                            last = pe.matmul(b[WIN * w:WIN * w + WIN, DH * (2 * c + hp):DH * (2 * c + hp + 1)],
                                             pT[r, pair, 64 * hp + 32 * wpar:64 * hp + 32 * wpar + 32], v,
                                             start=True, stop=True)
                last.then_inc(s["av"], 1)

            def transpose_att(q, half):
                pe.wait_ge(s["av_r"], q.count(2, -4, half + 1))
                if q.on(-2):
                    pe.wait_ge(s["qkT_r"], q.count(4, -2, 3 + half))
                else:
                    need(pe, s["pT_r"], q.count(2, -4, half + 1))
                for c in range(4):
                    last = pe.transpose(bank[2 + half][:, P * c:P * c + P],
                                        att[:, 512 * half + P * c:512 * half + P * c + P], ident[:, :])
                last.then_inc(s["aT_p"], 1)

            def out_proj(q):
                shared_bank("added", q.count(1, -4, 1))
                pe.wait_ge(s["aT_r"], q.count(2, -4, 2))
                if q.j == 0:
                    pe.wait_ge(s["wo_in"], weights_due(q.it, 1, 1))
                for c in range(PAIRS):
                    last = pe.matmul(bank[7][:, 0:D], attT[:, c, :], wo[:, c, :], start=(c == 0), stop=(c == PAIRS - 1))
                last.then_inc(s["wo_p"], 1)

            def project(q, n):
                part_no = n // 2
                if q.j == 0 and n % 2 == 0:
                    pe.wait_ge(s[("wq_in", "wk_in", "wv_in")[part_no]], weights_due(q.it, 0, 2))
                if n < 2:
                    if n == 0:
                        pe.wait_ge(s["xt_r"], q.count(1, 0, 1))
                    need(pe, s["v_r"], q.count(2, -1, 1 + n))
                else:
                    pe.wait_ge(s["ab"], q.count(4, 0, n - 1))
                lo = P * q.j
                col = INNER * part_no + 512 * (n % 2)
                pe.matmul(bank[n % 2][:, :], xT[:, 1, lo:lo + P], w_hi[:, col:col + 512], start=True, stop=False)
                pe.matmul(bank[n % 2][:, :], xT[:, 0, lo:lo + P], w_lo[:, col:col + 512], start=False, stop=False)
                pe.matmul(bank[n % 2][:, :], xT[:, 0, lo:lo + P], w_hi[:, col:col + 512],
                          start=False, stop=True).then_inc(s["proj"], 1)

            def body(it):
                first = Step(it, 0)
                if round_on(it, 3):
                    front_job[0] = (s["fadd"], it - 2)
                elif isinstance(it, int) and it > NIT:
                    front_job[0] = (s["added"], first.count(1, -5, 1))
                else:
                    front_job[0] = (s["xt_r"], first.count(1, 0, 1))
                for j in range(GPB):
                    q = Step(it, j)
                    if q.on(-2):
                        transpose_qk(q, 0)
                    ffn_place(q, 0)
                    if q.on(0):
                        project(q, 0)
                        project(q, 1)
                    ffn_place(q, 1)
                    if q.on(-2):
                        transpose_qk(q, 1)
                    ffn_place(q, 2)
                    if q.on(-2):
                        scores(q, 0)
                    if q.on(0):
                        project(q, 2)
                    if q.on(-2):
                        scores(q, 1)
                    if q.on(0):
                        project(q, 3)
                    ffn_place(q, 3)
                    if q.on(-4):
                        transpose_att(q, 0)
                        transpose_att(q, 1)
                    transpose_x(q)
                    if q.on(0):
                        project(q, 4)
                    if q.on(-3):
                        transpose_prob(q, 0)
                        transpose_prob(q, 1)
                    if q.on(0):
                        project(q, 5)
                    if q.on(-4):
                        out_proj(q)
                    if q.on(-3):
                        attend(q, 0)
                    ffn_place(q, 4)
                    if q.on(-3):
                        attend(q, 1)
                    ffn_place(q, 5)

            pe.wait_ge(s["zeroed"], 5)
            transpose_x(Step(0, -1))
            rounds(pe, body)

        @block.scalar
        def _(act):
            def copy_x(q):
                if not q.on(2):
                    return
                need(act, s["xt_p"], q.count(1, 0, 1))
                act.copy(xs[:, q.par(2), :], stream[:, q.slot(2), :])
                act.copy(xs_part[:, q.par(2), 0, :], stream[:, q.slot(2), :]).then_inc(s["xs_r"], 1)

            def shift_x(q):
                if not q.on(1):
                    return
                act.wait_ge(s["xt_p"], q.count(1, 1, 1))
                need(act, s["proj"], q.count(NPROJ, -2, NPROJ))
                lo = P * q.idx(1)
                src = bank[7][:, 0:2 * P].rearrange("p (n t) -> p n t", n=2)
                act.copy(xT[0:64, :, lo:lo + P], src[0:64])
                act.copy(xT[64:P, :, lo + 1:lo + 1 + P], src[64:P]).then_inc(s["xt_r"], 1)

            def store_qkT(q, n):
                kind, half = n // 2, n % 2
                act.wait_ge(s["qkT_p"], q.count(4, -2, n + 1))
                need(act, s["sc"], q.count(2, -3, 2))
                src = bank[2 + half][:, :].rearrange("p (c t) -> p c t", c=4)
                if kind == 0:
                    dst = qT[:, 4 * half:4 * half + 4, :]
                else:
                    lo = WIN + P * q.idx(-2)
                    dst = kT[:, 4 * half:4 * half + 4, lo:lo + P]
                act.copy(dst, src).then_inc(s["qkT_r"], 1)

            def store_attT(q, half):
                act.wait_ge(s["aT_p"], q.count(2, -4, half + 1))
                need(act, s["wo_p"], q.count(1, -5, 1))
                act.copy(attT[:, 4 * half:4 * half + 4, :].rearrange("p c t -> p (c t)"),
                         bank[2 + half][:, :]).then_inc(s["aT_r"], 1)

            def store_probT(q, half):
                act.wait_ge(s["pT_p"], q.count(2, -3, half + 1))
                need(act, s["av"], q.count(2, -4, 2))
                act.copy(pT[:, 4 * half:4 * half + 4, :].rearrange("p c t -> p (c t)"),
                         bank[2 + half][:, :]).then_inc(s["pT_r"], 1)

            def exponentials(q, half):
                act.wait_ge(s["dif"], q.count(2, -2, half + 1))
                need(act, s["pT_p"], q.count(2, -4, half + 1))
                act.activation(prob[:, q.par(-2), 512 * half:512 * half + 512], sdif[:, half, :],
                               ACT.Exp).then_inc(s["ex"], 1)

            def store_att(q, half):
                act.wait_ge(s["av"], q.count(2, -3, half + 1))
                need(act, s["aT_p"], q.count(2, -4, half + 1))
                act.copy(att[:, 512 * half:512 * half + 512], bank[6 if half == 0 else 4][:, :]).then_inc(s["av_r"], 1)

            def squares(q, n):
                act.wait_ge(s["proj"], q.count(NPROJ, 0, n + 1))
                need(act, s["red"], q.count(4, 0, n - 1))
                act.activation(sq[:, n % 2, :], bank[n % 2][:, :], ACT.Square).then_inc(s["sqr"], 1)

            def store_values(q, n):
                act.wait_ge(s["proj"], q.count(NPROJ, 0, 5 + n))
                need(act, s["av"], q.count(2, -4, 2))
                need_shifted(act, q, -3)
                act.copy(v_own[:, q.idx(0), 512 * n:512 * n + 512], bank[n % 2][:, :]).then_inc(s["v_r"], 1)

            def ffn_job(q, n):
                if not round_on(q.it, 2):
                    return
                row = q.it - 2
                if n < 9:
                    act.wait_ge(s["f_p"], row * FJOBS + (n + 1))
                if n == 0:
                    act.copy(f_xT[0:64, 0:SEQ], bank[7][0:64, :])
                    act.copy(f_xT[64:P, 1:SEQ + 1], bank[7][64:P, :]).then_inc(s["f1"], 1)
                elif n == 1:
                    act.copy(f_x[:, :, :].rearrange("p j d -> p (j d)"), bank[7][:, :]).then_inc(s["f2"], 1)
                elif n == 2:
                    act.activation(f_nT[:, :], bank[7][:, :], ACT.Identity, bias=lnb[:, 0:1],
                                   scale=lng[:, 0:1]).then_inc(s["f4"], 1)
                elif n in (3, 5, 7):
                    c = (n - 3) // 2
                    m = FCH[c][1]
                    act.activation(f_h[0:m, c, :], bank[7][0:m, :], ACT.Gelu,
                                   bias=b1c[0:m, 3 + c:4 + c]).then_inc(s["fg"], 1)
                elif n < 9:
                    c = (n - 4) // 2
                    m = FCH[c][1]
                    if c == 2:
                        act.wait_ge(s["fh"], row * 3 + 1)
                    act.activation(f_v[0:m, c % 2, :], bank[7][0:m, :], ACT.Identity,
                                   bias=b1c[0:m, c:c + 1]).then_inc(s["fv"], 1)

            def ffn_place(q, place):
                if (q.j, place) in FFN_PLACES:
                    ffn_job(q, FFN_PLACES[q.j, place])

            def copy_row(it):
                if not round_on(it, 2):
                    return
                act.wait_ge(s["added"], (it - 1) * GPB)
                act.copy(f_x[:, :, :], stream[:, bass.ds(((it - 2) % BATCH) * GPB, GPB), :]).then_inc(s["fx"], 1)

            def body(it):
                copy_row(it)
                for j in range(GPB):
                    q = Step(it, j)
                    if q.on(-2):
                        store_qkT(q, 0)
                        store_qkT(q, 1)
                    ffn_place(q, 0)
                    if q.on(0):
                        squares(q, 0)
                        squares(q, 1)
                    ffn_place(q, 1)
                    if q.on(-2):
                        store_qkT(q, 2)
                        store_qkT(q, 3)
                    ffn_place(q, 2)
                    if q.on(0):
                        squares(q, 2)
                        squares(q, 3)
                    ffn_place(q, 3)
                    if q.on(-4):
                        store_attT(q, 0)
                        store_attT(q, 1)
                    shift_x(q)
                    if q.on(0):
                        store_values(q, 0)
                    if q.on(-3):
                        store_probT(q, 0)
                        store_probT(q, 1)
                    if q.on(-2):
                        exponentials(q, 0)
                    if q.on(0):
                        store_values(q, 1)
                    if q.on(-2):
                        exponentials(q, 1)
                    if q.on(-3):
                        store_att(q, 0)
                    ffn_place(q, 4)
                    if q.on(-3):
                        store_att(q, 1)
                    ffn_place(q, 5)
                    copy_x(q)

            act.wait_ge(s["zeroed"], 5)
            copy_x(Step(0, -2))
            copy_x(Step(0, -1))
            shift_x(Step(0, -1))
            rounds(act, body)

        @block.gpsimd
        def _(pool):
            def normalise(q, kind):
                pool.wait_ge(s["nr"], q.count(1, -1, 1))
                pool.wait_ge(s["rotd"], q.count(2, -1, kind + 1))
                x = qk_c[:, q.par(-1), kind, :].rearrange("p (h d) -> p h d", d=DH)
                pool.tensor_tensor(x, x, bcast(nrm[:, q.par(-1), HEADS * kind:HEADS * (kind + 1)], 2, DH),
                                   ALU.mult).then_inc(s["qkn"], 1)

            def low_x(q):
                if not q.on(1):
                    return
                pool.wait_ge(s["xs_r"], q.count(1, 1, 1))
                pool.tensor_tensor(xs_part[:, q.par(1), 1, :], xs[:, q.par(1), :],
                                   xs_part[:, q.par(1), 0, :].bitcast(F32), ALU.subtract).then_inc(s["xlo"], 1)

            def ffn_product(q, c):
                if not round_on(q.it, 2):
                    return
                m = FCH[c][1]
                pool.wait_ge(s["fv"], (q.it - 2) * 3 + (c + 1))
                pool.tensor_tensor(f_h[0:m, c, :], f_h[0:m, c, :], f_v[0:m, c % 2, :], ALU.mult).then_inc(s["fh"], 1)

            def normalise_prob(q, half):
                pool.wait_ge(s["ps"], q.count(2, -2, half + 1))
                x = prob[:, q.par(-2), 512 * half:512 * half + 512].rearrange("p (c s) -> p c s", s=64)
                pool.tensor_tensor(x, x, bcast(pinv[:, half, :], 2, 64), ALU.mult).then_inc(s["pn"], 1)

            def rotate(q, kind):
                pool.wait_ge(s["ab"], q.count(4, 0, 2 * kind + 2))
                x = qk_c[:, q.par(0), kind, :]
                pool.tensor_tensor(x, x, qk_s[:, kind, :], ALU.add).then_inc(s["rotd"], 1)

            def body(it):
                for j in range(GPB):
                    q = Step(it, j)
                    low_x(q)
                    if q.on(-1):
                        normalise(q, 0)
                    if j == 3:
                        ffn_product(q, 0)
                    if q.on(-1):
                        normalise(q, 1)
                    if j == 3:
                        ffn_product(q, 1)
                        ffn_product(q, 2)
                    if q.on(0):
                        rotate(q, 0)
                        rotate(q, 1)
                    if q.on(-2):
                        normalise_prob(q, 0)
                        normalise_prob(q, 1)

            pool.memset(xT[:, :, 0:1].bitcast(F32), 0.0).then_inc(s["zeroed"], 1)
            pool.memset(kT[:, :, 0:WIN], 0.0).then_inc(s["zeroed"], 1)
            pool.memset(f_xT[:, 0:1], 0.0).then_inc(s["zeroed"], 1)
            pool.memset(v_back[0:WIN, 0, :], 0.0).then_inc(s["zeroed"], 1)
            pool.memset(f_h[:, 2, :], 1.0).then_inc(s["zeroed"], 1)
            low_x(Step(0, -1))
            rounds(pool, body)

        @block.vector
        def _(dve):
            links = [0]

            def link(ins):
                links[0] += 1
                ins.then_inc(s["link"], 1)
                return links[0]

            def linked(n):
                dve.wait_ge(s["link"], n)

            norm_link = [0]

            def norm_step(q, n):
                if not q.on(-1):
                    return
                w, y = ssq[:, q.par(-1), :], nrm[:, q.par(-1), :]
                if n == 0:
                    dve.wait_ge(s["red"], q.count(4, -1, 4))
                    norm_link[0] = link(dve.tensor_scalar(w, w, 1e-24, None, ALU.max))
                    return
                linked(norm_link[0])
                if n == 1:
                    need(dve, s["qkn"], q.count(2, -3, 2))
                    norm_link[0] = link(rsqrt_guess(dve, y, w))
                    return
                ins = rsqrt_step(dve, (n - 2) % 3, y, w, ntmp[:, :])
                if n == 10:
                    ins.then_inc(s["nr"], 1)
                else:
                    norm_link[0] = link(ins)

            def score_mask(q, half):
                dve.wait_ge(s["sc"], q.count(2, -2, half + 1))
                need(dve, s["ex"], q.count(2, -3, half + 1))
                ins = dve.tensor_tensor(sdif[:, half, :].rearrange("p (c s) -> p c s", s=P),
                                        bank[4 + half][:, :].rearrange("p (c s) -> p c s", s=P),
                                        bcast(mask[:, 1 if q.idx(-2) == 0 else 0, :], 1, 4), ALU.add)
                ins.then_inc(s["sub"], 1)

            def score_max(q, half):
                dve.wait_ge(s["sub"], q.count(2, -2, half + 1))
                return link(dve.tensor_reduce(smax[:, half, :], sdif[:, half, :].rearrange("p (c s) -> p c s", s=64),
                                              AX.X, ALU.max))

            def score_sub(q, half, after):
                linked(after)
                x = sdif[:, half, :].rearrange("p (c s) -> p c s", s=64)
                dve.tensor_tensor(x, x, bcast(smax[:, half, :], 2, 64), ALU.subtract).then_inc(s["dif"], 1)

            def prob_sum(q, half):
                dve.wait_ge(s["ex"], q.count(2, -2, half + 1))
                x = prob[:, q.par(-2), 512 * half:512 * half + 512].rearrange("p (c s) -> p c s", s=64)
                return link(dve.tensor_reduce(psm[:, half, :], x, AX.X, ALU.add))

            def prob_inv(q, half, after):
                linked(after)
                need(dve, s["pn"], q.count(2, -3, half + 1))
                dve.reciprocal(pinv[:, half, :], psm[:, half, :]).then_inc(s["ps"], 1)

            def add_attention(q):
                dve.wait_ge(s["wo_p"], q.count(1, -4, 1))
                x = stream[:, q.slot(-4), :]
                dve.tensor_tensor(x, bank[7][:, 0:D], x, ALU.add).then_inc(s["added"], 1)

            def cos_part(q, n):
                kind, half = n // 2, n % 2
                dve.wait_ge(s["sqr"], q.count(4, 0, n + 1))
                need(dve, s["qkT_p"], q.count(4, -2, 2 * kind + 2))
                dve.tensor_tensor(
                    qk_c[:, q.par(0), kind, 512 * half:512 * half + 512].rearrange("p (h d) -> p h d", d=DH),
                    bank[n % 2][:, :].rearrange("p (h d) -> p h d", d=DH),
                    bcast(table(q, 2 * kind), 1, 8), ALU.mult)

            def sin_part(q, n):
                kind, half = n // 2, n % 2
                if half == 0:
                    need(dve, s["rotd"], q.count(2, -1, kind + 1))
                b = bank[n % 2][:, :].rearrange("p (h r d) -> p h r d", r=2, d=DH // 2)
                dst = qk_s[:, kind, 512 * half:512 * half + 512].rearrange("p (h r d) -> p h r d", r=2, d=DH // 2)
                dve.tensor_tensor(dst[:, :, ::-1, :], b,
                                  bcast(table(q, 2 * kind + 1).rearrange("p (r d) -> p r d", r=2), 1, 8),
                                  ALU.mult).then_inc(s["ab"], 1)

            def table(q, kind):
                layer = q.it // BATCH
                lo = (layer * 4 + kind) * (GPB * DH) + q.j * DH
                flat = rot[:, :, :, :].rearrange("p l k n -> p (l k n)")
                return flat[:, lo:lo + DH] if isinstance(lo, int) else flat[:, bass.ds(lo, DH)]

            def square_sum(q, n):
                dve.wait_ge(s["sqr"], q.count(4, 0, n + 1))
                dve.tensor_reduce(ssq[:, q.par(0), 8 * n:8 * n + 8],
                                  sq[:, n % 2, :].rearrange("p (h d) -> p h d", d=DH),
                                  AX.X, ALU.add).then_inc(s["red"], 1)

            def ffn_norm(q):
                if not (q.j == 1 and round_on(q.it, 2)):
                    return
                w, y, t = lw[:, 0, :], lw[:, 1, :], lw[:, 2, :]
                dve.wait_ge(s["f2"], q.it - 1)
                for j in range(GPB):
                    n = link(dve.bn_stats(st[:, j, :], f_x[:, j, :]))
                yield
                linked(n)
                for j in range(GPB):
                    n = link(dve.bn_aggr(mv[:, j, :], st[:, j, :]))
                yield
                linked(n)
                n = link(dve.tensor_scalar(w, mv[:, :, 1], LN_EPS, None, ALU.add))
                yield
                linked(n)
                n = link(rsqrt_guess(dve, y, w))
                yield
                for i in range(9):
                    linked(n)
                    n = link(rsqrt_step(dve, i % 3, y, w, t))
                    yield
                linked(n)
                for j in range(GPB):
                    last = dve.tensor_scalar(f_n[:, j, :], f_x[:, j, :], mv[:, j, 0:1], y[:, j:j + 1],
                                             ALU.subtract, ALU.mult)
                last.then_inc(s["f3"], 1)
                yield

            def ffn_job(q, n):
                if not round_on(q.it, 2):
                    return
                row = q.it - 2
                if n == 9:
                    dve.wait_ge(s["f_p"], row * FJOBS + (n + 1))
                    x = stream[:, bass.ds((row % BATCH) * GPB, GPB), :]
                    dve.tensor_tensor(x, bank[7][:, :].rearrange("p (j d) -> p j d", d=D), x, ALU.add).then_inc(s["fadd"], 1)

            def ffn_place(q, place):
                if (q.j, place) in FFN_PLACES:
                    ffn_job(q, FFN_PLACES[q.j, place])

            def body(it):
                links[0] = 0
                for j in range(GPB):
                    q = Step(it, j)
                    norm_step(q, 0)
                    norm_step(q, 1)
                    ffn_place(q, 0)
                    for n in range(2):
                        if q.on(0):
                            cos_part(q, n)
                        norm_step(q, 2 + 3 * n)
                        if q.on(0):
                            sin_part(q, n)
                        norm_step(q, 3 + 3 * n)
                        if q.on(0):
                            square_sum(q, n)
                        norm_step(q, 4 + 3 * n)
                    ffn_place(q, 1)
                    for n in range(8, 11):
                        norm_step(q, n)
                    ffn_place(q, 2)
                    norm = ffn_norm(q)
                    if q.on(0):
                        for n in range(2, 4):
                            cos_part(q, n)
                            next(norm, None)
                            sin_part(q, n)
                            next(norm, None)
                            square_sum(q, n)
                            next(norm, None)
                    if q.on(-2):
                        score_mask(q, 0)
                        next(norm, None)
                        score_mask(q, 1)
                        next(norm, None)
                        m0 = score_max(q, 0)
                        next(norm, None)
                        m1 = score_max(q, 1)
                        next(norm, None)
                    if q.on(-4):
                        add_attention(q)
                    if q.on(-2):
                        score_sub(q, 0, m0)
                        next(norm, None)
                        score_sub(q, 1, m1)
                        next(norm, None)
                        p0 = prob_sum(q, 0)
                        next(norm, None)
                        p1 = prob_sum(q, 1)
                        next(norm, None)
                        prob_inv(q, 0, p0)
                        prob_inv(q, 1, p1)
                    for _ in norm:
                        pass
                    for place in range(3, 6):
                        ffn_place(q, place)
                if links[0]:
                    linked(links[0])
                    dve.sem_inc(s["link"], -links[0])

            rounds(dve, body)
            dve.wait_ge(s["fadd"], NIT)
            dve.tensor_tensor(skip[:, :, :], skip[:, :, :], stream[:, :, :], ALU.add).then_inc(s["sum_r"], 1)


_INS = ['x', 'ctx_1024', 'L0_attn_W_query', 'L0_attn_W_key', 'L0_attn_W_value', 'L0_xattn_fm_w', 'L0_xattn_fm_b',
        'L0_xattn_fc_w', 'L0_xattn_fc_b', 'L0_ffn_Wqkv', 'L0_ffn_q_scale', 'L0_ffn_k_scale', 'L0_ffn_Wo',
        'L0_ffn_ln_g', 'L0_ffn_ln_b', 'L0_ffn_W1', 'L0_ffn_b1', 'L0_ffn_W2', 'L0_ffn_b2']
_OUTS = [((4, 512, 128), 'float32')]


def kernel(**inputs):
    import numpy as _np
    import concourse.bacc as _bacc
    from concourse import mybir as _mybir
    from concourse.bass_utils import run_bass_kernel_spmd as _run

    nc = _bacc.Bacc("TRN2", target_bir_lowering=False, num_devices=1)
    arrays, args = {}, {}
    for name in _INS:
        a = _np.ascontiguousarray(inputs[name])
        arrays[f"in_{name}_dram"] = a
        args[name] = nc.dram_tensor(f"in_{name}_dram", a.shape, _mybir.dt.from_np(a.dtype), kind="ExternalInput").ap()
    outs = []
    for i, (shape, dtype) in enumerate(_OUTS):
        dt = _mybir.dt.from_np(_np.dtype(dtype))
        outs.append(nc.dram_tensor(f"out_{i}_dram", shape, dt, kind="ExternalOutput").ap())
    decoder(nc, args, *outs)
    r = _run(nc, [arrays], core_ids=[0])
    got = tuple(r.results[0][f"out_{i}_dram"] for i in range(len(_OUTS)))
    return got[0]
```

```python
from contextlib import ExitStack

import numpy as np

import concourse.bass as bass
from concourse import mybir

ALU = mybir.AluOpType
ACT = mybir.ActivationFunctionType
AX = mybir.AxisListType
F32 = mybir.dt.float32
F32R = mybir.dt.float32r
I32 = mybir.dt.int32

P = 128
D = 128
BATCH, SEQ = 4, 512
GPB = SEQ // P
DEPTH = 6
NIT = DEPTH * BATCH
HEADS, DH = 16, 64
INNER = HEADS * DH
WIN = 32
PAIRS = HEADS // 2
FF = 341
FCH = [(0, 128), (128, 128), (256, FF - 256)]
WPARTS = [INNER, INNER, INNER, 2 * FF]
WAT = [sum(WPARTS[:n]) for n in range(4)]
WCOLS = sum(WPARTS)
CTX = 77
XH, XE, XF = 16, 8, 16
ATT_SCALE = 1.0 / float(np.sqrt(128.0))
NEG = -1e30
RSQRT_MAGIC = float(0x5F3759DF)
LN_EPS = 1e-5
FFN_PLACES = {(0, 2): 0, (0, 3): 1, (2, 2): 2, (2, 4): 3, (2, 5): 4, (3, 1): 5, (3, 2): 6, (3, 3): 7, (3, 6): 8, (3, 5): 9}
FJOBS = 10
DMAS_FFN = 11


def rotary_tables():
    f = np.float32
    half = np.arange(0, DH, 2, dtype=f)
    inv_freq = (f(1.0) / np.power(f(10000.0), half / f(DH))).astype(f)
    t = np.arange(SEQ, dtype=f)
    ang = (t[:, None] * inv_freq[None, :]).astype(f).astype(np.float64)
    base = ((half + f(0.4 * DH)) / f(1.4 * DH)).astype(f)
    power = ((t - SEQ // 2) / f(WIN // 2)).astype(f)
    scale = np.power(base[None, :].astype(np.float64), power[:, None].astype(np.float64))
    cos, sin = np.cos(ang), np.sin(ang)
    kinds = []
    for s in (8.0 * scale, 1.0 / scale):
        kinds.append(np.concatenate([cos * s, cos * s], 1))
        kinds.append(np.concatenate([sin * s, -sin * s], 1))
    tab = np.stack(kinds, 1).astype(f)
    return np.ascontiguousarray(tab.reshape(GPB, P, 4, DH).transpose(1, 2, 0, 3))


def window_masks():
    m = np.zeros((2, P, 2, 64), np.float32)
    q = np.arange(WIN)[:, None]
    c = np.arange(WIN)[None, :]
    blk = np.concatenate([np.where(c >= q, 0.0, NEG), np.where(c <= q, 0.0, NEG)], 1)
    for first in range(2):
        for hp in range(2):
            for wpar in range(2):
                rows = slice(hp * 64 + wpar * 32, hp * 64 + wpar * 32 + 32)
                for half in range(2):
                    b = blk.copy()
                    if first and half == 0 and wpar == 0:
                        b[:, :WIN] = NEG
                    m[first, rows, half, :] = b
    return np.ascontiguousarray(m.reshape(2, P, P).transpose(1, 0, 2))


def causal_mask():
    q = np.arange(P)[:, None]
    return np.where(np.arange(P)[None, :] <= q, 0.0, NEG).astype(np.float32)


def feature_heads():
    return (np.arange(P)[:, None] // XF == np.arange(XH // 2)[None, :]).astype(np.float32)


def feature_signs():
    return np.where(np.arange(P)[:, None] % XF < XE, 1.0, -1.0).astype(np.float32)


def cnt(it, per, c):
    return it * per + c


def need(eng, semaphore, value):
    if isinstance(value, int) and value <= 0:
        return
    eng.wait_ge(semaphore, value)


def rsqrt_guess(v, y, w):
    return v.tensor_scalar(y.bitcast(I32), w.bitcast(I32), -0.5, RSQRT_MAGIC, ALU.mult, ALU.add)


def rsqrt_step(v, n, y, w, t):
    if n == 0:
        return v.scalar_tensor_tensor(out=t, in0=y, scalar=-0.5, in1=y, op0=ALU.mult, op1=ALU.mult)
    if n == 1:
        return v.tensor_tensor(t, t, w, ALU.mult)
    return v.scalar_tensor_tensor(out=y, in0=t, scalar=1.5, in1=y, op0=ALU.add, op1=ALU.mult)


def bcast(ap, axis, n):
    u = ap.unsqueeze(axis)
    shape = list(u.shape)
    shape[axis] = n
    return u.broadcast_to(shape)


def rows(dram, n):
    return bass.AP(tensor=dram.tensor, offset=dram.offset, ap=[[0, n]] + [list(x) for x in dram.ap])


def decoder(nc, a, out):
    with ExitStack() as ctx:
        def sb(name, shape, dt=F32):
            return ctx.enter_context(nc.sbuf_tensor(name, shape, dt))

        k = dict(
            bank=[ctx.enter_context(nc.psum_tensor(f"bank{i}", [P, 512], F32)) for i in range(8)],
            table_d=nc.inline_tensor(rotary_tables(), "rotary_const").ap(),
            mask_d=nc.inline_tensor(window_masks(), "mask_const").ap(),
            causal_d=nc.inline_tensor(causal_mask(), "causal_const").ap(),
            head_d=nc.inline_tensor(feature_heads(), "head_const").ap(),
            sign_d=nc.inline_tensor(feature_signs(), "sign_const").ap(),
            stream=sb("stream", [P, BATCH * GPB, D]),
            skip_d=nc.dram_tensor("skip", [P, BATCH * GPB * D], F32, kind="Internal").ap(),
            ident=sb("ident", [P, P]),
            mask=sb("mask", [P, 2, P]),
            w_hi=nc.dram_tensor("w_high", [DEPTH, P, WCOLS], F32, kind="Internal").ap(),
            w_lo=nc.dram_tensor("w_low", [DEPTH, P, WCOLS], F32, kind="Internal").ap(),
            rot=sb("rot", [P, DEPTH, 4, GPB * DH]),
        )
        with ExitStack() as part:
            front(nc, part, a, k)
        with ExitStack() as part:
            stack(nc, part, a, k, out)


def front(nc, part, a, k):
    bank, stream, ident, mask, rot = (k[n] for n in ("bank", "stream", "ident", "mask", "rot"))

    def sb(name, shape, dt=F32):
        return part.enter_context(nc.sbuf_tensor("front_" + name, shape, dt))

    def sem(name):
        return part.enter_context(nc.semaphore("front_" + name))

    T = BATCH * GPB
    NJ = XH // 4
    CW = 4 * CTX
    VW = 32
    table = sb("table", [P, 4, GPB * DH])
    qscl = sb("qscl", [P, DEPTH, DH])
    kscl = sb("kscl", [P, DEPTH, DH])
    raw = sb("raw", [P, WCOLS])
    high = sb("high", [P, WCOLS], F32R)
    low = sb("low", [P, WCOLS], F32R)
    causal = sb("causal", [P, P])
    head_of = sb("head_of", [P, XH // 2])
    sign = sb("sign", [P, 1])
    fmb = sb("fmb", [P, 1])
    fmbs = sb("fmbs", [P, 1])
    fmrow = sb("fmrow", [CTX, P])
    fcb = sb("fcb", [P, D])
    bd = sb("bd", [P, P])
    bdx = sb("bdx", [P, 2, P])
    fcw = sb("fcw", [P, NJ, 4, VW])
    fcT = sb("fcT", [P, NJ, P])
    wq = sb("wq", [P, P])
    wk = sb("wk", [P, P])
    wv = sb("wv", [P, P])
    mqk = sb("mqk", [P, P])
    wvT = sb("wvT", [P, P])
    cx = sb("cx", [CTX, BATCH, D])
    cxs = sb("cxs", [CTX, D])
    cxT = sb("cxT", [P, CTX])
    ek = sb("ek", [P, 2, CTX])
    zrow = sb("zrow", [CTX, P])
    vx = sb("vx", [CTX, XH, VW])
    kx = sb("kx", [P, 2, XH // 2, CTX])
    xn = sb("xn", [P, GPB, D])
    xnT = sb("xnT", [P, SEQ])
    qp = sb("qp", [P, SEQ])
    va = sb("va", [P, GPB, D])
    eq = sb("eq", [P, 2, SEQ])
    pa = sb("pa", [P, 2, SEQ])
    paT = sb("paT", [P, 2, SEQ])
    xd = sb("xd", [P, 2, CW])
    xp = sb("xp", [P, 4, CW])
    xpT = sb("xpT", [CTX, 2, 512])
    xoT = sb("xoT", [P, NJ, P])
    st = sb("st", [P, T, 6])
    mv = sb("mv", [P, T, 2])
    lw = sb("lw", [P, 3, T])
    amax = sb("amax", [P, GPB])
    asum = sb("asum", [P, GPB])
    ainv = sb("ainv", [P, GPB])
    xmax = sb("xmax", [P, 2, 4])
    xsum = sb("xsum", [P, 4, 4])
    xinv = sb("xinv", [P, 4, 4])

    s_x, s_wa, s_w, s_zero, s_bd, s_id = sem("x_in"), sem("wqkv_in"), sem("weights_in"), sem("edges_zeroed"), sem("bd_in"), sem("ident_made")
    s_const, s_feat, s_prep, s_prepped = sem("const_ready"), sem("features_ready"), sem("prep_made"), sem("prep_out")
    s_xn, s_xnT_p, s_xnT = sem("xn_ready"), sem("xnT_made"), sem("xnT_ready")
    s_qp_p, s_qp, s_va_p, s_va = sem("qp_made"), sem("qp_ready"), sem("va_made"), sem("va_ready")
    s_sc, s_nm, s_pa, s_paT_p, s_paT = sem("scores_made"), sem("max_ready"), sem("p_ready"), sem("pT_made"), sem("pT_ready")
    s_pv, s_att = sem("pv_made"), sem("att_added")
    s_cxs, s_cxT_p, s_cxT, s_zk, s_ek, s_zr, s_vx, s_kx = (
        sem(n) for n in ("cxs_ready", "cxT_made", "cxT_ready", "zk_made", "ek_ready", "zrow_ready", "vx_ready", "kx_ready"))
    s_zq, s_eq = sem("zq_made"), sem("eq_ready")
    s_xs, s_xd, s_xp, s_xi, s_xpn, s_xpT_p, s_xpT = (
        sem(n) for n in ("xscores_made", "xdiff_ready", "xp_ready", "xinv_ready", "xp_normed", "xpT_made", "xpT_ready"))
    s_xav, s_xoT, s_fc, s_xadd = (sem(n) for n in ("xav_made", "xoT_ready", "fc_made", "xatt_added"))
    s_skip, s_link = sem("skip_ready"), sem("dve_link")
    s_raw = [sem(f"raw_in_{c}") for c in range(4)]
    s_wst = [sem(f"parts_stored_{c}") for c in range(4)]
    s_high, s_low = sem("high_ready"), sem("low_ready")
    fm_b = a["L0_xattn_fm_b"]
    small = [
        (wq[:, :], a["L0_attn_W_query"]), (wk[:, :], a["L0_attn_W_key"]), (wv[:, :], a["L0_attn_W_value"]),
        (causal[:, :], k["causal_d"]), (head_of[:, :], k["head_d"]), (sign[:, :], k["sign_d"]),
        (cx[:, :, :], a["ctx_1024"].rearrange("b s d -> s b d")),
        (fcb[:, :], rows(a["L0_xattn_fc_b"], P)),
        (fmrow[:, :], bass.AP(tensor=fm_b.tensor, offset=0, ap=[[0, CTX], [0, XH], [1, XE]])),
        (fmb[:, :], bass.AP(tensor=fm_b.tensor, offset=0, ap=[[0, XH], [1, XE], [1, 1]])),
        (table[:, :, :].rearrange("p k (j d) -> p k j d", d=DH), k["table_d"]),
        (mask[:, :, :], k["mask_d"]),
        (qscl[:, :, :], rows(a["L0_ffn_q_scale"], P)), (kscl[:, :, :], rows(a["L0_ffn_k_scale"], P)),
    ]
    ALL_SMALL = 16 * (len(small) - 3 + NJ)
    x_d = a["x"].rearrange("b (j p) d -> p (b j) d", p=P)
    N = GPB * NJ

    with nc.Block() as block:
        @block.sync
        def _(sp):
            for b in range(BATCH):
                sp.dma_start(stream[:, GPB * b:GPB * (b + 1), :], x_d[:, GPB * b:GPB * (b + 1), :]).then_inc(s_x, 16)

            def split(layer):
                for c in range(4):
                    need(sp, s_low, 8 * layer + (2 * c - 6))
                    cols = slice(WAT[c], WAT[c] + WPARTS[c])
                    src = a["L0_ffn_Wqkv"][layer, :, cols] if c < 3 else a["L0_ffn_W1"][layer, :, :]
                    sp.dma_start(raw[:, cols], src).then_inc(s_raw[c], 16)
                for c in range(4):
                    sp.wait_ge(s_low, 8 * layer + (2 * c + 2))
                    cols = slice(WAT[c], WAT[c] + WPARTS[c])
                    sp.dma_start(k["w_hi"][layer, :, cols], high[:, cols].bitcast(F32)).then_inc(s_wst[c], 16)
                    sp.dma_start(k["w_lo"][layer, :, cols], low[:, cols].bitcast(F32)).then_inc(s_wst[c], 16)

            split(0)
            sp.wait_ge(s_zero, 3)
            with nc.allow_non_contiguous_dma(reason="8 x 8 transposed blocks"):
                for h in range(XH):
                    r = slice(XE * h, XE * h + XE)
                    sp.dma_start(bd[r, r], a["L0_xattn_fm_w"].rearrange("e d -> d e")).then_inc(s_bd, 16)
            with sp.Fori(1, DEPTH) as layer:
                split(layer)
            sp.wait_ge(s_xadd, T)
            sp.dma_start(k["skip_d"], stream[:, :, :].rearrange("p j d -> p (j d)")).then_inc(s_skip, 16)
            sp.wait_ge(s_skip, 16)
            for c in range(4):
                sp.wait_ge(s_wst[c], 32 * DEPTH)

        @block.gpsimd
        def _(pool):
            pool.memset(ident[:, :], 0.0).then_inc(s_id, 1)
            pool.wait_ge(s_id, 1)
            pool.affine_select(out=ident[:, :], in_=ident[:, :], compare_op=ALU.not_equal, fill=1.0, base=0,
                               pattern=[[-1, P]], channel_multiplier=1).then_inc(s_id, 1)
            pool.memset(fcw[:, :, :, :], 0.0).then_inc(s_zero, 1)
            pool.memset(bd[:, :], 0.0).then_inc(s_zero, 1)
            pool.memset(vx[:, :, :], 0.0).then_inc(s_zero, 1)

            def low_weights(layer, c, half):
                lo, hi = (0, 512) if half == 0 else (512, WPARTS[c])
                cols = slice(WAT[c] + lo, WAT[c] + hi)
                pool.wait_ge(s_high, 4 * layer + (c + 1))
                pool.tensor_tensor(low[:, cols], raw[:, cols], high[:, cols].bitcast(F32),
                                   ALU.subtract).then_inc(s_low, 1)

            for layer in range(2):
                for c in range(4):
                    for half in range(2):
                        low_weights(layer, c, half)
            pool.wait_ge(s_w, ALL_SMALL)
            for layer in range(DEPTH):
                for n, scl in enumerate((qscl, kscl)):
                    pool.tensor_tensor(
                        rot[:, layer, 2 * n:2 * n + 2, :].rearrange("p k (j d) -> p (k j) d", d=DH),
                        table[:, 2 * n:2 * n + 2, :].rearrange("p k (j d) -> p (k j) d", d=DH),
                        bcast(scl[:, layer, :], 1, 2 * GPB), ALU.mult).then_inc(s_const, 1)
            with pool.Fori(0, BATCH) as b:
                for n in range(N):
                    pool.wait_ge(s_xi, cnt(b, N, n + 1))
                    x = xp[:, n % 4, :].rearrange("p (h s) -> p h s", h=4)
                    pool.tensor_tensor(x, x, bcast(xinv[:, n % 4, :], 2, CTX), ALU.mult).then_inc(s_xpn, 1)
                    if n % 4 in (2, 3):
                        low_weights(b + 2, n // 4, n % 2)

        @block.tensor
        def _(pe):
            pe.wait_ge(s_id, 2)
            pe.wait_ge(s_wa, 16 * 3)
            pe.matmul(bank[0][:, 0:P], wq[:, :], wk[:, :], start=True, stop=True)
            pe.transpose(bank[0][:, P:2 * P], wv[:, :], ident[:, :]).then_inc(s_prep, 1)
            pe.wait_ge(s_w, ALL_SMALL)
            for c in range(NJ):
                last = pe.transpose(bank[2][:, P * c:P * c + P], fcw[:, c, :, :].rearrange("p h f -> p (h f)"), ident[:, :])
            last.then_inc(s_prep, 1)
            pe.wait_ge(s_prepped, 2)
            with pe.Fori(0, BATCH) as b:
                pe.wait_ge(s_xn, cnt(b, 1, 1))
                for j in range(GPB):
                    last = pe.transpose(bank[1][:, P * j:P * j + P], xn[:, j, :], ident[:, :])
                last.then_inc(s_xnT_p, 1)
                pe.wait_ge(s_xnT, cnt(b, 1, 1))
                pe.matmul(bank[7][:, :], mqk[:, :], xnT[:, :], start=True, stop=True).then_inc(s_qp_p, 1)
                for j in range(GPB):
                    last = pe.matmul(bank[0][:, P * j:P * j + P], xnT[:, P * j:P * j + P], wvT[:, :],
                                     start=True, stop=True)
                last.then_inc(s_va_p, 1)
                pe.wait_ge(s_qp, cnt(b, 1, 1))
                for i in range(GPB):
                    pe.matmul(bank[3 + i][:, 0:P * (i + 1)], qp[:, P * i:P * i + P], xnT[:, 0:P * (i + 1)],
                              start=True, stop=True).then_inc(s_sc, 1)
                pe.wait_ge(s_va, cnt(b, 1, 1))
                for n in range(GPB + 1):
                    if n < GPB:
                        pe.wait_ge(s_pa, cnt(b, GPB, n + 1))
                        if n >= 2:
                            pe.wait_ge(s_paT, cnt(b, GPB, n - 1))
                        tb = bank[7] if n % 2 == 0 else bank[1]
                        for c in range(n + 1):
                            last = pe.transpose(tb[:, P * c:P * c + P], pa[:, n % 2, P * c:P * c + P], ident[:, :])
                        last.then_inc(s_paT_p, 1)
                    if n == 0:
                        continue
                    i = n - 1
                    pe.wait_ge(s_paT, cnt(b, GPB, i + 1))
                    if i >= 2:
                        pe.wait_ge(s_att, cnt(b, GPB, i - 1))
                    for c in range(i + 1):
                        last = pe.matmul(bank[2 * (i % 2)][:, 0:P], paT[:, i % 2, P * c:P * c + P], va[:, c, :],
                                         start=(c == 0), stop=(c == i))
                    last.then_inc(s_pv, 1)
                pe.wait_ge(s_att, cnt(b, GPB, GPB - 1))
            pe.wait_ge(s_att, T)
            pe.wait_ge(s_bd, 16 * XH)
            pe.wait_ge(s_feat, 2)
            with pe.Fori(0, BATCH) as b:
                pe.wait_ge(s_cxs, cnt(b, 1, 1))
                pe.transpose(bank[3][:, 0:CTX], cxs[:, :], ident[0:CTX, 0:CTX]).then_inc(s_cxT_p, 1)
                pe.wait_ge(s_xn, cnt(b, 1, BATCH + 1))
                for j in range(GPB):
                    last = pe.transpose(bank[0][:, P * j:P * j + P], xn[:, j, :], ident[:, :])
                last.then_inc(s_xnT_p, 1)
                pe.wait_ge(s_cxT, cnt(b, 1, 1))
                for e in range(2):
                    pe.matmul(bank[4][:, P * e:P * e + CTX], bdx[:, e, :], cxT[:, :], start=True, stop=True)
                pe.matmul(bank[4][0:CTX, 2 * P:3 * P], cxT[:, :], bd[:, :], start=True, stop=True).then_inc(s_zk, 1)
                pe.wait_ge(s_xnT, cnt(b, 1, BATCH + 1))
                for e in range(2):
                    pe.matmul(bank[1 + e][:, :], bdx[:, e, :], xnT[:, :], start=True, stop=True).then_inc(s_zq, 1)
                pe.wait_ge(s_kx, cnt(b, 1, 1))
                pe.wait_ge(s_vx, cnt(b, 1, 1))
                for n in range(N + 8):
                    if n < N:
                        g, c = n // NJ, n % NJ
                        pe.wait_ge(s_eq, cnt(b, 2, 1 + c // 2))
                        if n >= 2:
                            pe.wait_ge(s_xd, cnt(b, N, n - 1))
                        h0 = 4 * (c % 2)
                        pe.matmul(bank[3 + n % 2][:, 0:CW], eq[:, c // 2, P * g:P * g + P],
                                  kx[:, c // 2, h0:h0 + 4, :].rearrange("p h s -> p (h s)"),
                                  start=True, stop=True).then_inc(s_xs, 1)
                    if 3 <= n < N + 3:
                        m = n - 3
                        pe.wait_ge(s_xpn, cnt(b, N, m + 1))
                        if m >= 2:
                            pe.wait_ge(s_xpT, cnt(b, N, m - 1))
                        for h in range(4):
                            last = pe.transpose(bank[5 + m % 2][0:CTX, P * h:P * h + P],
                                                xp[:, m % 4, CTX * h:CTX * h + CTX], ident[:, :])
                        last.then_inc(s_xpT_p, 1)
                    if 5 <= n < N + 5:
                        m = n - 5
                        g, c = m // NJ, m % NJ
                        pe.wait_ge(s_xpT, cnt(b, N, m + 1))
                        if c == 0 and g > 1:
                            pe.wait_ge(s_xoT, cnt(b, GPB, g - 1))
                        for h in range(4):
                            last = pe.matmul((bank[7], bank[2])[g % 2][VW * h:VW * h + VW, P * c:P * c + P], vx[:, 4 * c + h, :],
                                             xpT[:, m % 2, P * h:P * h + P], start=True, stop=True)
                        last.then_inc(s_xav, 1)
                    if n >= 8 and (n - 8) % NJ == NJ - 1:
                        g = (n - 8) // NJ
                        pe.wait_ge(s_xoT, cnt(b, GPB, g + 1))
                        if g > 0:
                            pe.wait_ge(s_xadd, cnt(b, GPB, g))
                        for c in range(NJ):
                            last = pe.matmul(bank[0][:, 0:D], xoT[:, c, :], fcT[:, c, :], start=(c == 0), stop=(c == NJ - 1))
                        last.then_inc(s_fc, 1)
                pe.wait_ge(s_xadd, cnt(b, GPB, GPB))

        @block.scalar
        def _(act):
            for n, (dst, src) in enumerate(small):
                act.dma_start(dst, src).then_inc(s_wa if n < 3 else s_w, 16)
            act.wait_ge(s_zero, 1)
            for c in range(NJ):
                act.dma_start(fcw[:, c, :, 0:XF], a["L0_xattn_fc_w"][:, 4 * XF * c:4 * XF * (c + 1)].rearrange(
                    "o (h f) -> o h f", f=XF)).then_inc(s_w, 16)

            def round_weights(layer, c):
                act.wait_ge(s_raw[c], 16 * (layer + 1))
                need(act, s_wst[c], 32 * layer)
                cols = slice(WAT[c], WAT[c] + WPARTS[c])
                act.copy(high[:, cols], raw[:, cols]).then_inc(s_high, 1)

            act.wait_ge(s_prep, 1)
            act.copy(mqk[:, :], bank[0][:, 0:P])
            act.copy(wvT[:, :], bank[0][:, P:2 * P]).then_inc(s_prepped, 1)
            act.wait_ge(s_prep, 2)
            act.copy(fcT[:, :, :].rearrange("p c o -> p (c o)"), bank[2][:, :]).then_inc(s_prepped, 1)
            for c in range(4):
                round_weights(0, c)
            with act.Fori(0, BATCH) as b:
                act.wait_ge(s_xnT_p, cnt(b, 1, 1))
                act.copy(xnT[:, :], bank[1][:, :]).then_inc(s_xnT, 1)
                act.wait_ge(s_qp_p, cnt(b, 1, 1))
                act.copy(qp[:, :], bank[7][:, :]).then_inc(s_qp, 1)
                act.wait_ge(s_va_p, cnt(b, 1, 1))
                act.copy(va[:, :, :].rearrange("p j d -> p (j d)"), bank[0][:, :]).then_inc(s_va, 1)
                for n in range(GPB + 1):
                    if n < GPB:
                        act.wait_ge(s_nm, cnt(b, GPB, n + 1))
                        if n >= 2:
                            act.wait_ge(s_paT_p, cnt(b, GPB, n - 1))
                        w = P * (n + 1)
                        act.activation(pa[:, n % 2, 0:w], bank[3 + n][:, 0:w], ACT.Exp, bias=amax[:, n:n + 1],
                                       scale=ATT_SCALE, accum_out=asum[:, n:n + 1]).then_inc(s_pa, 1)
                    if n == 0:
                        continue
                    i = n - 1
                    w = P * (i + 1)
                    act.wait_ge(s_paT_p, cnt(b, GPB, i + 1))
                    if i >= 2:
                        act.wait_ge(s_pv, cnt(b, GPB, i - 1))
                    tb = bank[7] if i % 2 == 0 else bank[1]
                    act.copy(paT[:, i % 2, 0:w], tb[:, 0:w]).then_inc(s_paT, 1)
            for c in range(4):
                round_weights(1, c)
            act.wait_ge(s_w, ALL_SMALL)
            act.wait_ge(s_bd, 16 * XH)
            act.mul(fmbs[:, :], fmb[:, :], sign[:, 0:1]).then_inc(s_feat, 1)
            for e in range(2):
                last = act.copy(bdx[:, e, :].rearrange("p (h r i) -> p h r i", r=2, i=XE),
                                bcast(bd[:, P // 2 * e:P // 2 * (e + 1)].rearrange("p (h i) -> p h i", i=XE), 2, 2))
            last.then_inc(s_feat, 1)
            act.wait_ge(s_feat, 2)
            with act.Fori(0, BATCH) as b:
                act.copy(cxs[:, :], cx[:, b, :]).then_inc(s_cxs, 1)
                act.wait_ge(s_cxT_p, cnt(b, 1, 1))
                act.copy(cxT[:, :], bank[3][:, 0:CTX]).then_inc(s_cxT, 1)
                act.wait_ge(s_xnT_p, cnt(b, 1, BATCH + 1))
                act.copy(xnT[:, :], bank[0][:, :]).then_inc(s_xnT, 1)
                act.wait_ge(s_zk, cnt(b, 1, 1))
                act.activation(ek[:, :, :], bank[4][:, 0:2 * P].rearrange("p (e t) -> p e t", e=2)[:, :, 0:CTX], ACT.Exp,
                               bias=fmbs[:, 0:1], scale=sign[:, 0:1]).then_inc(s_ek, 1)
                act.wait_ge(s_zr, cnt(b, 1, 1))
                z3 = zrow[:, :].rearrange("p (h e) -> p h e", e=XE)
                act.activation(vx[:, :, 0:XE], z3, ACT.Exp)
                act.activation(vx[:, :, XE:XF], z3, ACT.Exp, scale=-1.0).then_inc(s_vx, 1)
                for e in range(2):
                    act.wait_ge(s_zq, cnt(b, 2, e + 1))
                    act.activation(eq[:, e, :], bank[1 + e][:, :], ACT.Exp, bias=fmbs[:, 0:1],
                                   scale=sign[:, 0:1]).then_inc(s_eq, 1)
                for n in range(N + 6):
                    if n < N:
                        act.wait_ge(s_xd, cnt(b, N, n + 1))
                        if n >= 4:
                            act.wait_ge(s_xpT_p, cnt(b, N, n - 3))
                        if n % 4 == 2:
                            round_weights(b + 2, n // 4)
                        act.activation(xp[:, n % 4, :], xd[:, n % 2, :], ACT.Exp, scale=ATT_SCALE).then_inc(s_xp, 1)
                    if 3 <= n < N + 3:
                        m = n - 3
                        act.wait_ge(s_xpT_p, cnt(b, N, m + 1))
                        if m >= 2:
                            act.wait_ge(s_xav, cnt(b, N, m - 1))
                        act.copy(xpT[:, m % 2, :], bank[5 + m % 2][0:CTX, :]).then_inc(s_xpT, 1)
                    if n >= 6 and (n - 6) % NJ == NJ - 1:
                        g = (n - 6) // NJ
                        act.wait_ge(s_xav, cnt(b, N, NJ * (g + 1)))
                        if g > 0:
                            act.wait_ge(s_fc, cnt(b, GPB, g))
                        act.copy(xoT[:, :, :].rearrange("p c t -> p (c t)"), (bank[7], bank[2])[g % 2][:, :]).then_inc(s_xoT, 1)

        @block.vector
        def _(dve):
            links = [0]

            def link(ins, wait=True):
                links[0] += 1
                ins.then_inc(s_link, 1)
                if wait:
                    dve.wait_ge(s_link, links[0])

            def drop_links():
                dve.wait_ge(s_link, links[0])
                dve.sem_inc(s_link, -links[0])
                links[0] = 0

            w, y, t = lw[:, 0, :], lw[:, 1, :], lw[:, 2, :]

            def statistics():
                for j in range(T):
                    link(dve.bn_stats(st[:, j, :], stream[:, j, :]), j == T - 1)
                for j in range(T):
                    link(dve.bn_aggr(mv[:, j, :], st[:, j, :]), j == T - 1)
                link(dve.tensor_scalar(w, mv[:, :, 1], LN_EPS, None, ALU.add))
                link(rsqrt_guess(dve, y, w))
                for _ in range(3):
                    for n in range(3):
                        link(rsqrt_step(dve, n, y, w, t))
                drop_links()

            def normalise_row(b):
                dve.nop(nofuse=True)
                for j in range(GPB):
                    i = b * GPB + j
                    last = dve.tensor_scalar(xn[:, j, :], stream[:, i, :], mv[:, i, 0:1], lw[:, 1, bass.ds(i, 1)],
                                             ALU.subtract, ALU.mult)
                last.then_inc(s_xn, 1)

            dve.wait_ge(s_x, 16 * BATCH)
            statistics()
            dve.wait_ge(s_w, ALL_SMALL)
            with dve.Fori(0, BATCH) as b:
                def tile(j):
                    return stream[:, b * GPB + j, :]

                normalise_row(b)
                for i in range(GPB):
                    dve.wait_ge(s_sc, cnt(b, GPB, i + 1))
                    wide = P * (i + 1)
                    diag = bank[3 + i][:, P * i:wide]
                    link(dve.tensor_tensor(diag, diag, causal[:, :], ALU.add))
                    link(dve.tensor_reduce(amax[:, i:i + 1], bank[3 + i][:, 0:wide], AX.X, ALU.max))
                    dve.tensor_scalar(amax[:, i:i + 1], amax[:, i:i + 1], -ATT_SCALE, None, ALU.mult).then_inc(s_nm, 1)
                for i in range(GPB):
                    dve.wait_ge(s_pa, cnt(b, GPB, i + 1))
                    link(dve.reciprocal(ainv[:, i:i + 1], asum[:, i:i + 1]))
                    dve.wait_ge(s_pv, cnt(b, GPB, i + 1))
                    dve.scalar_tensor_tensor(out=tile(i), in0=bank[2 * (i % 2)][:, 0:P], scalar=ainv[:, i:i + 1],
                                             in1=tile(i), op0=ALU.mult, op1=ALU.add).then_inc(s_att, 1)
                drop_links()
            dve.wait_ge(s_att, T)
            statistics()
            with dve.Fori(0, BATCH) as b:
                def tile(j):
                    return stream[:, b * GPB + j, :]

                normalise_row(b)
                dve.wait_ge(s_ek, cnt(b, 1, 1))
                for e in range(2):
                    last = dve.tensor_tensor(kx[:, e, :, :], bcast(ek[:, e, :], 1, XH // 2), bcast(head_of[:, :], 2, CTX),
                                             ALU.mult)
                last.then_inc(s_kx, 1)
                dve.tensor_tensor(zrow[:, :], bank[4][0:CTX, 2 * P:3 * P], fmrow[:, :], ALU.add).then_inc(s_zr, 1)
                for n in range(N + 9):
                    if n < N:
                        dve.wait_ge(s_xs, cnt(b, N, n + 1))
                        sc = bank[3 + n % 2][:, 0:CW].rearrange("p (h s) -> p h s", h=4)
                        link(dve.tensor_reduce(xmax[:, n % 2, :], sc, AX.X, ALU.max))
                        if n >= 2:
                            dve.wait_ge(s_xp, cnt(b, N, n - 1))
                        dve.tensor_tensor(xd[:, n % 2, :].rearrange("p (h s) -> p h s", h=4), sc,
                                          bcast(xmax[:, n % 2, :], 2, CTX), ALU.subtract).then_inc(s_xd, 1)
                    if 1 <= n < N + 1:
                        m = n - 1
                        dve.wait_ge(s_xp, cnt(b, N, m + 1))
                        link(dve.tensor_reduce(xsum[:, m % 4, :], xp[:, m % 4, :].rearrange("p (h s) -> p h s", h=4),
                                               AX.X, ALU.add))
                        if m >= 4:
                            dve.wait_ge(s_xpn, cnt(b, N, m - 3))
                        dve.reciprocal(xinv[:, m % 4, :], xsum[:, m % 4, :]).then_inc(s_xi, 1)
                    if n >= 9 and (n - 9) % NJ == NJ - 1:
                        g = (n - 9) // NJ
                        dve.wait_ge(s_fc, cnt(b, GPB, g + 1))
                        link(dve.tensor_tensor(tile(g), bank[0][:, 0:D], tile(g), ALU.add))
                        dve.tensor_tensor(tile(g), tile(g), fcb[:, :], ALU.add).then_inc(s_xadd, 1)
                drop_links()
            dve.wait_ge(s_xadd, T)
            statistics()
            dve.wait_ge(s_skip, 16)
            for j in range(T):
                dve.tensor_scalar(stream[:, j, :], stream[:, j, :], mv[:, j, 0:1], y[:, j:j + 1], ALU.subtract, ALU.mult)


def stack(nc, part, a, k, out):
    bank, stream, ident, mask, rot = (k[n] for n in ("bank", "stream", "ident", "mask", "rot"))

    def sb(name, shape, dt=F32):
        return part.enter_context(nc.sbuf_tensor(name, shape, dt))

    def sem(name):
        return part.enter_context(nc.semaphore(name))

    xT = sb("xT", [P, 2, SEQ + 1], F32R)
    xs = sb("xs", [P, 2, D])
    xs_part = sb("xs_part", [P, 2, 2, D], F32R)
    w_hi = sb("w_hi", [P, 3 * INNER], F32R)
    w_lo = sb("w_lo", [P, 3 * INNER], F32R)
    wo = sb("wo", [P, PAIRS, D])
    w1_hi = sb("w1_hi", [P, 2 * FF], F32R)
    w1_lo = sb("w1_lo", [P, 2 * FF], F32R)
    w2 = sb("w2", [P, 3, D])
    lng = sb("lng", [P, 1])
    lnb = sb("lnb", [P, 1])
    b1c = sb("b1c", [P, 6])
    sq = sb("sq", [P, 2, 512])
    qk_c = sb("qk_c", [P, 2, 2, INNER])
    qk_s = sb("qk_s", [P, 2, INNER])
    ssq = sb("ssq", [P, 2, 2 * HEADS])
    nrm = sb("nrm", [P, 2, 2 * HEADS])
    ntmp = sb("ntmp", [P, 2 * HEADS])
    qT = sb("qT", [P, PAIRS, P])
    kT = sb("kT", [P, PAIRS, WIN + SEQ])
    v_own = sb("v_own", [P, GPB, INNER])
    v_back = sb("v_back", [P, GPB, INNER])
    smax = sb("smax", [P, 2, PAIRS])
    sdif = sb("sdif", [P, 2, 512])
    prob = sb("prob", [P, 2, 2 * 512])
    psm = sb("psm", [P, 2, 8])
    pinv = sb("pinv", [P, 2, 8])
    pT = sb("pT", [P, PAIRS, P])
    att = sb("att", [P, INNER])
    attT = sb("attT", [P, PAIRS, P])
    f_x = sb("f_x", [P, GPB, D])
    f_xT = sb("f_xT", [P, SEQ + 1])
    f_n = sb("f_n", [P, GPB, D])
    f_nT = sb("f_nT", [P, SEQ], F32R)
    f_nT_lo = sb("f_nT_lo", [P, SEQ], F32R)
    f_v = sb("f_v", [P, 2, SEQ])
    f_h = sb("f_h", [P, 3, SEQ])
    st = sb("st", [P, GPB, 6])
    mv = sb("mv", [P, GPB, 2])
    lw = sb("lw", [P, 3, GPB])

    total = v_own[:, 0:2, :].rearrange("p a (b d) -> p (a b) d", d=D)

    names = dict(
        zeroed="edges_zeroed", wq_in="wq_in", wk_in="wk_in", wv_in="wv_in", wo_in="wo_in", wf_in="ffn_weights_in",
        xs_r="xs_ready", xt_p="xT_made", xt_r="xT_ready", xlo="x_low_ready", proj="proj_made", ab="cos_sin_ready", sqr="squares_ready",
        red="square_sums_ready", nr="norms_ready", rotd="rotated", qkn="qk_normed", v_r="values_ready",
        qkT_p="qkT_made", qkT_r="qkT_ready", sc="scores_made", sub="scores_read", dif="scores_less_max", ex="exp_ready", ps="prob_sums_ready",
        pn="prob_normed", pT_p="probT_made", pT_r="probT_ready", av="av_made", av_r="att_ready", aT_p="attT_made",
        aT_r="attT_ready", wo_p="attn_out_made", added="attn_added", fx="ffn_x_ready",
        f_p="ffn_made", f1="ffn_shifted_ready", f2="ffn_shiftedT_ready", f3="ffn_normed", f4="ffn_normedT_ready", f5="ffn_low_ready",
        fg="ffn_gate_ready", fv="ffn_value_ready", fh="ffn_hidden_ready", fadd="ffn_added", link="dve_chain",
        sum_r="out_summed", skip_in="skip_in", stored="out_stored")
    s = {key: sem(name) for key, name in names.items()}

    class Step:

        def __init__(self, it, j):
            self.it, self.j = it, j

        def on(self, off):
            return not isinstance(self.it, int) or 0 <= GPB * self.it + self.j + off < GPB * NIT

        def next(self):
            return Step(self.it, self.j + 1) if self.j < GPB - 1 else Step(self.it + 1, 0)

        def count(self, per, off, c):
            return self.it * (per * GPB) + (per * (self.j + off) + c)

        def idx(self, off):
            return (self.j + off) % GPB

        def slot(self, off):
            return (self.it * GPB + (self.j + off)) % (BATCH * GPB)

        def par(self, off):
            return (self.j + off) % 2

    def round_on(it, back):
        return not isinstance(it, int) or 0 <= it - back < NIT

    def weights_due(it, back, dmas):
        return ((it - back) // BATCH + 1) * (16 * dmas)

    shifted = [sem(f"values_shifted_{j}") for j in range(GPB)]

    def need_shifted(eng, q, off):
        row, j = (q.j + off) // GPB, (q.j + off) % GPB
        need(eng, shifted[j], (q.it + (row + 1)) * (16 if j == 0 else 32))

    w_d = {n: a["L0_ffn_" + n] for n in ("Wo", "ln_g", "ln_b", "b1", "W2", "b2")}
    NPROJ = 6
    FIRST_LOOP = 3

    def rounds(eng, body):
        for it in range(FIRST_LOOP):
            body(it)
        with eng.Fori(FIRST_LOOP, NIT - 1) as it:
            body(it)
        for it in (NIT - 1, NIT, NIT + 1):
            body(it)

    with nc.Block() as block:
        @block.sync
        def _(sp):
            def load(layer, part_no):
                cols = slice(INNER * part_no, INNER * (part_no + 1))
                for dst, src in ((w_hi, k["w_hi"]), (w_lo, k["w_lo"])):
                    sp.dma_start(dst[:, cols].bitcast(F32), src[layer, :, cols]).then_inc(s[("wq_in", "wk_in", "wv_in")[part_no]], 16)

            def load_wo(layer):
                sp.dma_start(wo[:, :, :], w_d["Wo"][layer, :, :].rearrange("(c p) d -> p c d", p=P)).then_inc(s["wo_in"], 16)

            def load_ffn(layer):
                for dst, src in ((w1_hi, k["w_hi"]), (w1_lo, k["w_lo"])):
                    sp.dma_start(dst[:, :].bitcast(F32), src[layer, :, WAT[3]:WCOLS]).then_inc(s["wf_in"], 16)
                w2_d = w_d["W2"][layer, :, :]
                sp.dma_start(w2[:, 0:2, :], w2_d[0:2 * P, :].rearrange("(c p) d -> p c d", p=P)).then_inc(s["wf_in"], 16)
                lo, m = FCH[2]
                sp.dma_start(w2[0:m, 2, :], w2_d[lo:lo + m, :]).then_inc(s["wf_in"], 16)

                def col(v):
                    return v.rearrange("(p o) -> p o", o=1)

                sp.dma_start(lng[:, :], col(w_d["ln_g"][layer, :])).then_inc(s["wf_in"], 16)
                sp.dma_start(lnb[:, :], col(w_d["ln_b"][layer, :])).then_inc(s["wf_in"], 16)
                b1 = w_d["b1"][layer, :]
                for n in range(2):
                    sp.dma_start(b1c[:, 3 * n:3 * n + 2],
                                 b1[FF * n:FF * n + 2 * P].rearrange("(c p) -> p c", p=P)).then_inc(s["wf_in"], 16)
                    sp.dma_start(b1c[0:m, 3 * n + 2:3 * n + 3], col(b1[FF * n + lo:FF * n + lo + m])).then_inc(s["wf_in"], 16)
                sp.dma_start(w2[m:m + 1, 2, :], w_d["b2"][layer:layer + 1, :]).then_inc(s["wf_in"], 16)

            with nc.allow_non_contiguous_dma(reason="bias columns"):
                for n in range(3):
                    load(0, n)
                load_wo(0)
                load_ffn(0)
                def shift_values(it, j):
                    q = Step(it, j)
                    sp.wait_ge(s["v_r"], q.count(2, 0, 2))
                    if j > 0:
                        sp.dma_start(v_back[0:WIN, j, :], v_own[P - WIN:P, j - 1, :]).then_inc(shifted[j], 16)
                    sp.dma_start(v_back[WIN:P, j, :], v_own[0:P - WIN, j, :]).then_inc(shifted[j], 16)

                def load_next(layer, n):
                    sp.wait_ge(s["proj"], NPROJ * (BATCH * GPB * (layer + 1) - 1) + 2 * n + 2)
                    load(layer + 1, n)

                def layer_rows(layer):
                    g = BATCH * GPB * layer
                    for row in range(BATCH):
                        for j in range(GPB):
                            if layer > 0 and row == 1 and j == 0:
                                sp.wait_ge(s["wo_p"], g)
                                load_wo(layer)
                            last = row == BATCH - 1 and j == GPB - 1 and layer + 1 < DEPTH
                            if last:
                                load_next(layer, 0)
                                load_next(layer, 1)
                            shift_values(BATCH * layer + row, j)
                            if last:
                                load_next(layer, 2)
                            if layer > 0 and row == 2 and j == 0:
                                sp.wait_ge(s["fadd"], BATCH * layer)
                                load_ffn(layer)

                for layer in range(DEPTH):
                    layer_rows(layer)
            sp.wait_ge(s["av"], 2 * GPB * NIT)
            sp.dma_start(v_own[:, 0:2, :].rearrange("p a n -> p (a n)"), k["skip_d"]).then_inc(s["skip_in"], 16)
            sp.wait_ge(s["sum_r"], 1)
            sp.dma_start(out.rearrange("b (j p) d -> p (b j) d", p=P), total).then_inc(s["stored"], 16)
            sp.wait_ge(s["stored"], 16)

        @block.tensor
        def _(pe):
            front_job = [None]

            def shared_bank(reader, value):
                if front_job[0] is not None:
                    pe.wait_ge(*front_job[0])
                front_job[0] = (s[reader], value)

            def transpose_x(q):
                if not q.on(1):
                    return
                shared_bank("xt_r", q.count(1, 1, 1))
                pe.wait_ge(s["xlo"], q.count(1, 1, 1))
                for n in range(2):
                    last = pe.transpose(bank[7][:, P * n:P * n + P], xs_part[:, q.par(1), n, :].bitcast(F32), ident[:, :])
                last.then_inc(s["xt_p"], 1)

            def ffn_job(q, n):
                if not round_on(q.it, 2):
                    return
                row = q.it - 2
                if n < 2:
                    shared_bank(("f1", "f2")[n], row + 1)
                elif n == 2:
                    shared_bank("f4", row + 1)
                elif n < 9:
                    shared_bank(("fg", "fv")[(n - 3) % 2], row * 3 + ((n - 3) // 2 + 1))
                else:
                    shared_bank("fadd", row + 1)
                b7 = bank[7]
                if n == 0:
                    pe.wait_ge(s["fx"], row + 1)
                    for c in range(GPB):
                        last = pe.transpose(b7[:, P * c:P * c + P], f_x[:, c, :], ident[:, :])
                elif n == 1:
                    pe.wait_ge(s["f1"], row + 1)
                    for c in range(GPB):
                        last = pe.transpose(b7[:, P * c:P * c + P], f_xT[:, P * c:P * c + P], ident[:, :])
                elif n == 2:
                    pe.wait_ge(s["wf_in"], weights_due(q.it, 2, DMAS_FFN))
                    pe.wait_ge(s["f3"], row + 1)
                    for c in range(GPB):
                        last = pe.transpose(b7[:, P * c:P * c + P], f_n[:, c, :], ident[:, :])
                elif n < 9:
                    c, value = (n - 3) // 2, (n - 3) % 2
                    lo, m = FCH[c]
                    if n == 3:
                        pe.wait_ge(s["f5"], row + 1)
                    col = lo if value else FF + lo
                    pe.matmul(b7[0:m, :], w1_hi[:, col:col + m], f_nT_lo[:, :], start=True, stop=False)
                    pe.matmul(b7[0:m, :], w1_lo[:, col:col + m], f_nT[:, :], start=False, stop=False)
                    last = pe.matmul(b7[0:m, :], w1_hi[:, col:col + m], f_nT[:, :], start=False, stop=True)
                else:
                    pe.wait_ge(s["fh"], row * 3 + 3)
                    for t in range(GPB):
                        for c, (lo, m) in enumerate(FCH):
                            m += c == 2
                            last = pe.matmul(b7[:, P * t:P * t + P], f_h[0:m, c, P * t:P * t + P], w2[0:m, c, :],
                                             start=(c == 0), stop=(c == 2))
                last.then_inc(s["f_p"], 1)

            def ffn_place(q, place):
                if (q.j, place) in FFN_PLACES:
                    ffn_job(q, FFN_PLACES[q.j, place])

            def transpose_qk(q, kind):
                for half in range(2):
                    if half == 0:
                        pe.wait_ge(s["qkn"], q.count(2, -2, kind + 1))
                    if kind == 0:
                        need(pe, s["pT_r"], q.count(2, -4, half + 1))
                    else:
                        pe.wait_ge(s["qkT_r"], q.count(4, -2, half + 1))
                    for c in range(4):
                        pair = 4 * half + c
                        last = pe.transpose(bank[2 + half][:, P * c:P * c + P],
                                            qk_c[:, q.par(-2), kind, P * pair:P * pair + P], ident[:, :])
                    last.then_inc(s["qkT_p"], 1)

            def scores(q, half):
                b = bank[4 + half]
                if half == 0:
                    need(pe, s["av_r"], q.count(2, -4, 2))
                else:
                    need(pe, s["sub"], q.count(2, -3, 2))
                pe.wait_ge(s["qkT_r"], q.count(4, -2, 3 + half))
                j = q.idx(-2)
                pe.nop(nofuse=True)
                for c in range(4):
                    pair = 4 * half + c
                    for w in range(4):
                        for hp in range(2):
                            half_w, wpar = w // 2, w % 2
                            r = slice(64 * hp, 64 * hp + 64)
                            o = 64 * hp + 32 * wpar
                            last = pe.matmul(
                                b[o:o + 32, P * c + 64 * half_w:P * c + 64 * half_w + 64],
                                qT[r, pair, WIN * w:WIN * w + WIN],
                                kT[r, pair, P * j + WIN * w:P * j + WIN * w + 64],
                                start=True, stop=True)
                last.then_inc(s["sc"], 1)

            def transpose_prob(q, half):
                pe.wait_ge(s["pn"], q.count(2, -3, half + 1))
                if q.on(-4):
                    pe.wait_ge(s["aT_r"], q.count(2, -4, half + 1))
                else:
                    need(pe, s["qkT_r"], q.count(4, -2, 3 + half))
                for c in range(4):
                    last = pe.transpose(bank[2 + half][:, P * c:P * c + P],
                                        prob[:, q.par(-3), 512 * half + P * c:512 * half + P * c + P], ident[:, :])
                last.then_inc(s["pT_p"], 1)

            def attend(q, half):
                if half == 0:
                    b = bank[6]
                    need(pe, s["av_r"], q.count(2, -4, 1))
                else:
                    b = bank[4]
                    if q.on(-2):
                        pe.wait_ge(s["sub"], q.count(2, -2, 1))
                    else:
                        pe.wait_ge(s["av_r"], q.count(2, -4, 2))
                pe.wait_ge(s["pT_r"], q.count(2, -3, half + 1))
                pe.wait_ge(s["v_r"], q.count(2, -3, half + 1))
                need_shifted(pe, q, -3)
                pe.nop(nofuse=True)
                j = q.idx(-3)
                for c in range(4):
                    pair = 4 * half + c
                    for w in range(4):
                        for hp in range(2):
                            half_w, wpar = w // 2, w % 2
                            r = slice(64 * half_w, 64 * half_w + 64)
                            v = (v_own if wpar else v_back)[r, j, DH * (2 * pair + hp):DH * (2 * pair + hp + 1)]
                            last = pe.matmul(b[WIN * w:WIN * w + WIN, DH * (2 * c + hp):DH * (2 * c + hp + 1)],
                                             pT[r, pair, 64 * hp + 32 * wpar:64 * hp + 32 * wpar + 32], v,
                                             start=True, stop=True)
                last.then_inc(s["av"], 1)

            def transpose_att(q, half):
                pe.wait_ge(s["av_r"], q.count(2, -4, half + 1))
                if q.on(-2):
                    pe.wait_ge(s["qkT_r"], q.count(4, -2, 3 + half))
                else:
                    need(pe, s["pT_r"], q.count(2, -4, half + 1))
                for c in range(4):
                    last = pe.transpose(bank[2 + half][:, P * c:P * c + P],
                                        att[:, 512 * half + P * c:512 * half + P * c + P], ident[:, :])
                last.then_inc(s["aT_p"], 1)

            def out_proj(q):
                shared_bank("added", q.count(1, -4, 1))
                pe.wait_ge(s["aT_r"], q.count(2, -4, 2))
                if q.j == 0:
                    pe.wait_ge(s["wo_in"], weights_due(q.it, 1, 1))
                for c in range(PAIRS):
                    last = pe.matmul(bank[7][:, 0:D], attT[:, c, :], wo[:, c, :], start=(c == 0), stop=(c == PAIRS - 1))
                last.then_inc(s["wo_p"], 1)

            def project(q, n):
                part_no = n // 2
                if q.j == 0 and n % 2 == 0:
                    pe.wait_ge(s[("wq_in", "wk_in", "wv_in")[part_no]], weights_due(q.it, 0, 2))
                if n < 2:
                    if n == 0:
                        pe.wait_ge(s["xt_r"], q.count(1, 0, 1))
                    need(pe, s["v_r"], q.count(2, -1, 1 + n))
                else:
                    pe.wait_ge(s["ab"], q.count(4, 0, n - 1))
                lo = P * q.j
                col = INNER * part_no + 512 * (n % 2)
                pe.matmul(bank[n % 2][:, :], xT[:, 1, lo:lo + P], w_hi[:, col:col + 512], start=True, stop=False)
                pe.matmul(bank[n % 2][:, :], xT[:, 0, lo:lo + P], w_lo[:, col:col + 512], start=False, stop=False)
                pe.matmul(bank[n % 2][:, :], xT[:, 0, lo:lo + P], w_hi[:, col:col + 512],
                          start=False, stop=True).then_inc(s["proj"], 1)

            def body(it):
                first = Step(it, 0)
                if round_on(it, 3):
                    front_job[0] = (s["fadd"], it - 2)
                elif isinstance(it, int) and it > NIT:
                    front_job[0] = (s["added"], first.count(1, -5, 1))
                else:
                    front_job[0] = (s["xt_r"], first.count(1, 0, 1))
                for j in range(GPB):
                    q = Step(it, j)
                    ffn_place(q, 0)
                    if q.on(-2):
                        transpose_qk(q, 1)
                    ffn_place(q, 1)
                    if q.on(0):
                        project(q, 2)
                    ffn_place(q, 2)
                    if q.on(-2):
                        scores(q, 0)
                    if q.on(0):
                        project(q, 3)
                    if q.on(-2):
                        scores(q, 1)
                    ffn_place(q, 3)
                    if q.on(-4):
                        transpose_att(q, 0)
                        transpose_att(q, 1)
                    transpose_x(q)
                    if q.on(0):
                        project(q, 4)
                    if q.on(-3):
                        transpose_prob(q, 0)
                    ffn_place(q, 6)
                    if q.on(-3):
                        transpose_prob(q, 1)
                    if q.on(0):
                        project(q, 5)
                    if q.on(-4):
                        out_proj(q)
                    if q.on(-1):
                        transpose_qk(q.next(), 0)
                    if q.on(-3):
                        attend(q, 0)
                    ffn_place(q, 4)
                    if q.on(1):
                        project(q.next(), 0)
                    if q.on(-3):
                        attend(q, 1)
                    if q.on(1):
                        project(q.next(), 1)
                    ffn_place(q, 5)

            pe.wait_ge(s["zeroed"], 5)
            transpose_x(Step(0, -1))
            project(Step(0, 0), 0)
            project(Step(0, 0), 1)
            rounds(pe, body)

        @block.scalar
        def _(act):
            def copy_x(q):
                if not q.on(2):
                    return
                need(act, s["xt_p"], q.count(1, 0, 1))
                act.copy(xs[:, q.par(2), :], stream[:, q.slot(2), :])
                act.copy(xs_part[:, q.par(2), 0, :], stream[:, q.slot(2), :]).then_inc(s["xs_r"], 1)

            def shift_x(q):
                if not q.on(1):
                    return
                act.wait_ge(s["xt_p"], q.count(1, 1, 1))
                need(act, s["proj"], q.count(NPROJ, -2, NPROJ))
                lo = P * q.idx(1)
                src = bank[7][:, 0:2 * P].rearrange("p (n t) -> p n t", n=2)
                act.copy(xT[0:64, :, lo:lo + P], src[0:64])
                act.copy(xT[64:P, :, lo + 1:lo + 1 + P], src[64:P]).then_inc(s["xt_r"], 1)

            def store_qkT(q, n):
                kind, half = n // 2, n % 2
                act.wait_ge(s["qkT_p"], q.count(4, -2, n + 1))
                need(act, s["sc"], q.count(2, -3, 2))
                src = bank[2 + half][:, :].rearrange("p (c t) -> p c t", c=4)
                if kind == 0:
                    dst = qT[:, 4 * half:4 * half + 4, :]
                else:
                    lo = WIN + P * q.idx(-2)
                    dst = kT[:, 4 * half:4 * half + 4, lo:lo + P]
                act.copy(dst, src).then_inc(s["qkT_r"], 1)

            def store_attT(q, half):
                act.wait_ge(s["aT_p"], q.count(2, -4, half + 1))
                need(act, s["wo_p"], q.count(1, -5, 1))
                act.copy(attT[:, 4 * half:4 * half + 4, :].rearrange("p c t -> p (c t)"),
                         bank[2 + half][:, :]).then_inc(s["aT_r"], 1)

            def store_probT(q, half):
                act.wait_ge(s["pT_p"], q.count(2, -3, half + 1))
                need(act, s["av"], q.count(2, -4, 2))
                act.copy(pT[:, 4 * half:4 * half + 4, :].rearrange("p c t -> p (c t)"),
                         bank[2 + half][:, :]).then_inc(s["pT_r"], 1)

            def exponentials(q, half):
                act.wait_ge(s["dif"], q.count(2, -2, half + 1))
                need(act, s["pT_p"], q.count(2, -4, half + 1))
                act.activation(prob[:, q.par(-2), 512 * half:512 * half + 512], sdif[:, half, :],
                               ACT.Exp).then_inc(s["ex"], 1)

            def store_att(q, half):
                act.wait_ge(s["av"], q.count(2, -3, half + 1))
                need(act, s["aT_p"], q.count(2, -4, half + 1))
                act.copy(att[:, 512 * half:512 * half + 512], bank[6 if half == 0 else 4][:, :]).then_inc(s["av_r"], 1)

            def squares(q, n):
                act.wait_ge(s["proj"], q.count(NPROJ, 0, n + 1))
                need(act, s["red"], q.count(4, 0, n - 1))
                act.activation(sq[:, n % 2, :], bank[n % 2][:, :], ACT.Square).then_inc(s["sqr"], 1)

            def store_values(q, n):
                act.wait_ge(s["proj"], q.count(NPROJ, 0, 5 + n))
                need(act, s["av"], q.count(2, -4, 2))
                need_shifted(act, q, -3)
                act.copy(v_own[:, q.idx(0), 512 * n:512 * n + 512], bank[n % 2][:, :]).then_inc(s["v_r"], 1)

            def ffn_job(q, n):
                if not round_on(q.it, 2):
                    return
                row = q.it - 2
                if n < 9:
                    act.wait_ge(s["f_p"], row * FJOBS + (n + 1))
                if n == 0:
                    act.copy(f_xT[0:64, 0:SEQ], bank[7][0:64, :])
                    act.copy(f_xT[64:P, 1:SEQ + 1], bank[7][64:P, :]).then_inc(s["f1"], 1)
                elif n == 1:
                    act.copy(f_x[:, :, :].rearrange("p j d -> p (j d)"), bank[7][:, :]).then_inc(s["f2"], 1)
                elif n == 2:
                    act.activation(f_nT[:, :], bank[7][:, :], ACT.Identity, bias=lnb[:, 0:1], scale=lng[:, 0:1])
                    act.activation(f_x[:, :, :].rearrange("p j d -> p (j d)"), bank[7][:, :], ACT.Identity,
                                   bias=lnb[:, 0:1], scale=lng[:, 0:1]).then_inc(s["f4"], 1)
                elif n in (3, 5, 7):
                    c = (n - 3) // 2
                    m = FCH[c][1]
                    act.activation(f_h[0:m, c, :], bank[7][0:m, :], ACT.Gelu,
                                   bias=b1c[0:m, 3 + c:4 + c]).then_inc(s["fg"], 1)
                elif n < 9:
                    c = (n - 4) // 2
                    m = FCH[c][1]
                    if c == 2:
                        act.wait_ge(s["fh"], row * 3 + 1)
                    act.activation(f_v[0:m, c % 2, :], bank[7][0:m, :], ACT.Identity,
                                   bias=b1c[0:m, c:c + 1]).then_inc(s["fv"], 1)

            def ffn_place(q, place):
                if (q.j, place) in FFN_PLACES:
                    ffn_job(q, FFN_PLACES[q.j, place])

            def copy_row(it):
                if not round_on(it, 2):
                    return
                act.wait_ge(s["added"], (it - 1) * GPB)
                act.copy(f_x[:, :, :], stream[:, bass.ds(((it - 2) % BATCH) * GPB, GPB), :]).then_inc(s["fx"], 1)

            def body(it):
                copy_row(it)
                for j in range(GPB):
                    q = Step(it, j)
                    ffn_place(q, 0)
                    if q.on(-2):
                        store_qkT(q, 2)
                        store_qkT(q, 3)
                    ffn_place(q, 1)
                    if q.on(0):
                        squares(q, 2)
                    ffn_place(q, 2)
                    if q.on(0):
                        squares(q, 3)
                    ffn_place(q, 3)
                    if q.on(-4):
                        store_attT(q, 0)
                        store_attT(q, 1)
                    shift_x(q)
                    if q.on(0):
                        store_values(q, 0)
                    if q.on(-3):
                        store_probT(q, 0)
                    ffn_place(q, 6)
                    if q.on(-3):
                        store_probT(q, 1)
                    if q.on(-2):
                        exponentials(q, 0)
                    if q.on(0):
                        store_values(q, 1)
                    if q.on(-2):
                        exponentials(q, 1)
                    if q.on(-1):
                        store_qkT(q.next(), 0)
                        store_qkT(q.next(), 1)
                    copy_x(q)
                    if q.on(-3):
                        store_att(q, 0)
                    ffn_place(q, 4)
                    if q.on(1):
                        squares(q.next(), 0)
                    if q.on(-3):
                        store_att(q, 1)
                    if q.on(1):
                        squares(q.next(), 1)
                    ffn_place(q, 5)

            act.wait_ge(s["zeroed"], 5)
            copy_x(Step(0, -2))
            copy_x(Step(0, -1))
            shift_x(Step(0, -1))
            squares(Step(0, 0), 0)
            squares(Step(0, 0), 1)
            rounds(act, body)

        @block.gpsimd
        def _(pool):
            def normalise(q, kind):
                pool.wait_ge(s["nr"], q.count(1, -1, 1))
                pool.wait_ge(s["rotd"], q.count(2, -1, kind + 1))
                x = qk_c[:, q.par(-1), kind, :].rearrange("p (h d) -> p h d", d=DH)
                pool.tensor_tensor(x, x, bcast(nrm[:, q.par(-1), HEADS * kind:HEADS * (kind + 1)], 2, DH),
                                   ALU.mult).then_inc(s["qkn"], 1)

            def low_x(q):
                if not q.on(1):
                    return
                pool.wait_ge(s["xs_r"], q.count(1, 1, 1))
                pool.tensor_tensor(xs_part[:, q.par(1), 1, :], xs[:, q.par(1), :],
                                   xs_part[:, q.par(1), 0, :].bitcast(F32), ALU.subtract).then_inc(s["xlo"], 1)

            def low_ffn(q):
                if not round_on(q.it, 2):
                    return
                pool.wait_ge(s["f4"], q.it - 1)
                pool.tensor_tensor(f_nT_lo[:, :],
                                   f_x[:, :, :].rearrange("p j d -> p (j d)"), f_nT[:, :].bitcast(F32),
                                   ALU.subtract).then_inc(s["f5"], 1)

            def ffn_product(q, c):
                if not round_on(q.it, 2):
                    return
                m = FCH[c][1]
                pool.wait_ge(s["fv"], (q.it - 2) * 3 + (c + 1))
                pool.tensor_tensor(f_h[0:m, c, :], f_h[0:m, c, :], f_v[0:m, c % 2, :], ALU.mult).then_inc(s["fh"], 1)

            def normalise_prob(q, half):
                pool.wait_ge(s["ps"], q.count(2, -2, half + 1))
                x = prob[:, q.par(-2), 512 * half:512 * half + 512].rearrange("p (c s) -> p c s", s=64)
                pool.tensor_tensor(x, x, bcast(pinv[:, half, :], 2, 64), ALU.mult).then_inc(s["pn"], 1)

            def rotate(q, kind):
                pool.wait_ge(s["ab"], q.count(4, 0, 2 * kind + 2))
                x = qk_c[:, q.par(0), kind, :]
                pool.tensor_tensor(x, x, qk_s[:, kind, :], ALU.add).then_inc(s["rotd"], 1)

            def body(it):
                for j in range(GPB):
                    q = Step(it, j)
                    low_x(q)
                    if q.on(-1):
                        normalise(q, 0)
                    if j == 3:
                        ffn_product(q, 0)
                    if q.on(-1):
                        normalise(q, 1)
                    if j == 2:
                        low_ffn(q)
                    if j == 3:
                        ffn_product(q, 1)
                    if q.on(0):
                        rotate(q, 0)
                        rotate(q, 1)
                    if j == 3:
                        ffn_product(q, 2)
                    if q.on(-2):
                        normalise_prob(q, 0)
                        normalise_prob(q, 1)

            pool.memset(xT[:, :, 0:1].bitcast(F32), 0.0).then_inc(s["zeroed"], 1)
            pool.memset(kT[:, :, 0:WIN], 0.0).then_inc(s["zeroed"], 1)
            pool.memset(f_xT[:, 0:1], 0.0).then_inc(s["zeroed"], 1)
            pool.memset(v_back[0:WIN, 0, :], 0.0).then_inc(s["zeroed"], 1)
            pool.memset(f_h[:, 2, :], 1.0).then_inc(s["zeroed"], 1)
            low_x(Step(0, -1))
            rounds(pool, body)

        @block.vector
        def _(dve):
            links = [0]

            def link(ins):
                links[0] += 1
                ins.then_inc(s["link"], 1)
                return links[0]

            def linked(n):
                dve.wait_ge(s["link"], n)

            norm_link = [0]

            def norm_step(q, n):
                if not q.on(-1):
                    return
                w, y = ssq[:, q.par(-1), :], nrm[:, q.par(-1), :]
                if n == 0:
                    dve.wait_ge(s["red"], q.count(4, -1, 4))
                    norm_link[0] = link(dve.tensor_scalar(w, w, 1e-24, None, ALU.max))
                    return
                linked(norm_link[0])
                if n == 1:
                    need(dve, s["qkn"], q.count(2, -3, 2))
                    norm_link[0] = link(rsqrt_guess(dve, y, w))
                    return
                ins = rsqrt_step(dve, (n - 2) % 3, y, w, ntmp[:, :])
                if n == 10:
                    ins.then_inc(s["nr"], 1)
                else:
                    norm_link[0] = link(ins)

            def score_mask(q, half):
                dve.wait_ge(s["sc"], q.count(2, -2, half + 1))
                need(dve, s["ex"], q.count(2, -3, half + 1))
                ins = dve.tensor_tensor(sdif[:, half, :].rearrange("p (c s) -> p c s", s=P),
                                        bank[4 + half][:, :].rearrange("p (c s) -> p c s", s=P),
                                        bcast(mask[:, 1 if q.idx(-2) == 0 else 0, :], 1, 4), ALU.add)
                ins.then_inc(s["sub"], 1)

            def score_max(q, half):
                dve.wait_ge(s["sub"], q.count(2, -2, half + 1))
                return link(dve.tensor_reduce(smax[:, half, :], sdif[:, half, :].rearrange("p (c s) -> p c s", s=64),
                                              AX.X, ALU.max))

            def score_sub(q, half, after):
                linked(after)
                x = sdif[:, half, :].rearrange("p (c s) -> p c s", s=64)
                dve.tensor_tensor(x, x, bcast(smax[:, half, :], 2, 64), ALU.subtract).then_inc(s["dif"], 1)

            def prob_sum(q, half):
                dve.wait_ge(s["ex"], q.count(2, -2, half + 1))
                x = prob[:, q.par(-2), 512 * half:512 * half + 512].rearrange("p (c s) -> p c s", s=64)
                return link(dve.tensor_reduce(psm[:, half, :], x, AX.X, ALU.add))

            def prob_inv(q, half, after):
                linked(after)
                need(dve, s["pn"], q.count(2, -3, half + 1))
                dve.reciprocal(pinv[:, half, :], psm[:, half, :]).then_inc(s["ps"], 1)

            def add_attention(q):
                dve.wait_ge(s["wo_p"], q.count(1, -4, 1))
                x = stream[:, q.slot(-4), :]
                dve.tensor_tensor(x, bank[7][:, 0:D], x, ALU.add).then_inc(s["added"], 1)

            def cos_part(q, n):
                kind, half = n // 2, n % 2
                dve.wait_ge(s["sqr"], q.count(4, 0, n + 1))
                need(dve, s["qkT_p"], q.count(4, -2, 2 * kind + 2))
                dve.tensor_tensor(
                    qk_c[:, q.par(0), kind, 512 * half:512 * half + 512].rearrange("p (h d) -> p h d", d=DH),
                    bank[n % 2][:, :].rearrange("p (h d) -> p h d", d=DH),
                    bcast(table(q, 2 * kind), 1, 8), ALU.mult)

            def sin_part(q, n):
                kind, half = n // 2, n % 2
                if half == 0:
                    need(dve, s["rotd"], q.count(2, -1, kind + 1))
                b = bank[n % 2][:, :].rearrange("p (h r d) -> p h r d", r=2, d=DH // 2)
                dst = qk_s[:, kind, 512 * half:512 * half + 512].rearrange("p (h r d) -> p h r d", r=2, d=DH // 2)
                dve.tensor_tensor(dst[:, :, ::-1, :], b,
                                  bcast(table(q, 2 * kind + 1).rearrange("p (r d) -> p r d", r=2), 1, 8),
                                  ALU.mult).then_inc(s["ab"], 1)

            def table(q, kind):
                layer = q.it // BATCH
                lo = (layer * 4 + kind) * (GPB * DH) + q.j * DH
                flat = rot[:, :, :, :].rearrange("p l k n -> p (l k n)")
                return flat[:, lo:lo + DH] if isinstance(lo, int) else flat[:, bass.ds(lo, DH)]

            def square_sum(q, n):
                dve.wait_ge(s["sqr"], q.count(4, 0, n + 1))
                dve.tensor_reduce(ssq[:, q.par(0), 8 * n:8 * n + 8],
                                  sq[:, n % 2, :].rearrange("p (h d) -> p h d", d=DH),
                                  AX.X, ALU.add).then_inc(s["red"], 1)

            def ffn_norm(q):
                if not (q.j == 1 and round_on(q.it, 2)):
                    return
                w, y, t = lw[:, 0, :], lw[:, 1, :], lw[:, 2, :]
                dve.wait_ge(s["f2"], q.it - 1)
                for j in range(GPB):
                    n = link(dve.bn_stats(st[:, j, :], f_x[:, j, :]))
                yield
                linked(n)
                for j in range(GPB):
                    n = link(dve.bn_aggr(mv[:, j, :], st[:, j, :]))
                yield
                linked(n)
                n = link(dve.tensor_scalar(w, mv[:, :, 1], LN_EPS, None, ALU.add))
                yield
                linked(n)
                n = link(rsqrt_guess(dve, y, w))
                yield
                for i in range(9):
                    linked(n)
                    n = link(rsqrt_step(dve, i % 3, y, w, t))
                    yield
                linked(n)
                for j in range(GPB):
                    last = dve.tensor_scalar(f_n[:, j, :], f_x[:, j, :], mv[:, j, 0:1], y[:, j:j + 1],
                                             ALU.subtract, ALU.mult)
                last.then_inc(s["f3"], 1)
                yield

            def add_ffn(row):
                dve.wait_ge(s["f_p"], row * FJOBS + FJOBS)
                x = stream[:, bass.ds((row % BATCH) * GPB, GPB), :]
                dve.tensor_tensor(x, bank[7][:, :].rearrange("p (j d) -> p j d", d=D), x, ALU.add).then_inc(s["fadd"], 1)

            def body(it):
                links[0] = 0
                for j in range(GPB):
                    q = Step(it, j)
                    norm_step(q, 0)
                    norm_step(q, 1)
                    for n in range(2):
                        if q.on(0):
                            cos_part(q, n)
                        norm_step(q, 2 + 3 * n)
                        if q.on(0):
                            sin_part(q, n)
                        norm_step(q, 3 + 3 * n)
                        if q.on(0):
                            square_sum(q, n)
                        norm_step(q, 4 + 3 * n)
                        if j == 0 and n == 0 and round_on(it, 3):
                            add_ffn(it - 3)
                    for n in range(8, 11):
                        norm_step(q, n)
                    norm = ffn_norm(q)
                    if q.on(0):
                        for n in range(2, 4):
                            cos_part(q, n)
                            next(norm, None)
                            sin_part(q, n)
                            next(norm, None)
                            square_sum(q, n)
                            next(norm, None)
                    if q.on(-2):
                        score_mask(q, 0)
                        next(norm, None)
                        score_mask(q, 1)
                        next(norm, None)
                        m0 = score_max(q, 0)
                        next(norm, None)
                        m1 = score_max(q, 1)
                        next(norm, None)
                    if q.on(-2):
                        score_sub(q, 0, m0)
                        next(norm, None)
                        score_sub(q, 1, m1)
                        next(norm, None)
                    if q.on(-4):
                        add_attention(q)
                    if q.on(-2):
                        p0 = prob_sum(q, 0)
                        next(norm, None)
                        p1 = prob_sum(q, 1)
                        next(norm, None)
                        prob_inv(q, 0, p0)
                        prob_inv(q, 1, p1)
                    for _ in norm:
                        pass
                if links[0]:
                    linked(links[0])
                    dve.sem_inc(s["link"], -links[0])

            rounds(dve, body)
            add_ffn(NIT - 1)
            dve.wait_ge(s["fadd"], NIT)
            dve.wait_ge(s["skip_in"], 16)
            dve.tensor_tensor(total, total, stream[:, :, :], ALU.add).then_inc(s["sum_r"], 1)


_INS = ['x', 'ctx_1024', 'L0_attn_W_query', 'L0_attn_W_key', 'L0_attn_W_value', 'L0_xattn_fm_w', 'L0_xattn_fm_b',
        'L0_xattn_fc_w', 'L0_xattn_fc_b', 'L0_ffn_Wqkv', 'L0_ffn_q_scale', 'L0_ffn_k_scale', 'L0_ffn_Wo',
        'L0_ffn_ln_g', 'L0_ffn_ln_b', 'L0_ffn_W1', 'L0_ffn_b1', 'L0_ffn_W2', 'L0_ffn_b2']
_OUTS = [((4, 512, 128), 'float32')]


def kernel(**inputs):
    import numpy as _np
    import concourse.bacc as _bacc
    from concourse import mybir as _mybir
    from concourse.bass_utils import run_bass_kernel_spmd as _run

    nc = _bacc.Bacc("TRN2", target_bir_lowering=False, num_devices=1)
    arrays, args = {}, {}
    for name in _INS:
        a = _np.ascontiguousarray(inputs[name])
        arrays[f"in_{name}_dram"] = a
        args[name] = nc.dram_tensor(f"in_{name}_dram", a.shape, _mybir.dt.from_np(a.dtype), kind="ExternalInput").ap()
    outs = []
    for i, (shape, dtype) in enumerate(_OUTS):
        dt = _mybir.dt.from_np(_np.dtype(dtype))
        outs.append(nc.dram_tensor(f"out_{i}_dram", shape, dt, kind="ExternalOutput").ap())
    decoder(nc, args, *outs)
    r = _run(nc, [arrays], core_ids=[0])
    got = tuple(r.results[0][f"out_{i}_dram"] for i in range(len(_OUTS)))
    return got[0]
```
